# Optimizing a Trainium2 kernel written in Bass

```python
import numpy as np
import jax
import jax.numpy as jnp

def _softmax(x, axis=-1):
    return jax.nn.softmax(x, axis=axis)

def _gelu(x):
    return jax.nn.gelu(x, approximate=True)

def _silu(x):
    return jax.nn.silu(x)

def _sigmoid(x):
    return jax.nn.sigmoid(x)

def _layernorm(x, axis=-1, eps=1e-05):
    m = jnp.mean(x, axis=axis, keepdims=True)
    v = jnp.var(x, axis=axis, keepdims=True)
    return (x - m) / jnp.sqrt(v + eps)

def _scatter_add(tgt, idx, src, axis=0):
    return tgt.at[idx].add(src)

def _segment_sum(src, seg, n):
    return jax.ops.segment_sum(src, seg, n)
kernel_name = 'mk_gnn_resnorm_d4_gnn_r8_227f29'

def setup_inputs(seed: int=0):
    np.random.seed(seed)
    _w = jnp.asarray

    def _rec_inputs():
        import jax
        import jax.numpy as jnp
        _gk = jax.random.key(seed)
        x = -0.000202 + 1 * jax.random.normal(jax.random.fold_in(_gk, 1), (12500, 64), jnp.float32)
        src = jax.random.randint(jax.random.fold_in(_gk, 2), (400000,), 0, 12500, jnp.int32)
        dst = jax.random.randint(jax.random.fold_in(_gk, 3), (400000,), 0, 12500, jnp.int32)
        _o = jnp.argsort(dst, stable=True)
        src = src[_o]
        dst = dst[_o]
        edge_attr_32 = 0.000189758 + 1.00013 * jax.random.normal(jax.random.fold_in(_gk, 11), (400000, 32), jnp.float32)
        edge_attr_64 = -6.74381e-05 + 0.999835 * jax.random.normal(jax.random.fold_in(_gk, 12), (400000, 64), jnp.float32)
        return (x, src, dst, edge_attr_32, edge_attr_64)
    x, src, dst, edge_attr_32, edge_attr_64 = _rec_inputs()

    def _L0_gnn_setup():
        import jax, jax.numpy as jnp
        import numpy as np
        N_NODES = 12500
        N_EDGES = 200000
        D_FEAT = 64
        key = jax.random.key(seed)
        k1, k2, k3 = jax.random.split(key, 3)
        h = jax.random.normal(k1, (N_NODES, D_FEAT), dtype=jnp.float32)
        src = jax.random.randint(k2, (N_EDGES,), 0, N_NODES, dtype=jnp.int32)
        dst = jax.random.randint(k3, (N_EDGES,), 0, N_NODES, dtype=jnp.int32)
        edge_index = jnp.stack([src, dst], axis=0)
        return {'h': h, 'edge_index': edge_index}
    _L0_gnn_all = _L0_gnn_setup()
    _L0_gnn_in = {k: v for k, v in _L0_gnn_all.items() if k in ()}
    del _L0_gnn_all

    def _L1_gnn_setup():
        import jax, jax.numpy as jnp
        import numpy as np
        N_NODES = 6250
        N_EDGES = 156250
        D_FEAT = 64
        key = jax.random.key(seed)
        k1, k2, k3 = jax.random.split(key, 3)
        x = jax.random.normal(k1, (N_NODES, D_FEAT), dtype=jnp.float32)
        edge_attr = jax.random.normal(k2, (N_EDGES, D_FEAT), dtype=jnp.float32)
        edge_index = jax.random.randint(k3, (2, N_EDGES), 0, N_NODES, dtype=jnp.int64)
        return {'x': x, 'edge_attr': edge_attr, 'edge_index': edge_index}
    _L1_gnn_all = _L1_gnn_setup()
    _L1_gnn_in = {k: v for k, v in _L1_gnn_all.items() if k in ()}
    del _L1_gnn_all

    def _L2_gnn_setup():
        import jax, jax.numpy as jnp
        import numpy as np
        N = 12500
        E = 200000
        D_IN = 64
        D_HID = 64
        D_OUT = 64

        def _gcn_norm(edge_index, num_nodes):
            loops = jnp.arange(num_nodes, dtype=edge_index.dtype)
            row = jnp.concatenate([edge_index[0], loops])
            col = jnp.concatenate([edge_index[1], loops])
            ones = jnp.ones(row.shape[0], dtype=jnp.float32)
            deg = jax.ops.segment_sum(ones, col, num_segments=num_nodes)
            dis = jnp.where(deg > 0, jax.lax.rsqrt(deg), 0.0)
            norm = dis[row] * dis[col]
            return (row, col, norm)

        def _gcn_conv(h, W, b, row, col, norm, num_nodes):
            h = h @ W.T
            msg = h[row] * norm[:, None]
            out = jax.ops.segment_sum(msg, col, num_segments=num_nodes)
            return out + b
        key = jax.random.key(seed)
        k_x, k_src, k_dst, k_w1, k_b1, k_w2, k_b2 = jax.random.split(key, 7)
        x = jax.random.normal(k_x, (N, D_IN), dtype=jnp.float32)
        src = jax.random.randint(k_src, (E,), 0, N, dtype=jnp.int64)
        dst = jax.random.randint(k_dst, (E,), 0, N, dtype=jnp.int64)
        edge_index = jnp.stack([src, dst], axis=0)
        s1 = 1.0 / np.sqrt(D_IN)
        s2 = 1.0 / np.sqrt(D_HID)
        W1 = jax.random.uniform(k_w1, (D_HID, D_IN), jnp.float32, -s1, s1)
        b1 = jax.random.uniform(k_b1, (D_HID,), jnp.float32, -s1, s1)
        W2 = jax.random.uniform(k_w2, (D_OUT, D_HID), jnp.float32, -s2, s2)
        b2 = jax.random.uniform(k_b2, (D_OUT,), jnp.float32, -s2, s2)
        return {'x': x, 'edge_index': edge_index, 'W1': W1, 'b1': b1, 'W2': W2, 'b2': b2}
    _L2_gnn_all = _L2_gnn_setup()
    _L2_gnn_in = {k: v for k, v in _L2_gnn_all.items() if k in ('W1', 'b1', 'W2', 'b2')}
    del _L2_gnn_all

    def _L3_gnn_setup():
        import jax, jax.numpy as jnp
        import numpy as np
        import math
        N_NODES = 6250
        N_EDGES = 200000
        DIM = 64
        HEADS = 8
        EDGE_DIM = 32

        def graph_softmax(src, index, num_segments):
            smax = jax.ops.segment_max(src, index, num_segments=num_segments)
            smax = jnp.where(jnp.isfinite(smax), smax, 0.0)
            e = jnp.exp(src - smax[index])
            ssum = jax.ops.segment_sum(e, index, num_segments=num_segments) + 1e-12
            return e / ssum[index]
        key = jax.random.key(seed)
        ks = jax.random.split(key, 12)
        s = 1.0 / math.sqrt(DIM)
        se = 1.0 / math.sqrt(EDGE_DIM)
        return {'x': jax.random.normal(ks[0], (N_NODES, DIM), jnp.float32), 'edge_index': jax.random.randint(ks[1], (2, N_EDGES), 0, N_NODES), 'edge_attr': jax.random.normal(ks[2], (N_EDGES, EDGE_DIM), jnp.float32), 'WQ': jax.random.normal(ks[3], (DIM, DIM), jnp.float32) * s, 'bQ': jnp.zeros((DIM,), jnp.float32), 'WK': jax.random.normal(ks[4], (DIM, DIM), jnp.float32) * s, 'bK': jnp.zeros((DIM,), jnp.float32), 'WV': jax.random.normal(ks[5], (DIM, DIM), jnp.float32) * s, 'bV': jnp.zeros((DIM,), jnp.float32), 'WO': jax.random.normal(ks[6], (DIM, DIM), jnp.float32) * s, 'bO': jnp.zeros((DIM,), jnp.float32), 'We1': jax.random.normal(ks[7], (EDGE_DIM, EDGE_DIM), jnp.float32) * se, 'be1': jnp.zeros((EDGE_DIM,), jnp.float32), 'We2': jax.random.normal(ks[8], (EDGE_DIM, HEADS), jnp.float32) * se, 'be2': jnp.zeros((HEADS,), jnp.float32)}
    _L3_gnn_all = _L3_gnn_setup()
    _L3_gnn_in = {k: v for k, v in _L3_gnn_all.items() if k in ('WQ', 'bQ', 'WK', 'bK', 'WV', 'bV', 'WO', 'bO', 'We1', 'be1', 'We2', 'be2')}
    del _L3_gnn_all
    return {'x': x, 'src': src, 'dst': dst, 'edge_attr_32': edge_attr_32, 'edge_attr_64': edge_attr_64, 'L2_gnn_W1': _L2_gnn_in['W1'], 'L2_gnn_b1': _L2_gnn_in['b1'], 'L2_gnn_W2': _L2_gnn_in['W2'], 'L2_gnn_b2': _L2_gnn_in['b2'], 'L3_gnn_WQ': _L3_gnn_in['WQ'], 'L3_gnn_bQ': _L3_gnn_in['bQ'], 'L3_gnn_WK': _L3_gnn_in['WK'], 'L3_gnn_bK': _L3_gnn_in['bK'], 'L3_gnn_WV': _L3_gnn_in['WV'], 'L3_gnn_bV': _L3_gnn_in['bV'], 'L3_gnn_WO': _L3_gnn_in['WO'], 'L3_gnn_bO': _L3_gnn_in['bO'], 'L3_gnn_We1': _L3_gnn_in['We1'], 'L3_gnn_be1': _L3_gnn_in['be1'], 'L3_gnn_We2': _L3_gnn_in['We2'], 'L3_gnn_be2': _L3_gnn_in['be2']}

def reference(x, src, dst, edge_attr_32, edge_attr_64, L2_gnn_W1, L2_gnn_b1, L2_gnn_W2, L2_gnn_b2, L3_gnn_WQ, L3_gnn_bQ, L3_gnn_WK, L3_gnn_bK, L3_gnn_WV, L3_gnn_bV, L3_gnn_WO, L3_gnn_bO, L3_gnn_We1, L3_gnn_be1, L3_gnn_We2, L3_gnn_be2):
    import jax
    import jax.numpy as jnp

    def _L0_gnn_ref(h, edge_index):
        import jax, jax.numpy as jnp
        import numpy as np
        N_NODES = 12500
        N_EDGES = 200000
        D_FEAT = 64
        src, dst = (edge_index[0], edge_index[1])
        msgs = h[src]
        agg = jax.ops.segment_max(msgs, dst, num_segments=N_NODES)
        return jnp.where(jnp.isneginf(agg), jnp.zeros_like(agg), agg)

    def _L1_gnn_ref(x, edge_attr, edge_index):
        import jax, jax.numpy as jnp
        import numpy as np
        N_NODES = 6250
        N_EDGES = 156250
        D_FEAT = 64
        src = edge_index[0]
        dst = edge_index[1]
        messages = x[src] + x[dst] + edge_attr
        out = jax.ops.segment_sum(messages, dst, num_segments=x.shape[0])
        return out

    def _L2_gnn_ref(x, edge_index, W1, b1, W2, b2):
        import jax, jax.numpy as jnp
        import numpy as np
        N = 12500
        E = 200000
        D_IN = 64
        D_HID = 64
        D_OUT = 64

        def _gcn_norm(edge_index, num_nodes):
            loops = jnp.arange(num_nodes, dtype=edge_index.dtype)
            row = jnp.concatenate([edge_index[0], loops])
            col = jnp.concatenate([edge_index[1], loops])
            ones = jnp.ones(row.shape[0], dtype=jnp.float32)
            deg = jax.ops.segment_sum(ones, col, num_segments=num_nodes)
            dis = jnp.where(deg > 0, jax.lax.rsqrt(deg), 0.0)
            norm = dis[row] * dis[col]
            return (row, col, norm)

        def _gcn_conv(h, W, b, row, col, norm, num_nodes):
            h = h @ W.T
            msg = h[row] * norm[:, None]
            out = jax.ops.segment_sum(msg, col, num_segments=num_nodes)
            return out + b
        num_nodes = x.shape[0]
        row, col, norm = _gcn_norm(edge_index, num_nodes)
        h = _gcn_conv(x, W1, b1, row, col, norm, num_nodes)
        h = jax.nn.relu(h)
        out = _gcn_conv(h, W2, b2, row, col, norm, num_nodes)
        return out

    def _L3_gnn_ref(x, edge_index, edge_attr, WQ, bQ, WK, bK, WV, bV, WO, bO, We1, be1, We2, be2):
        import jax, jax.numpy as jnp
        import numpy as np
        import math
        N_NODES = 6250
        N_EDGES = 200000
        DIM = 64
        HEADS = 8
        EDGE_DIM = 32

        def graph_softmax(src, index, num_segments):
            smax = jax.ops.segment_max(src, index, num_segments=num_segments)
            smax = jnp.where(jnp.isfinite(smax), smax, 0.0)
            e = jnp.exp(src - smax[index])
            ssum = jax.ops.segment_sum(e, index, num_segments=num_segments) + 1e-12
            return e / ssum[index]
        num_nodes = x.shape[0]
        d_k = DIM // HEADS
        i, j = (edge_index[0], edge_index[1])
        Q = (x @ WQ + bQ).reshape(num_nodes, HEADS, d_k)
        K = (x @ WK + bK).reshape(num_nodes, HEADS, d_k)
        V = (x @ WV + bV).reshape(num_nodes, HEADS, d_k)
        query = Q[j]
        key = K[i]
        value = V[i]
        h = jax.nn.silu(edge_attr @ We1 + be1)
        bias = h @ We2 + be2
        scores = jnp.sum(query * key, axis=-1) / math.sqrt(d_k) + bias
        alpha = graph_softmax(scores, j, num_nodes)
        weighted = (alpha[..., None] * value).reshape(-1, DIM)
        attn_out = jax.ops.segment_sum(weighted, j, num_segments=num_nodes)
        return attn_out @ WO + bO
    edge_index = jnp.stack([src, dst])
    x = _layernorm(x + _L0_gnn_ref(x, edge_index), axis=-1)
    x = _layernorm(x + _L1_gnn_ref(x, edge_attr_64, edge_index), axis=-1)
    x = _layernorm(x + _L2_gnn_ref(x, edge_index, L2_gnn_W1, L2_gnn_b1, L2_gnn_W2, L2_gnn_b2), axis=-1)
    x = _layernorm(x + _L3_gnn_ref(x, edge_index, edge_attr_32, L3_gnn_WQ, L3_gnn_bQ, L3_gnn_WK, L3_gnn_bK, L3_gnn_WV, L3_gnn_bV, L3_gnn_WO, L3_gnn_bO, L3_gnn_We1, L3_gnn_be1, L3_gnn_We2, L3_gnn_be2), axis=-1)
    return x

_drawn_inputs = setup_inputs


def setup_inputs(seed=0):
    import zlib

    import numpy as np

    out = dict(_drawn_inputs(seed))
    spreads = {'L3_gnn_bQ': (0.0, 0.287),
     'L3_gnn_bK': (0.0, 0.8),
     'L3_gnn_bV': (0.0, 0.1),
     'L3_gnn_bO': (0.0, 0.1),
     'L3_gnn_be1': (0.0, 0.8),
     'L3_gnn_be2': (0.0, 0.8)}
    factors = {'L2_gnn_W1': 3.29}
    for name, (base, spread) in spreads.items():
        noise = np.random.default_rng([zlib.crc32(name.encode()), seed]).standard_normal(out[name].shape)
        drawn = base * np.exp(spread * noise) if base else spread * noise
        out[name] = jnp.asarray(drawn.astype(out[name].dtype))
    for name, factor in factors.items():
        out[name] = (out[name] * factor).astype(out[name].dtype)
    return out
```

```python
import concourse.bass as bass
from concourse import mybir
from contextlib import ExitStack

P = 128


def ring(eng, count, step):
    with eng.Fori(0, count // 2) as g:
        step(2 * g, 0, g)
        step(2 * g + 1, 1, g)
    if count % 2:
        step(count - 1, 0, count // 2)


def chunks(eng, count, step):
    with eng.Fori(0, count) as c:
        step(c)


class Chain:

    def __init__(self, eng, sem, base=0):
        self.eng, self.sem, self.base, self.n = eng, sem, base, 0

    def __call__(self, ins):
        self.n += 1
        ins.then_inc(self.sem, 1)
        self.eng.wait_ge(self.sem, self.base + self.n)


def build_gnn(nc, x, src, dst, ea32, ea64, W1, b1, W2, b2, WQ, bQ, WK, bK, WV, bV, WO, bO,
              We1, be1, We2, be2, out):
    F32, I32 = mybir.dt.float32, mybir.dt.int32
    ALU, ACT, AX = mybir.AluOpType, mybir.ActivationFunctionType, mybir.AxisListType

    N, F = x.shape
    E = src.shape[0]
    D32 = ea32.shape[1]
    H = be2.shape[0]
    DK = F // H
    EP = E // P
    T = 125
    NB = EP // T
    TS = 25
    NS = T // TS
    NT = -(-N // P)
    NPAD = NT * P
    LAST = N - (NT - 1) * P
    CT = 14
    NC = NT // CT
    DB = 625
    NR = E // DB
    G4 = P // D32
    MG = 16
    NG = -(-T // MG)
    JB = MG // G4
    HT = CT // 2
    W3 = F + 2 * H
    A3 = F + H
    BIG = 1.5e38
    LOW = 1.0e30
    EPS = 1e-5

    nc_ctx = ExitStack()
    with nc_ctx as ctx:
        def dram(name, shape, dt=F32):
            return nc.dram_tensor(name, shape, dt).ap()

        def sem(name):
            return ctx.enter_context(nc.semaphore(name))

        tab_x1 = dram("tab_x1", (NPAD, F))
        tab_t2 = dram("tab_t2", (NPAD, F))
        tab_t3 = dram("tab_t3", (NPAD, F))
        tab_x3 = dram("tab_x3", (NPAD, F))
        tab_q = dram("tab_q", (NPAD, F))
        tab_kv = dram("tab_kv", (NPAD, 2 * F))
        scan_max = dram("scan_max", (E, F))
        scan_ea = dram("scan_ea", (E, F))
        scan_x1 = dram("scan_x1", (E, F))
        scan_t2 = dram("scan_t2", (E, F))
        scan_t3 = dram("scan_t3", (E, F))
        scan_att = dram("scan_att", (E, W3))
        q_edge = dram("q_edge", (E + P, F))
        bias_edge = dram("bias_edge", (E, H))

        def keep(name, shape, dt=F32):
            return ctx.enter_context(nc.sbuf_tensor(name, shape, dt))

        inside = keep("inside", [P, EP])
        ident = keep("ident", [P, P])
        ones_row = keep("ones_row", [1, P])
        node_id = keep("node_id", [P, NT])
        row_first = keep("row_first", [P, NT + 1])
        end_idx = keep("end_idx", [P, NT], I32)
        q_idx = keep("q_idx", [P, NT], I32)
        blk_idx = keep("blk_idx", [P, NT], I32)
        has = keep("has", [P, NT])
        deg = keep("deg", [P, NT])
        dis = keep("dis", [P, NT])
        seam_idx = keep("seam_idx", [P, 1], I32)
        first_idx = keep("first_idx", [P, 1], I32)
        same = keep("same", [P, P])
        through = keep("through", [P, P])
        same_neg = keep("same_neg", [P, P])
        through_neg = keep("through_neg", [P, P])
        carry = keep("carry", [P, F])
        carry_ea = keep("carry_ea", [P, F])
        carry_q = keep("carry_q", [P, F])
        blk_mask = keep("blk_mask", [P, 2, T])
        idx_st = keep("idx_st", [P, 2, T], I32)
        w1_bd = keep("w1_bd", [P, P])
        w2_bd = keep("w2_bd", [P, P])
        wo_bd = keep("wo_bd", [P, P])
        wqkv_bd = keep("wqkv_bd", [P, 2 * 3 * F])
        we1_bd = keep("we1_bd", [P, P])
        we2_bd = keep("we2_bd", [P, G4 * H])
        be1_col = keep("be1_col", [P, 1])
        be2_row = keep("be2_row", [1, MG * H])
        b1_row = keep("b1_row", [1, 8 * F])
        b2_row = keep("b2_row", [1, 8 * F])
        bo_row = keep("bo_row", [1, 8 * F])
        bqkv_row = keep("bqkv_row", [1, 2 * 3 * F])
        deg1 = keep("deg1", [P, NT])
        cnt = keep("cnt", [P, NT])
        blk_base = keep("blk_base", [P, NT])
        small = keep("small", [P, 8])
        seam_row = keep("seam_row", [P, W3])
        seam = keep("seam", [P, 3, P])
        st = keep("st", [P, 4, CT])
        rden = keep("rden", [P, CT, H])
        ln_a = keep("ln_a", [P, CT, F])
        ln_b = keep("ln_b", [P, CT, F])

        AR = nc.sbuf_bytes_remaining // 4 // 16 * 16 - 64
        arena = keep("arena", [P, AR])
        used = [0]

        def lay(shape, dt=F32, at=None):
            n = 1
            for s in shape[1:]:
                n *= s
            if at is not None:
                used[0] = at
            o = used[0]
            used[0] += -(-n // 16) * 16
            assert used[0] <= AR, (used[0], AR)
            v = arena[:, o:o + n]
            if dt is not F32:
                v = v.bitcast(dt)
            if len(shape) == 2:
                return v
            names = "abcd"[:len(shape) - 1]
            return v.rearrange("p (%s) -> p %s" % (" ".join(names), " ".join(names)),
                               **dict(zip(names, shape[1:])))

        dst_i = lay([P, EP], I32, at=0)
        dst_f = lay([P, EP])
        junk = lay([P, EP])
        samp_i = lay([P, NR], I32)
        samp_f = lay([P, NR])
        samp_bc = lay([P, NR])
        ends_bc = lay([P, 2, P])
        rows0 = lay([P, 2, T, F], at=0)
        eat = lay([P, 2, T, F])
        ea_in = lay([P, T * D32])
        ea_T = lay([P, JB * P])
        mlp_h = lay([P, JB * P])
        bias_o = lay([P, 2, T * H])
        found = lay([P, 2, CT, DB], I32, at=0)
        found_f = lay([P, 2, CT, DB])
        junk_s = lay([P, DB])
        shift1 = lay([P, P])
        shift2 = lay([P, P])
        xcur = lay([P, NT, F], at=0)
        tcur = lay([P, NT, F])
        node_end = used[0]
        got = lay([P, NT, W3])
        got_ea = lay([P, NT, F], at=node_end + NT * F)
        kv_o = lay([P, NT, 2 * F], at=node_end + NT * W3)
        q_o = lay([P, NT, F])
        zc = lay([P, CT, F])
        zT = lay([P, HT * P])
        got64 = arena[:, node_end:node_end + NT * F].rearrange("p (a b) -> p a b", a=NT)
        rows12 = lay([P, 2, T, F], at=node_end)
        zeros_z = lay([P, T * F])
        kv = lay([P, NS, TS, 2 * F], at=0)
        qf = lay([P, T, F])
        acc = lay([P, T + 1, W3])
        prod = lay([P, TS, F])
        score = lay([P, TS, H])
        arg = lay([P, 2, TS, H])
        keepf = lay([P, T, H])
        bias_i = lay([P, T, H])
        seam_m = lay([P, 8, P], at=0)

        bank = [ctx.enter_context(nc.psum_tensor(f"bank{i}", [P, 512], F32)) for i in range(8)]

        s_ident = sem("s_ident")
        s_iota = sem("s_iota")
        s_zeroed = sem("s_zeroed")
        s_dst = sem("s_dst")
        s_samp = sem("s_samp")
        s_wt = sem("s_wt")
        s_wt_cp = sem("s_wt_cp")
        s_wt_T = sem("s_wt_T")
        s_ends = sem("s_ends")
        s_ends_bc = sem("s_ends_bc")
        s_samp_f = sem("s_samp_f")
        s_samp_bc = sem("s_samp_bc")
        s_chain = sem("s_chain")
        s_setup_done = sem("s_setup_done")
        s_level1 = sem("s_level1")
        s_found = [sem(f"s_found{i}") for i in range(2)]
        s_found_f = [sem(f"s_found_f{i}") for i in range(2)]
        s_found_used = [sem(f"s_found_used{i}") for i in range(2)]
        s_search = sem("s_search")
        s_first = sem("s_first")
        s_shift = sem("s_shift")
        s_shifted = sem("s_shifted")
        s_sqrt = sem("s_sqrt")
        s_nodes = sem("s_nodes")

        e_idx = [sem(f"edge_idx{i}") for i in range(2)]
        e_scanned = [sem(f"edge_scanned{i}") for i in range(2)]
        e_stored = [sem(f"edge_stored{i}") for i in range(2)]
        e_free = [sem(f"edge_free{i}") for i in range(2)]
        e_mask = sem("edge_mask")
        e_carry = sem("edge_carry_saved")
        e_all_stored = sem("edge_all_stored")
        e_table = sem("edge_table_stored")
        node_var = sem("node_var")
        node_std = sem("node_std")

        class Seam:
            def __init__(self, name):
                self.t = sem(f"{name}_seam_transposed")
                self.scan = sem(f"{name}_seam_scanned")
                self.back = sem(f"{name}_seam_back")
                self.row = sem(f"{name}_seam_row")
                self.sum = sem(f"{name}_seam_sum")
                self.put = sem(f"{name}_seam_put")

        edge_seam = Seam("edge")

        class EdgePass:
            def __init__(self, i, name, table, scan, maximum, rows):
                self.i, self.table, self.scan, self.maximum, self.rows = i, table, scan, maximum, rows
                self.v = [i * ((NB + 1) // 2), i * (NB // 2)]
                self.gathered = [sem(f"{name}_gathered{i}") for i in range(2)]
                self.mask0 = NB * (i + 1) if i else 0
                self.carry0 = i * (NB + 1) + 1

        class NodeStage:
            def __init__(self, i, name, product=True):
                self.norm0 = NC * i
                self.got = [sem(f"{name}_got{i}") for i in range(2)]
                self.chain = sem(f"{name}_chain")
                self.rows = sem(f"{name}_rows")
                if product:
                    self.z = sem(f"{name}_z")
                    self.zt = sem(f"{name}_z_transposed")
                    self.ztc = sem(f"{name}_zt_copied")
                    self.mm = sem(f"{name}_product")

        p0 = EdgePass(0, "max", x, scan_max, True, rows0)
        p1 = EdgePass(1, "sum1", tab_x1, scan_x1, False, rows12)
        p2 = EdgePass(2, "sum2", tab_t2, scan_t2, False, rows12)
        p3 = EdgePass(3, "sum3", tab_t3, scan_t3, False, rows12)
        n0, n1 = NodeStage(0, "n0", False), NodeStage(1, "n1", False)
        n2, n3, n4 = NodeStage(2, "n2"), NodeStage(2, "n3"), NodeStage(3, "n4")
        ea_seam, a_seam = Seam("ea"), Seam("att")
        ea_loaded = [sem(f"ea_loaded{i}") for i in range(2)]
        ea_scanned = [sem(f"ea_scanned{i}") for i in range(2)]
        ea_stored = [sem(f"ea_stored{i}") for i in range(2)]
        ea_carry = sem("ea_carry")
        mlp_in = sem("mlp_in")
        mlp_stored = [sem(f"mlp_stored{i}") for i in range(2)]
        mlp_T = sem("mlp_T")
        mlp_Tc = sem("mlp_Tc")
        mlp_z = sem("mlp_z")
        mlp_a = sem("mlp_a")
        mlp_b = sem("mlp_b")
        mlp_bc = sem("mlp_bc")
        s_zero_edge = sem("s_zero_edge")
        s_zeros = sem("s_zeros")
        x_loaded = sem("x_loaded")
        x_pad = sem("x_pad")
        x3_loaded = sem("x3_loaded")
        x3_stored = sem("x3_stored")
        qkv_mm = sem("qkv_mm")
        qkv_copied = sem("qkv_copied")
        q_tab = sem("q_tab")
        q_scat = sem("q_scat")
        q_first = sem("q_first")
        q_first_put = sem("q_first_put")
        a_idx = [sem(f"a_idx{i}") for i in range(2)]
        a_kv = [sem(f"a_kv{i}") for i in range(NS)]
        a_free = [sem(f"a_free{i}") for i in range(NS)]
        a_init = sem("a_init")
        a_slot = sem("a_slot")
        ea_back_read = sem("ea_back_read")
        a_q = sem("a_q")
        a_bias = sem("a_bias")
        a_chain = sem("a_chain")
        a_q_used = sem("a_q_used")
        a_arg = sem("a_arg")
        a_exp = sem("a_exp")
        a_scan = sem("a_scan")
        a_stored = sem("a_stored")
        a_all_stored = sem("a_all_stored")
        a_tail = sem("a_tail")
        a_dexp = sem("a_dexp")
        a_dexped = sem("a_dexped")
        out_rows = sem("out_rows")
        pool_begun = sem("pool_begun")

        src_v = src.rearrange("(p t) -> p t", p=P)
        dst_v = dst.rearrange("(p t) -> p t", p=P)
        dst_rows = dst.rearrange("(r c) -> r c", c=DB)
        ea64_v = ea64.rearrange("(p t) f -> p (t f)", p=P)
        ea32_v = ea32.rearrange("(p t) f -> p (t f)", p=P)
        bias_v = bias_edge.rearrange("(p t) f -> p (t f)", p=P)
        q_edge_v = q_edge[0:E, :].rearrange("(p t) f -> p (t f)", p=P)

        def scan_v(s):
            return s.rearrange("(p t) f -> p (t f)", p=P)

        def tiles(t):
            return t.rearrange("(t p) f -> p t f", p=P)

        def flat(v):
            return v.rearrange("p a b -> p (a b)")

        def over(v, n):
            a = v.shape[1]
            return v.rearrange("p (a o) -> p a o", o=1).to_broadcast([v.shape[0], a, n])

        def chunk(v, c):
            return v[:, bass.ds(c * CT, CT), :]

        n_weights = 2 * 6 + G4 * 3 + 4 + 3

        block = ctx.enter_context(nc.Block())

        @block.sync
        def _(sp):
            sp.dma_start(dst_i, dst_v).then_inc(s_dst, 16)
            sp.dma_start(samp_i[0:1, :], dst.rearrange("(o r c) -> o r c", o=1, c=DB)[:, :, 0],
                         allow_slow_non_contiguous=True).then_inc(s_samp, 16)
            sp.wait_ge(s_zeroed, 1)
            nw = 0
            for h in range(2):
                d = slice(h * F, (h + 1) * F)
                for w, o in ((W1, w1_bd), (W2, w2_bd), (WO, wo_bd)):
                    sp.dma_start(o[d, d], w).then_inc(s_wt, 16)
                for i, w in enumerate((WQ, WK, WV)):
                    a = h * 3 * F + i * F
                    sp.dma_start(wqkv_bd[d, a:a + F], w).then_inc(s_wt, 16)
                nw += 6
            for i in range(G4):
                d = slice(i * D32, (i + 1) * D32)
                sp.dma_start(we1_bd[d, d], We1).then_inc(s_wt, 16)
                sp.dma_start(we2_bd[d, i * H:(i + 1) * H], We2).then_inc(s_wt, 16)
                sp.dma_start(be1_col[d, :], be1.rearrange("(p o) -> p o", o=1)).then_inc(s_wt, 16)
                nw += 3
            for b, o, k in ((be2, be2_row, MG), (b1, b1_row, 8), (b2, b2_row, 8), (bO, bo_row, 8)):
                n = b.shape[0]
                sp.dma_start(o[:, :].rearrange("o (k n) -> o k n", k=k),
                             b.rearrange("(o k n) -> o k n", o=1, k=1).to_broadcast([1, k, n])).then_inc(s_wt, 16)
                nw += 1
            for i, b in enumerate((bQ, bK, bV)):
                o = bqkv_row[:, :].rearrange("o (k i n) -> o k i n", k=2, i=3)[:, :, i, :]
                sp.dma_start(o, b.rearrange("(o k n) -> o k n", o=1, k=1).to_broadcast([1, 2, F])).then_inc(s_wt, 16)
                nw += 1
            assert nw == n_weights

            def edge_pass(p, layer0=False, fill=False):
                for k in range(2):
                    sp.dma_start(idx_st[:, k, :], src_v[:, k * T:(k + 1) * T]).then_inc(e_idx[k], 16)
                    sp.sem_inc(e_free[k], 1)
                if layer0:
                    sp.wait_ge(s_setup_done, 1)
                    for k in range(2):
                        sp.dma_start(flat(eat[:, k]), ea64_v[:, k * T * F:(k + 1) * T * F]).then_inc(ea_loaded[k], 16)
                    sp.dma_start(ea_in, ea32_v[:, 0:T * D32]).then_inc(mlp_in, 16)
                if fill:
                    sp.wait_ge(s_zeros, 1)

                def step(k, b, n, more=2):
                    sp.wait_ge(p.gathered[b], (n + 1) * (16 * T))
                    if more > 1:
                        sp.dma_start(idx_st[:, b, :], src_v[:, bass.ds((k + 2) * T, T)]).then_inc(e_idx[b], 16)
                    if layer0:
                        sp.wait_ge(ea_scanned[b], n + 1)
                        sp.dma_start(scan_v(scan_ea)[:, bass.ds(k * (T * F), T * F)], flat(eat[:, b])).then_inc(ea_stored[b], 16)
                        sp.wait_ge(mlp_bc, (k + 1) * NG)
                        sp.dma_start(bias_v[:, bass.ds(k * (T * H), T * H)], bias_o[:, b]).then_inc(mlp_stored[b], 16)
                        sp.wait_ge(ea_carry, k + 2)
                        if more > 0:
                            sp.dma_start(ea_in, ea32_v[:, bass.ds((k + 1) * (T * D32), T * D32)]).then_inc(mlp_in, 16)
                    sp.wait_ge(e_scanned[b], n + (p.v[b] + 1))
                    sp.dma_start(scan_v(p.scan)[:, bass.ds(k * (T * F), T * F)], flat(p.rows[:, b])).then_inc(e_stored[b], 16)
                    if fill:
                        sp.dma_start(q_edge_v[:, bass.ds(k * (T * F), T * F)], zeros_z).then_inc(s_zero_edge, 16)
                    if layer0:
                        sp.wait_ge(ea_stored[b], (n + 1) * 16)
                        sp.wait_ge(mlp_stored[b], (n + 1) * 16)
                        if more > 1:
                            sp.dma_start(flat(eat[:, b]), ea64_v[:, bass.ds((k + 2) * (T * F), T * F)]).then_inc(ea_loaded[b], 16)
                    sp.wait_ge(e_stored[b], (n + (p.v[b] + 1)) * 16)
                    sp.sem_inc(e_free[b], 1)
                with sp.Fori(0, NB // 2 - 1) as g:
                    step(2 * g, 0, g)
                    step(2 * g + 1, 1, g)
                step(NB - 3, 0, NB // 2 - 1)
                step(NB - 2, 1, NB // 2 - 1, more=1)
                step(NB - 1, 0, NB // 2, more=0)
                if fill:
                    sp.wait_ge(s_zero_edge, 16 * NB)
                sp.wait_ge(e_carry, p.carry0 + 1 + NB)
                sp.sem_inc(e_all_stored, 1)

            def store_rows(s, done, table, rows):
                def step(c):
                    sp.wait_ge(s.rows, c + 1)
                    sp.dma_start(chunk(tiles(table), c), chunk(rows, c)).then_inc(done, 16)
                chunks(sp, NC, step)

            edge_pass(p0, layer0=True)
            sp.wait_ge(x_pad, 1)
            sp.dma_start(xcur[:, 0:NT - 1, :], x[0:(NT - 1) * P, :].rearrange("(t p) f -> p t f", p=P)).then_inc(x_loaded, 16)
            sp.dma_start(xcur[0:LAST, NT - 1, :], x[(NT - 1) * P:N, :]).then_inc(x_loaded, 16)
            store_rows(n0, e_table, tab_x1, xcur)
            edge_pass(p1, fill=True)
            store_rows(n1, e_table, tab_t2, tcur)
            edge_pass(p2)
            store_rows(n2, e_table, tab_t3, tcur)
            edge_pass(p3)

            def tables(c):
                sp.wait_ge(n3.rows, c + 1)
                sp.dma_start(chunk(tiles(tab_x3), c), chunk(xcur, c)).then_inc(x3_stored, 16)
                sp.wait_ge(qkv_copied, (c + 1) * HT)
                sp.dma_start(chunk(tiles(tab_kv), c), chunk(kv_o, c)).then_inc(q_tab, 16)
                sp.dma_start(chunk(tiles(tab_q), c), chunk(q_o, c)).then_inc(q_tab, 16)
            chunks(sp, NC, tables)
            sp.wait_ge(x3_stored, 16 * NC)
            sp.wait_ge(q_scat, 16 * NT)
            sp.wait_ge(q_first, 16)
            sp.dma_start(q_edge[0:E, :].rearrange("(p t) f -> p t f", p=P)[:, 0, :], seam_row[:, 0:F]).then_inc(q_first_put, 16)
            sp.wait_ge(q_first_put, 16)

            sp.wait_ge(q_tab, 2 * 16 * NC)
            sp.sem_inc(a_slot, 1)
            for k in range(2):
                sp.dma_start(idx_st[:, k, :], src_v[:, k * T:(k + 1) * T]).then_inc(a_idx[k], 16)
            sp.dma_start(flat(qf), q_edge_v[:, 0:T * F]).then_inc(a_q, 16)
            sp.dma_start(flat(bias_i), bias_v[:, 0:T * H]).then_inc(a_bias, 16)

            def att(k, b, n, more=2):
                if more > 1:
                    for u in range(NS):
                        sp.wait_ge(a_kv[u], (k + 1) * (16 * TS))
                    sp.dma_start(idx_st[:, b, :], src_v[:, bass.ds((k + 2) * T, T)]).then_inc(a_idx[b], 16)
                sp.wait_ge(a_q_used, k + 1)
                if more > 0:
                    sp.dma_start(flat(qf), q_edge_v[:, bass.ds((k + 1) * (T * F), T * F)]).then_inc(a_q, 16)
                    sp.dma_start(flat(bias_i), bias_v[:, bass.ds((k + 1) * (T * H), T * H)]).then_inc(a_bias, 16)
                sp.wait_ge(a_scan, k + 1)
                sp.dma_start(scan_v(scan_att)[:, bass.ds(k * (T * W3), T * W3)], flat(acc[:, 1:T + 1, :])).then_inc(a_stored, 16)
                sp.wait_ge(a_stored, (k + 1) * 16)
                sp.sem_inc(a_slot, 1)
            with sp.Fori(0, NB // 2 - 1) as g:
                att(2 * g, 0, g)
                att(2 * g + 1, 1, g)
            att(NB - 3, 0, NB // 2 - 1)
            att(NB - 2, 1, NB // 2 - 1, more=1)
            att(NB - 1, 0, NB // 2, more=0)
            sp.wait_ge(a_stored, 16 * NB)
            sp.sem_inc(a_all_stored, 1)
            sp.wait_ge(a_seam.put, 16)
            sp.dma_start(xcur, tiles(tab_x3)).then_inc(x3_loaded, 16)

            with sp.Fori(0, NC - 1) as c:
                sp.wait_ge(n4.rows, c + 1)
                sp.dma_start(out[bass.ds(c * (CT * P), CT * P), :].rearrange("(t p) f -> p t f", p=P), chunk(xcur, c)).then_inc(out_rows, 16)
            sp.wait_ge(n4.rows, NC)
            a = (NC - 1) * CT
            sp.dma_start(out[a * P:(NT - 1) * P, :].rearrange("(t p) f -> p t f", p=P), xcur[:, a:NT - 1, :]).then_inc(out_rows, 16)
            sp.dma_start(out[(NT - 1) * P:N, :], xcur[0:LAST, NT - 1, :]).then_inc(out_rows, 16)
            sp.wait_ge(out_rows, 16 * (NC + 1))

        @block.gpsimd
        def _(pool):
            def gather(dst_ap, table, idx):
                return pool.indirect_dma_start(dst_ap, None, table, bass.IndirectOffsetOnAxis(ap=idx, axis=0))

            def scatter(table, idx, src_ap):
                return pool.indirect_dma_start(table, bass.IndirectOffsetOnAxis(ap=idx, axis=0), src_ap, None)

            pool.memset(ident[:, :], 0.0).then_inc(s_ident, 1)
            pool.iota(node_id[:, :], [[P, NT]], base=0, channel_multiplier=1, allow_small_or_imprecise_dtypes=True).then_inc(s_iota, 1)
            pool.iota(small[:, 0:1], [[0, 1]], base=0, channel_multiplier=1, allow_small_or_imprecise_dtypes=True).then_inc(s_iota, 1)
            pool.wait_ge(s_ident, 1)
            pool.affine_select(out=ident[:, :], in_=ident[:, :], compare_op=ALU.not_equal, fill=1.0, base=0,
                               pattern=[[-1, P]], channel_multiplier=1).then_inc(s_ident, 1)
            pool.wait_ge(s_setup_done, 1)

            def edge_pass(p):
                def step(k, b, n):
                    pool.wait_ge(e_idx[b], (n + (p.v[b] + 1)) * 16)
                    pool.wait_ge(e_free[b], n + (p.v[b] + p.i + 1))
                    pool.wait_ge(e_carry, k + p.carry0)
                    pool.sem_inc(pool_begun, 1)
                    for t in range(T):
                        gather(p.rows[:, b, t, :], p.table, idx_st[:, b, t:t + 1]).then_inc(p.gathered[b], 16)
                ring(pool, NB, step)

            def seam_fix(scan, sm, i=1, width=F):
                gather(seam_row[:, 0:W3 if width == A3 else F], scan, seam_idx[:, :]).then_inc(sm.row, 16)
                pool.wait_ge(sm.sum, i)
                scatter(scan, seam_idx[:, :], seam_row[:, 0:W3 if width == A3 else F]).then_inc(sm.put, 16)
                pool.wait_ge(sm.put, 16 * i)

            def node_rows(s, pieces):
                per = 16 * CT * len(pieces)
                for c in range(NC):
                    if c >= 2:
                        pool.wait_ge(s.got[c % 2], per * (c // 2))
                    for t in range(c * CT, (c + 1) * CT):
                        for rows, scan in pieces:
                            gather(rows[:, t, :], scan, end_idx[:, t:t + 1]).then_inc(s.got[c % 2], 16)

            edge_pass(p0)
            pool.wait_ge(e_all_stored, 1)
            pool.wait_ge(s_level1, 1)
            for c in range(NC):
                if c >= 2:
                    pool.wait_ge(s_found_f[c % 2], c // 2)
                for i in range(CT):
                    t = c * CT + i
                    gather(found[:, c % 2, i, :], dst_rows, blk_idx[:, t:t + 1]).then_inc(s_found[c % 2], 16)
            seam_fix(scan_max, edge_seam, 1)
            seam_fix(scan_ea, ea_seam)
            pool.wait_ge(s_nodes, 1)
            node_rows(n0, [(got64, scan_max)])
            pool.wait_ge(e_table, 1 * 16 * NC)
            edge_pass(p1)
            pool.wait_ge(e_all_stored, 2)
            seam_fix(scan_x1, edge_seam, 2)
            node_rows(n1, [(got64, scan_x1), (got_ea, scan_ea)])
            pool.wait_ge(e_table, 2 * 16 * NC)
            edge_pass(p2)
            pool.wait_ge(e_all_stored, 3)
            seam_fix(scan_t2, edge_seam, 3)
            node_rows(n2, [(got64, scan_t2)])
            pool.wait_ge(e_table, 3 * 16 * NC)
            edge_pass(p3)
            pool.wait_ge(e_all_stored, 4)
            seam_fix(scan_t3, edge_seam, 4)
            node_rows(n3, [(got64, scan_t3)])
            pool.wait_ge(s_zero_edge, 16 * NB)
            pool.wait_ge(qkv_copied, HT * NC)
            for t in range(NT):
                scatter(q_edge, q_idx[:, t:t + 1], q_o[:, t, :]).then_inc(q_scat, 16)
            pool.wait_ge(q_tab, 2 * 16 * NC)
            gather(seam_row[:, 0:F], tab_q, first_idx[:, :]).then_inc(q_first, 16)
            pool.wait_ge(q_scat, 16 * NT)
            pool.wait_ge(x3_stored, 16 * NC)

            def att(k, b, n):
                pool.wait_ge(a_idx[b], (n + 1) * 16)
                for u in range(NS):
                    pool.wait_ge(a_free[u], k + 1)
                    pool.sem_inc(pool_begun, 1)
                    for t in range(TS):
                        i = u * TS + t
                        gather(kv[:, u, t, :], tab_kv, idx_st[:, b, i:i + 1]).then_inc(a_kv[u], 16)
            ring(pool, NB, att)
            pool.wait_ge(a_all_stored, 1)
            seam_fix(scan_att, a_seam, 1, A3)
            node_rows(n4, [(got, scan_att)])

        @block.scalar
        def _(act):
            for i, w in enumerate((w1_bd, w2_bd)):
                act.wait_ge(s_wt_T, i + 1)
                act.activation(w[:, :], bank[i][:, 0:P], ACT.Copy).then_inc(s_wt_cp, 1)
            act.wait_ge(s_samp, 16)
            act.activation(samp_f[0:1, :], samp_i[0:1, :], ACT.Copy).then_inc(s_samp_f, 1)
            act.wait_ge(s_samp_bc, 1)
            act.activation(samp_bc[:, 0:512], bank[2][:, :], ACT.Copy).then_inc(s_samp_f, 1)
            act.activation(samp_bc[:, 512:NR], bank[3][:, 0:NR - 512], ACT.Copy).then_inc(s_samp_f, 1)

            def mlp(k, b, n):
                for q in range(NG):
                    act.wait_ge(mlp_T, k * NG + (q + 1))
                    act.activation(ea_T, bank[0][:, :], ACT.Copy).then_inc(mlp_Tc, 1)
                    act.wait_ge(mlp_z, k * NG + (q + 1))
                    act.activation(mlp_h, bank[1][:, :], ACT.Silu, bias=be1_col[:, :]).then_inc(mlp_a, 1)
                    t0 = min(q * MG, T - MG)
                    act.wait_ge(mlp_b, k * NG + (q + 1))
                    if q == 0:
                        act.wait_ge(e_free[b], n + 1)
                    act.activation(bias_o[:, b, t0 * H:(t0 + MG) * H], bank[2][:, 0:MG * H], ACT.Copy).then_inc(mlp_bc, 1)
            ring(act, NB, mlp)

            def conv(c, b, n):
                act.wait_ge(s_found[b], (n + 1) * (16 * CT))
                act.wait_ge(s_found_used[b], n + 1)
                act.activation(flat(found_f[:, b]), flat(found[:, b]), ACT.Copy).then_inc(s_found_f[b], 1)
            ring(act, NC, conv)
            act.wait_ge(s_sqrt, 1)
            act.activation(dis[:, :], deg1[:, :], ACT.Sqrt).then_inc(s_sqrt, 1)

            def std(s, c):
                act.wait_ge(node_var, c + (s.norm0 + 1))
                act.activation(st[:, 2, :], st[:, 1, :], ACT.Sqrt).then_inc(node_std, 1)

            def copies(s, z):
                act.wait_ge(s.zt, z)
                act.activation(zT[:, 0:4 * P], bank[0][:, :], ACT.Copy).then_inc(s.ztc, 1)
                act.activation(zT[:, 4 * P:HT * P], bank[1][:, 0:(HT - 4) * P], ACT.Copy).then_inc(s.ztc, 1)

            chunks(act, NC, lambda c: std(n0, c))
            chunks(act, NC, lambda c: std(n1, c))
            chunks(act, NC, lambda c: copies(n2, c + 1))

            def stage3(c):
                copies(n3, 2 * c + 1)
                std(n3, c)
                copies(n3, 2 * c + 2)
                for j in range(HT):
                    act.wait_ge(qkv_mm, c * HT + (j + 1))
                    v = bank[4 + j % 4][:, 0:6 * F].rearrange("p (a b) -> p a b", a=2)
                    act.activation(kv_o[:, bass.ds(c * CT + 2 * j, 2), :], v[:, :, F:3 * F], ACT.Copy)
                    act.activation(q_o[:, bass.ds(c * CT + 2 * j, 2), :], v[:, :, 0:F], ACT.Copy,
                                   scale=float(DK) ** -0.5).then_inc(qkv_copied, 1)
            chunks(act, NC, stage3)

            def att(k):
                for u in range(NS):
                    act.wait_ge(a_arg, k * NS + (u + 1))
                    act.activation(acc[:, 1 + u * TS:1 + (u + 1) * TS, F:A3], arg[:, 0], ACT.Exp)
                    act.activation(keepf[:, u * TS:(u + 1) * TS, :], arg[:, 1], ACT.Exp).then_inc(a_exp, 1)
            chunks(act, NB, att)
            act.wait_ge(a_dexp, 1)
            act.activation(seam_m[0:A3, 3:5, :], seam_m[0:A3, 3:5, :], ACT.Exp).then_inc(a_dexped, 1)
            act.wait_ge(a_dexp, 2)
            act.activation(seam_m[:, 6:8, 0:A3], seam_m[:, 6:8, 0:A3], ACT.Exp).then_inc(a_dexped, 1)

            def stage4(c):
                copies(n4, c + 1)
                std(n4, c)
            chunks(act, NC, stage4)

        @block.tensor
        def _(pe):
            pe.wait_ge(s_ident, 2)
            pe.wait_ge(s_wt, 16 * n_weights)
            for i, w in enumerate((w1_bd, w2_bd)):
                pe.transpose(bank[i][:, 0:P], w[:, :], ident[:, :]).then_inc(s_wt_T, 1)
            pe.wait_ge(s_samp_f, 1)
            pe.wait_ge(s_zeroed, 1)
            pe.matmul(bank[2][:, :], ones_row[:, :], samp_f[0:1, 0:512], start=True, stop=True)
            pe.matmul(bank[3][:, 0:NR - 512], ones_row[:, :], samp_f[0:1, 512:NR], start=True, stop=True).then_inc(s_samp_bc, 1)
            pe.wait_ge(s_ends, 1)
            for i in range(2):
                pe.matmul(bank[6 + i][:, 0:P], ends_bc[:, i, :], ident[:, :], start=True, stop=True).then_inc(s_ends_bc, 1)

            def mlp(k, b, n):
                for q in range(NG):
                    g = k * NG + q
                    t0 = min(q * MG, T - MG)
                    if q == 0:
                        pe.wait_ge(mlp_in, (k + 1) * 16)
                    for j in range(JB):
                        i = pe.transpose(bank[0][:, j * P:(j + 1) * P],
                                         ea_in[:, t0 * D32 + j * P:t0 * D32 + (j + 1) * P], ident[:, :])
                    i.then_inc(mlp_T, 1)
                    pe.wait_ge(mlp_Tc, g + 1)
                    pe.matmul(bank[1][:, :], we1_bd[:, :], ea_T, start=True, stop=True).then_inc(mlp_z, 1)
                    pe.wait_ge(mlp_a, g + 1)
                    pe.matmul(bank[2][:, 0:MG * H], ones_row[:, :], be2_row[:, :], start=True, stop=False)
                    for j in range(JB):
                        i = pe.matmul(bank[2][:, j * G4 * H:(j + 1) * G4 * H], mlp_h[:, j * P:(j + 1) * P], we2_bd[:, :],
                                      start=False, stop=j == JB - 1)
                    i.then_inc(mlp_b, 1)
                    pe.wait_ge(mlp_bc, g + 1)
            pe.wait_ge(s_wt_cp, 2)
            pe.wait_ge(s_samp_f, 3)
            ring(pe, NB, mlp)

            def seam_turn(sm, i, tails, ready, extra=1, width=F):
                pe.wait_ge(ready, i * (NB + 1) + extra)
                pe.transpose(bank[6][0:width, 0:P], tails, ident[:, :]).then_inc(sm.t, 1)
                pe.wait_ge(sm.scan, i)
                pe.transpose(bank[7][:, 0:width], seam[0:width, 1, :], ident[0:width, 0:width]).then_inc(sm.back, 1)

            seam_turn(ea_seam, 1, carry_ea[:, :], ea_carry, 0)
            pe.wait_ge(ea_back_read, 1)
            seam_turn(edge_seam, 1, carry[:, :], e_carry)
            pe.wait_ge(s_first, 1)
            pe.wait_ge(s_shift, 2)
            pe.matmul(bank[3][:, 0:NT], shift1, row_first[:, 0:NT], start=True, stop=False)
            pe.matmul(bank[3][:, 0:NT], shift2, row_first[:, 1:NT + 1], start=False, stop=True).then_inc(s_shifted, 1)

            def product(s, z, w, brow):
                pe.wait_ge(s.ztc, 2 * z)
                for h, (a, b) in enumerate(((0, 4), (4, HT))):
                    pe.matmul(bank[2 + h][:, 0:(b - a) * P], ones_row[:, :], brow[:, 0:(b - a) * P], start=True, stop=False)
                    for j in range(a, b):
                        i = pe.matmul(bank[2 + h][:, (j - a) * P:(j - a + 1) * P], zT[:, j * P:(j + 1) * P], w[:, :],
                                      start=False, stop=j == b - 1)
                i.then_inc(s.mm, 1)

            def turn(s, z, v):
                pe.wait_ge(s.z, z)
                for j in range(HT):
                    i = pe.transpose(bank[j // 4][:, (j % 4) * P:(j % 4 + 1) * P], v(j), ident[:, :])
                i.then_inc(s.zt, 1)

            def from_z(j):
                return flat(zc[:, 2 * j:2 * j + 2, :])

            def stage2(c):
                turn(n2, c + 1, from_z)
                product(n2, c + 1, w1_bd, b1_row)

            def stage3(c):
                turn(n3, 2 * c + 1, from_z)
                product(n3, 2 * c + 1, w2_bd, b2_row)
                turn(n3, 2 * c + 2, from_z)
                pe.wait_ge(n3.ztc, 4 * c + 4)
                for j in range(HT):
                    if j >= 4:
                        pe.wait_ge(qkv_copied, c * HT + (j - 3))
                    pe.matmul(bank[4 + j % 4][:, 0:6 * F], ones_row[:, :], bqkv_row[:, :], start=True, stop=False)
                    pe.matmul(bank[4 + j % 4][:, 0:6 * F], zT[:, j * P:(j + 1) * P], wqkv_bd[:, :], start=False, stop=True)\
                      .then_inc(qkv_mm, 1)

            def stage4(c):
                turn(n4, c + 1, from_z)
                product(n4, c + 1, wo_bd, bo_row)

            seam_turn(edge_seam, 2, carry[:, :], e_carry)
            seam_turn(edge_seam, 3, carry[:, :], e_carry)
            chunks(pe, NC, stage2)
            seam_turn(edge_seam, 4, carry[:, :], e_carry)
            chunks(pe, NC, stage3)
            pe.wait_ge(a_tail, 1)
            pe.transpose(bank[6][0:A3, 0:P], seam_m[:, 0, 0:A3], ident[:, :])
            pe.transpose(bank[5][0:A3, 0:P], seam_m[:, 1, 0:A3], ident[:, :]).then_inc(a_seam.t, 1)
            pe.wait_ge(a_seam.scan, 1)
            pe.transpose(bank[7][:, 0:A3], seam_m[0:A3, 5, :], ident[0:A3, 0:A3])
            pe.transpose(bank[4][:, 0:A3], seam_m[0:A3, 2, :], ident[0:A3, 0:A3]).then_inc(a_seam.back, 1)
            chunks(pe, NC, stage4)

        @block.vector
        def _(dve):
            ch = Chain(dve, s_chain)
            for w in (w1_bd, w2_bd, wo_bd, wqkv_bd, we1_bd, we2_bd, carry, carry_ea, carry_q):
                dve.memset(w[:, :], 0.0)
            dve.memset(blk_idx[:, :], 0)
            ch(dve.memset(ones_row[:, :], 1.0))
            dve.sem_inc(s_zeroed, 1)
            dve.wait_ge(s_dst, 16)
            ch(dve.tensor_copy(dst_f, dst_i))
            ch(dve.tensor_copy(first_idx[:, :], dst_i[:, 0:1]))
            for i, c in enumerate((0, EP - 1)):
                ch(dve.tensor_copy(ends_bc[:, i, :], dst_f[:, c:c + 1].to_broadcast([P, P])))
            dve.sem_inc(s_ends, 1)
            dve.memset(inside[:, 0:1], 0.0)
            ch(dve.tensor_tensor(inside[:, 1:EP], dst_f[:, 1:EP], dst_f[:, 0:EP - 1], ALU.is_equal))
            ch(dve.tensor_scalar(junk, dst_f, dst_f[:, 0:1], 0.0, ALU.is_equal, ALU.add, accum_out=small[:, 1:2]))
            dve.wait_ge(s_iota, 2)
            ch(dve.tensor_scalar(small[:, 2:3], small[:, 0:1], float(EP), -1.0, ALU.mult, ALU.add))
            ch(dve.tensor_tensor(seam_idx[:, :], small[:, 2:3], small[:, 1:2], ALU.add))
            dve.wait_ge(s_ends_bc, 2)
            first, last = bank[6][:, 0:P], bank[7][:, 0:P]
            ch(dve.tensor_copy(ends_bc[:, 0, :], first))
            ch(dve.memset(same[:, 0:1], 0.0))
            ch(dve.tensor_tensor(same[:, 1:P], ends_bc[:, 0, 1:P], last[:, 0:P - 1], ALU.is_equal))
            ch(dve.memset(through[:, 0:1], 0.0))
            ch(dve.tensor_tensor(through[:, 1:P], ends_bc[:, 0, 0:P - 1], last[:, 0:P - 1], ALU.is_equal))
            ch(dve.tensor_tensor(through[:, :], through[:, :], same[:, :], ALU.mult))
            for a, b in ((same, same_neg), (through, through_neg)):
                ch(dve.tensor_scalar(b[:, :], a[:, :], 1.0, None, ALU.subtract))
            dve.wait_ge(s_samp_f, 3)
            with dve.Fori(0, NT) as t:
                dve.tensor_scalar(junk[:, 0:NR], samp_bc, node_id[:, bass.ds(t, 1)], 0.0, ALU.is_lt, ALU.add,
                                  accum_out=cnt[:, bass.ds(t, 1)]).then_inc(s_search, 1)
                dve.wait_ge(s_search, t + 1)
            ch(dve.tensor_scalar(blk_base[:, :], cnt[:, :], 1.0, 0.0, ALU.subtract, ALU.max))
            ch(dve.tensor_copy(blk_idx[:, :], blk_base[:, :]))
            ch(dve.tensor_scalar(blk_base[:, :], blk_base[:, :], float(DB), None, ALU.mult))
            dve.sem_inc(s_level1, 1)
            dve.sem_inc(s_setup_done, 1)

            def run_scan(p, buf, c, mask, chain, maximum):
                for f in range(F):
                    i = dve.tensor_tensor_scan(buf[:, :, f], mask, buf[:, :, f], c[:, f:f + 1],
                                               ALU.add if maximum else ALU.mult, ALU.max if maximum else ALU.add)
                return i

            def mask_of(k, out, low=None):
                m = inside[:, bass.ds(k * T, T)]
                if low is None:
                    return dve.tensor_scalar(out, m, 1.0, None, ALU.mult)
                return dve.tensor_scalar(out, m, 1.0, low, ALU.subtract, ALU.mult)

            def edge_pass(p, layer0=False):
                dve.sem_inc(e_carry, 1)
                if layer0:
                    dve.sem_inc(e_carry, 1)
                    dve.sem_inc(ea_carry, 1)

                def step(k, b, n):
                    if layer0:
                        mask_of(k, blk_mask[:, 1, :]).then_inc(e_mask, 1)
                        dve.wait_ge(e_mask, k * 2 + 1)
                        dve.wait_ge(ea_loaded[b], (n + 1) * 16)
                        dve.wait_ge(ea_carry, k + 1)
                        run_scan(p, eat[:, b], carry_ea, blk_mask[:, 1, :], None, False).then_inc(ea_scanned[b], 1)
                        dve.wait_ge(ea_scanned[b], n + 1)
                        dve.tensor_copy(carry_ea[:, :], eat[:, b, T - 1, :]).then_inc(ea_carry, 1)
                        mask_of(k, blk_mask[:, 0, :], BIG).then_inc(e_mask, 1)
                        dve.wait_ge(e_mask, k * 2 + 2)
                    else:
                        mask_of(k, blk_mask[:, 0, :]).then_inc(e_mask, 1)
                        dve.wait_ge(e_mask, k + (p.mask0 + 1))
                    dve.wait_ge(p.gathered[b], (n + 1) * (16 * T))
                    dve.wait_ge(e_carry, k + (p.carry0 + 1))
                    run_scan(p, p.rows[:, b], carry, blk_mask[:, 0, :], None, p.maximum).then_inc(e_scanned[b], 1)
                    dve.wait_ge(e_scanned[b], n + (p.v[b] + 1))
                    dve.tensor_copy(carry[:, :], p.rows[:, b, T - 1, :]).then_inc(e_carry, 1)
                ring(dve, NB, step)

            def seam_scan(sm, i, maximum):
                a, b = (same_neg, through_neg) if maximum else (same, through)
                ch(dve.memset(seam[:, 1, 0:1], -BIG if maximum else 0.0))
                dve.wait_ge(sm.t, i)
                if maximum:
                    ch(dve.tensor_scalar(seam[:, 0, :], a[:, :], BIG, None, ALU.mult))
                    ch(dve.tensor_scalar(seam[:, 2, :], b[:, :], BIG, None, ALU.mult))
                    ch(dve.tensor_tensor(seam[0:F, 0, 1:P], bank[6][0:F, 0:P - 1], seam[0:F, 0, 1:P], ALU.add))
                    ch(dve.tensor_tensor_scan(seam[0:F, 1, 1:P], seam[0:F, 2, 1:P], seam[0:F, 0, 1:P], -BIG, ALU.add, ALU.max))
                else:
                    ch(dve.tensor_tensor(seam[0:F, 0, 1:P], bank[6][0:F, 0:P - 1], a[0:F, 1:P], ALU.mult))
                    ch(dve.tensor_tensor_scan(seam[0:F, 1, 1:P], b[0:F, 1:P], seam[0:F, 0, 1:P], 0.0, ALU.mult, ALU.add))
                dve.sem_inc(sm.scan, 1)

            def seam_add(sm, i, maximum):
                dve.wait_ge(sm.back, i)
                dve.wait_ge(sm.row, 16 * i)
                dve.tensor_tensor(seam_row[:, 0:F], seam_row[:, 0:F], bank[7][:, 0:F],
                                  ALU.max if maximum else ALU.add).then_inc(sm.sum, 1)

            edge_pass(p0, layer0=True)

            for b in range(2):
                dve.sem_inc(s_found_used[b], 1)

            def count(c, b, n):
                dve.wait_ge(s_found_f[b], n + 1)
                for i in range(CT):
                    t = c * CT + i
                    dve.tensor_scalar(junk_s, found_f[:, b, i, :], node_id[:, bass.ds(t, 1)], 0.0, ALU.is_lt, ALU.add,
                                      accum_out=cnt[:, bass.ds(t, 1)]).then_inc(s_search, 1)
                    dve.wait_ge(s_search, t + (NT + 1))
                dve.sem_inc(s_found_used[b], 1)
            ring(dve, NC, count)
            ch(dve.memset(row_first[:, NT:NT + 1], float(E)))
            ch(dve.tensor_tensor(row_first[:, 0:NT], cnt[:, :], blk_base[:, :], ALU.add))
            dve.sem_inc(s_first, 1)
            ch(dve.memset(shift1, 0.0))
            ch(dve.memset(shift2, 0.0))
            ch(dve.tensor_copy(shift1[:, 0:P - 1], ident[:, 1:P]))
            ch(dve.tensor_copy(shift2[:, P - 1:P], ident[:, 0:1]))
            dve.sem_inc(s_shift, 2)
            seam_scan(ea_seam, 1, False)
            dve.wait_ge(ea_seam.back, 1)
            ch(dve.tensor_copy(ln_a[:, 0, :], bank[7][:, 0:F]))
            dve.sem_inc(ea_back_read, 1)
            seam_scan(edge_seam, 1, True)
            seam_add(edge_seam, 1, True)
            dve.wait_ge(edge_seam.put, 16)
            dve.wait_ge(ea_seam.row, 16)
            dve.tensor_tensor(seam_row[:, 0:F], seam_row[:, 0:F], ln_a[:, 0, :], ALU.add).then_inc(ea_seam.sum, 1)
            dve.wait_ge(s_shifted, 1)
            ch(dve.tensor_tensor(deg[:, :], bank[3][:, 0:NT], row_first[:, 0:NT], ALU.subtract))
            ch(dve.tensor_scalar(has[:, :], deg[:, :], 1.0, None, ALU.min))
            ch(dve.tensor_scalar(deg1[:, :], deg[:, :], 1.0, None, ALU.add))
            dve.sem_inc(s_sqrt, 1)
            ch(dve.tensor_scalar(end_idx[:, :], bank[3][:, 0:NT], -1.0, 0.0, ALU.add, ALU.max))
            ch(dve.tensor_scalar(small[:, 3:4], small[:, 0:1], float(E), None, ALU.add))
            ch(dve.tensor_scalar(cnt[:, :], row_first[:, 0:NT], small[:, 3:4], None, ALU.subtract))
            ch(dve.tensor_tensor(cnt[:, :], cnt[:, :], has[:, :], ALU.mult))
            ch(dve.tensor_scalar(q_idx[:, :], cnt[:, :], small[:, 3:4], None, ALU.add))
            dve.wait_ge(s_sqrt, 2)
            ch(dve.reciprocal(dis[:, :], dis[:, :]))
            dve.wait_ge(ea_seam.put, 16)
            ch(dve.memset(xcur[:, NT - 1, :], 0.0))
            dve.sem_inc(x_pad, 1)
            dve.sem_inc(s_nodes, 1)

            def cols(v, c):
                return v[:, bass.ds(c * CT, CT)]

            def norm(s, ch, c):
                ch(dve.reduce_sum(st[:, 0, :], ln_a[:, :, :], AX.X))
                ch(dve.tensor_scalar(st[:, 0, :], st[:, 0, :], 1.0 / F, None, ALU.mult))
                ch(dve.tensor_tensor(ln_a[:, :, :], ln_a[:, :, :], over(st[:, 0, :], F), ALU.subtract))
                ch(dve.tensor_tensor(ln_b[:, :, :], ln_a[:, :, :], ln_a[:, :, :], ALU.mult))
                ch(dve.reduce_sum(st[:, 1, :], ln_b[:, :, :], AX.X))
                ch(dve.tensor_scalar(st[:, 1, :], st[:, 1, :], 1.0 / F, EPS, ALU.mult, ALU.add))
                dve.sem_inc(node_var, 1)
                dve.wait_ge(node_std, c + (s.norm0 + 1))
                ch(dve.reciprocal(st[:, 3, :], st[:, 2, :]))
                ch(dve.tensor_tensor(chunk(xcur, c), ln_a[:, :, :], over(st[:, 3, :], F), ALU.mult))

            def stage0(c, b, n):
                ch = Chain(dve, n0.chain, c * 10)
                dve.wait_ge(n0.got[b], (n + 1) * (16 * CT))
                ch(dve.tensor_tensor(ln_a[:, :, :], chunk(got64, c), over(cols(has, c), F), ALU.mult))
                ch(dve.tensor_tensor(ln_a[:, :, :], ln_a[:, :, :], chunk(xcur, c), ALU.add))
                norm(n0, ch, c)
                assert ch.n == 10
                dve.sem_inc(n0.rows, 1)
            dve.wait_ge(x_loaded, 32)
            ring(dve, NC, stage0)
            dve.memset(zeros_z, 0.0).then_inc(s_zeros, 1)

            edge_pass(p1)
            seam_scan(edge_seam, 2, False)
            seam_add(edge_seam, 2, False)

            def stage1(c, b, n):
                ch = Chain(dve, n1.chain, c * 13)
                dve.wait_ge(n1.got[b], (n + 1) * (2 * 16 * CT))
                ch(dve.tensor_tensor(ln_a[:, :, :], chunk(got64, c), chunk(got_ea, c), ALU.add))
                ch(dve.tensor_tensor(ln_a[:, :, :], ln_a[:, :, :], over(cols(has, c), F), ALU.mult))
                ch(dve.tensor_tensor(ln_b[:, :, :], chunk(xcur, c), over(cols(deg1, c), F), ALU.mult))
                ch(dve.tensor_tensor(ln_a[:, :, :], ln_a[:, :, :], ln_b[:, :, :], ALU.add))
                norm(n1, ch, c)
                ch(dve.tensor_tensor(chunk(tcur, c), chunk(xcur, c), over(cols(dis, c), F), ALU.mult))
                assert ch.n == 13
                dve.sem_inc(n1.rows, 1)
            ring(dve, NC, stage1)

            def conv_in(s, ch, c, b, n):
                dve.wait_ge(s.got[b], (n + 1) * (16 * CT))
                ch(dve.tensor_tensor(zc, chunk(got64, c), over(cols(has, c), F), ALU.mult))
                ch(dve.tensor_tensor(zc, zc, chunk(tcur, c), ALU.add))
                ch(dve.tensor_tensor(zc, zc, over(cols(dis, c), F), ALU.mult))

            def halves():
                for h, (a, e) in enumerate(((0, 8), (8, CT))):
                    yield a, e, bank[2 + h][:, 0:(e - a) * F].rearrange("p (a b) -> p a b", b=F)

            edge_pass(p2)
            seam_scan(edge_seam, 3, False)
            seam_add(edge_seam, 3, False)

            def stage2(c, b, n):
                ch = Chain(dve, n2.chain, c * 5)
                conv_in(n2, ch, c, b, n)
                dve.sem_inc(n2.z, 1)
                dve.wait_ge(n2.mm, c + 1)
                for a, e, v in halves():
                    ch(dve.scalar_tensor_tensor(tcur[:, bass.ds(c * CT + a, e - a), :], v, 0.0,
                                                over(dis[:, bass.ds(c * CT + a, e - a)], F), ALU.max, ALU.mult))
                assert ch.n == 5
                dve.sem_inc(n2.rows, 1)
            ring(dve, NC, stage2)

            edge_pass(p3)
            seam_scan(edge_seam, 4, False)
            seam_add(edge_seam, 4, False)

            def stage3(c, b, n):
                ch = Chain(dve, n3.chain, c * 14)
                conv_in(n3, ch, c, b, n)
                dve.sem_inc(n3.z, 1)
                dve.wait_ge(n3.mm, 2 * 0 + c + 1)
                for a, e, v in halves():
                    ch(dve.tensor_tensor(ln_a[:, a:e, :], v, xcur[:, bass.ds(c * CT + a, e - a), :], ALU.add))
                norm(n3, ch, c)
                ch(dve.tensor_scalar(zc, chunk(xcur, c), 1.0, None, ALU.mult))
                assert ch.n == 14
                dve.sem_inc(n3.z, 1)
                dve.sem_inc(n3.rows, 1)
                dve.wait_ge(n3.zt, 2 * c + 2)
            ring(dve, NC, stage3)

            dve.wait_ge(q_scat, 16 * NT)
            dve.wait_ge(x3_stored, 16 * NC)
            dve.wait_ge(q_tab, 2 * 16 * NC)
            dve.memset(acc[:, 0, :], 0.0).then_inc(a_init, 1)
            for u in range(NS):
                dve.sem_inc(a_free[u], 1)
            KA = 1 + 1 + NS * 7 + 2

            def heads(v):
                return v.rearrange("p a (h d) -> p a h d", h=H)

            def per_feature(v):
                return v.rearrange("p a (h o) -> p a h o", o=1).to_broadcast([P, TS, H, DK])

            def att(k):
                ch = Chain(dve, a_chain, k * KA)
                ch(mask_of(k, blk_mask[:, 0, :]))
                dve.wait_ge(a_q, (k + 1) * 16)
                dve.wait_ge(a_bias, (k + 1) * 16)
                for f in range(F):
                    i = dve.tensor_tensor_scan(qf[:, :, f], blk_mask[:, 0, :], qf[:, :, f], carry_q[:, f:f + 1], ALU.mult, ALU.add)
                ch(i)
                for u in range(NS):
                    t = slice(u * TS, (u + 1) * TS)
                    t1 = slice(1 + u * TS, 1 + (u + 1) * TS)
                    if u == 0:
                        dve.tensor_copy(carry_q[:, :], qf[:, T - 1, :])
                        dve.tensor_scalar(blk_mask[:, 1, :], blk_mask[:, 0, :], 1.0, LOW, ALU.subtract, ALU.mult)
                    dve.wait_ge(a_kv[u], (k + 1) * (16 * TS))
                    ch(dve.tensor_tensor(prod, kv[:, u, :, 0:F], qf[:, t, :], ALU.mult))
                    ch(dve.reduce_sum(score, heads(prod), AX.X))
                    ch(dve.tensor_tensor(score, score, bias_i[:, t, :], ALU.add))
                    if u == 0:
                        dve.wait_ge(a_slot, k + 1)
                    for h in range(H):
                        i = dve.tensor_tensor_scan(acc[:, t1, A3 + h], blk_mask[:, 1, t], score[:, :, h],
                                                   acc[:, u * TS, A3 + h:A3 + h + 1], ALU.add, ALU.max)
                    ch(i)
                    dve.tensor_tensor(arg[:, 0], score, acc[:, t1, A3:W3], ALU.subtract)
                    ch(dve.tensor_tensor(arg[:, 1], acc[:, t, A3:W3], over(blk_mask[:, 1, t], H), ALU.add))
                    ch(dve.tensor_tensor(arg[:, 1], arg[:, 1], acc[:, t1, A3:W3], ALU.subtract))
                    dve.sem_inc(a_arg, 1)
                    if u == NS - 1:
                        dve.sem_inc(a_q_used, 1)
                    dve.wait_ge(a_exp, k * NS + (u + 1))
                    ch(dve.tensor_tensor(heads(acc[:, t1, 0:F]), heads(kv[:, u, :, F:2 * F]),
                                         per_feature(acc[:, t1, F:A3]), ALU.mult))
                    dve.sem_inc(a_free[u], 1)
                for f in range(A3):
                    h = f // DK if f < F else f - F
                    i = dve.tensor_tensor_scan(acc[:, 1:T + 1, f], keepf[:, :, h], acc[:, 1:T + 1, f], acc[:, 0, f:f + 1],
                                               ALU.mult, ALU.add)
                ch(i)
                ch(dve.tensor_copy(acc[:, 0, :], acc[:, T, :]))
                assert ch.n == KA, ch.n
                dve.sem_inc(a_scan, 1)
            dve.wait_ge(a_init, 1)
            chunks(dve, NB, att)

            dve.wait_ge(a_all_stored, 1)

            def spread(out, m):
                dve.tensor_copy(out[:, 0:F].rearrange("p (h d) -> p h d", h=H), m.rearrange("p (h o) -> p h o", o=1).to_broadcast([P, H, DK]))
                return dve.tensor_copy(out[:, F:A3], m)
            dve.tensor_copy(seam_m[:, 0, 0:A3], acc[:, 0, 0:A3])
            ch(spread(seam_m[:, 1, :], acc[:, 0, A3:W3]))
            dve.sem_inc(a_tail, 1)
            dve.wait_ge(a_seam.t, 1)
            q = slice(0, A3)
            aT, mT = bank[6][q, 0:P - 1], bank[5][q, 0:P - 1]
            row = seam_m[q]
            ch(dve.tensor_scalar(seam_m[:, 6, :], same_neg[:, :], LOW, None, ALU.mult))
            ch(dve.tensor_scalar(seam_m[:, 7, :], through_neg[:, :], LOW, None, ALU.mult))
            ch(dve.memset(row[:, 2, 0:1], -LOW))
            ch(dve.tensor_tensor(row[:, 6, 1:P], mT, row[:, 6, 1:P], ALU.add))
            ch(dve.tensor_tensor_scan(row[:, 2, 1:P], row[:, 7, 1:P], row[:, 6, 1:P], -LOW, ALU.add, ALU.max))
            ch(dve.memset(row[:, 3:5, 0:1], 0.0))
            ch(dve.tensor_tensor(row[:, 3, 1:P], row[:, 2, 0:P - 1], row[:, 7, 1:P], ALU.add))
            ch(dve.tensor_tensor(row[:, 3, 1:P], row[:, 3, 1:P], row[:, 2, 1:P], ALU.subtract))
            ch(dve.tensor_tensor(row[:, 4, 1:P], row[:, 6, 1:P], row[:, 2, 1:P], ALU.subtract))
            dve.sem_inc(a_dexp, 1)
            dve.wait_ge(a_dexped, 1)
            ch(dve.tensor_tensor(row[:, 4, 1:P], aT, row[:, 4, 1:P], ALU.mult))
            ch(dve.memset(row[:, 5, 0:1], 0.0))
            ch(dve.tensor_tensor_scan(row[:, 5, 1:P], row[:, 3, 1:P], row[:, 4, 1:P], 0.0, ALU.mult, ALU.add))
            dve.sem_inc(a_seam.scan, 1)
            dve.wait_ge(a_seam.back, 1)
            dve.wait_ge(a_seam.row, 16)
            ch(spread(seam_m[:, 0, :], seam_row[:, A3:W3]))
            ch(dve.tensor_tensor(seam_m[:, 1, 0:A3], seam_m[:, 0, 0:A3], bank[4][:, 0:A3], ALU.max))
            dve.tensor_tensor(seam_m[:, 6, 0:A3], seam_m[:, 0, 0:A3], seam_m[:, 1, 0:A3], ALU.subtract)
            ch(dve.tensor_tensor(seam_m[:, 7, 0:A3], bank[4][:, 0:A3], seam_m[:, 1, 0:A3], ALU.subtract))
            dve.sem_inc(a_dexp, 1)
            dve.wait_ge(a_dexped, 2)
            ch(dve.tensor_tensor(seam_row[:, 0:A3], seam_row[:, 0:A3], seam_m[:, 6, 0:A3], ALU.mult))
            ch(dve.tensor_tensor(seam_m[:, 7, 0:A3], bank[7][:, 0:A3], seam_m[:, 7, 0:A3], ALU.mult))
            ch(dve.tensor_tensor(seam_row[:, 0:A3], seam_row[:, 0:A3], seam_m[:, 7, 0:A3], ALU.add))
            dve.sem_inc(a_seam.sum, 1)

            def stage4(c, b, n):
                ch = Chain(dve, n4.chain, c * 14)
                dve.wait_ge(n4.got[b], (n + 1) * (16 * CT))
                g = chunk(got, c)
                ch(dve.tensor_scalar(rden[:, :, :], g[:, :, F:A3], 1e-12, None, ALU.add))
                ch(dve.reciprocal(rden[:, :, :], rden[:, :, :]))
                ch(dve.tensor_tensor(heads(zc), heads(g[:, :, 0:F]),
                                     rden[:, :, :].rearrange("p a (h o) -> p a h o", o=1).to_broadcast([P, CT, H, DK]), ALU.mult))
                ch(dve.tensor_tensor(zc, zc, over(cols(has, c), F), ALU.mult))
                dve.sem_inc(n4.z, 1)
                dve.wait_ge(n4.mm, c + 1)
                for a, e, v in halves():
                    ch(dve.tensor_tensor(ln_a[:, a:e, :], v, xcur[:, bass.ds(c * CT + a, e - a), :], ALU.add))
                norm(n4, ch, c)
                assert ch.n == 14
                dve.sem_inc(n4.rows, 1)
            dve.wait_ge(x3_loaded, 16)
            ring(dve, NC, stage4)


_INS = ['x', 'src', 'dst', 'edge_attr_32', 'edge_attr_64', 'L2_gnn_W1', 'L2_gnn_b1', 'L2_gnn_W2', 'L2_gnn_b2',
        'L3_gnn_WQ', 'L3_gnn_bQ', 'L3_gnn_WK', 'L3_gnn_bK', 'L3_gnn_WV', 'L3_gnn_bV', 'L3_gnn_WO', 'L3_gnn_bO',
        'L3_gnn_We1', 'L3_gnn_be1', 'L3_gnn_We2', 'L3_gnn_be2']


def kernel(**inputs):
    import numpy as _np
    import concourse.bacc as _bacc
    from concourse import mybir as _mybir
    from concourse.bass_utils import run_bass_kernel_spmd as _run

    nc = _bacc.Bacc("TRN2", target_bir_lowering=False, num_devices=1)
    arrays, args = {}, []
    for name in _INS:
        a = _np.ascontiguousarray(inputs[name])
        arrays[f"in_{name}_dram"] = a
        args.append(nc.dram_tensor(f"in_{name}_dram", a.shape, _mybir.dt.from_np(a.dtype), kind="ExternalInput").ap())
    out = nc.dram_tensor("out_0_dram", inputs["x"].shape, _mybir.dt.float32, kind="ExternalOutput").ap()
    build_gnn(nc, *args, out)
    r = _run(nc, [arrays], core_ids=[0])
    return r.results[0]["out_0_dram"]
```

```python
import concourse.bass as bass
from concourse import mybir
from contextlib import ExitStack

P = 128


def ring(eng, count, step):
    with eng.Fori(0, count // 2) as g:
        step(2 * g, 0, g)
        step(2 * g + 1, 1, g)
    if count % 2:
        step(count - 1, 0, count // 2)


def chunks(eng, count, step):
    with eng.Fori(0, count) as c:
        step(c)


class Chain:

    def __init__(self, eng, sem, base=0):
        self.eng, self.sem, self.base, self.n = eng, sem, base, 0

    def __call__(self, ins):
        self.n += 1
        ins.then_inc(self.sem, 1)
        self.eng.wait_ge(self.sem, self.base + self.n)


def build_gnn(nc, x, src, dst, ea32, ea64, W1, b1, W2, b2, WQ, bQ, WK, bK, WV, bV, WO, bO,
              We1, be1, We2, be2, out):
    F32, I32, BF16, I16 = mybir.dt.float32, mybir.dt.int32, mybir.dt.bfloat16, mybir.dt.int16
    ALU, ACT, AX = mybir.AluOpType, mybir.ActivationFunctionType, mybir.AxisListType

    N, F = x.shape
    E = src.shape[0]
    D32 = ea32.shape[1]
    H = be2.shape[0]
    DK = F // H
    EP = E // P
    T = 125
    NB = EP // T
    TS = 25
    NS = T // TS
    NT = -(-N // P)
    NPAD = NT * P
    LAST = N - (NT - 1) * P
    CT = 14
    NC = NT // CT
    DB = 625
    NR = E // DB
    SC = 7
    W = F
    HB = 2 * NT // 2
    WB = 4
    NBH = P // 2 // WB
    GH = 7
    GC = NT // GH
    GB = 4
    NGR = NT // GB
    G4 = P // D32
    MG = 16
    NG = -(-T // MG)
    JB = MG // G4
    HT = CT // 2
    W3 = F + 2 * H
    A3 = F + H
    BIG = 1.5e38
    LOW = 1.0e30
    EPS = 1e-5

    nc_ctx = ExitStack()
    with nc_ctx as ctx:
        def dram(name, shape, dt=F32):
            return nc.dram_tensor(name, shape, dt).ap()

        def sem(name):
            return ctx.enter_context(nc.semaphore(name))

        tab_x1 = dram("tab_x1", (NPAD, F))
        tab_t2 = dram("tab_t2", (NPAD, F))
        tab_t3 = dram("tab_t3", (NPAD, F))
        tab_x3 = dram("tab_x3", (NPAD, F))
        tab_q = dram("tab_q", (NPAD, F))
        tab_kv = dram("tab_kv", (NPAD, 2 * F))
        scan_max = dram("scan_max", (E, F))
        scan_ea = dram("scan_ea", (E, F))
        scan_x1 = dram("scan_x1", (E, F))
        scan_t2 = dram("scan_t2", (E, F))
        scan_t3 = dram("scan_t3", (E, F))
        scan_att = dram("scan_att", (E, W3))
        q_edge = dram("q_edge", (E + P, F))
        adj = [dram(f"adj{i}", (NT, P, NT // 2, P), BF16) for i in range(2)]

        def keep(name, shape, dt=F32):
            return ctx.enter_context(nc.sbuf_tensor(name, shape, dt))

        inside = keep("inside", [P, EP], BF16)
        ident = keep("ident", [P, P])
        ones_row = keep("ones_row", [1, P])
        node_id = keep("node_id", [P, NT])
        row_first = keep("row_first", [P, NT + 1])
        end_idx = keep("end_idx", [P, NT], I32)
        q_idx = keep("q_idx", [P, NT], I32)
        blk_idx = keep("blk_idx", [P, NT], I32)
        has = keep("has", [P, NT])
        deg = keep("deg", [P, NT])
        dis = keep("dis", [P, NT])
        seam_idx = keep("seam_idx", [P, 1], I32)
        first_idx = keep("first_idx", [P, 1], I32)
        same = keep("same", [P, P])
        through = keep("through", [P, P])
        same_neg = keep("same_neg", [P, P])
        through_neg = keep("through_neg", [P, P])
        carry = keep("carry", [P, F])
        carry_ea = keep("carry_ea", [P, F])
        carry_q = keep("carry_q", [P, F])
        blk_mask = keep("blk_mask", [P, 2, T])
        idx_st = keep("idx_st", [P, 2, T], I32)
        w1_bd = keep("w1_bd", [P, P])
        w2_bd = keep("w2_bd", [P, P])
        wo_bd = keep("wo_bd", [P, P])
        wqkv_bd = keep("wqkv_bd", [P, 2 * 3 * F])
        we1_bd = keep("we1_bd", [P, P])
        we2_bd = keep("we2_bd", [P, G4 * H])
        be1_col = keep("be1_col", [P, 1])
        be2_row = keep("be2_row", [1, H])
        b1_row = keep("b1_row", [1, F])
        b2_row = keep("b2_row", [1, F])
        bo_row = keep("bo_row", [1, F])
        bqkv_row = keep("bqkv_row", [1, 3 * F])
        deg1 = keep("deg1", [P, NT])
        cnt = keep("cnt", [P, NT])
        blk_base = keep("blk_base", [P, NT])
        small = keep("small", [P, 8])
        fold = keep("fold", [P, F])
        lane = keep("lane", [P, P])
        lane_bf = keep("lane_bf", [P, P], BF16)
        flag = keep("flag", [1, 1], I32)
        seam_c = keep("seam_c", [P, F])
        seam_row = keep("seam_row", [P, W3])
        seam = keep("seam", [P, 3, P])
        st = keep("st", [P, 4, CT])
        rden = keep("rden", [P, CT, H])
        ln_a = keep("ln_a", [P, CT, F])
        ln_b = keep("ln_b", [P, CT, F])

        win_idx = keep("win_idx", [P, NT], I32)

        AR = nc.sbuf_bytes_remaining // 4 // 16 * 16 - 64
        arena = keep("arena", [P, AR])
        used = [0]

        def lay(shape, dt=F32, at=None):
            n = 1
            for s in shape[1:]:
                n *= s
            if at is not None:
                used[0] = at
            o = used[0]
            used[0] += -(-n // 16) * 16
            assert used[0] <= AR, (used[0], AR)
            v = arena[:, o:o + n]
            if dt is not F32:
                v = v.bitcast(dt)
            if len(shape) == 2:
                return v
            names = "abcd"[:len(shape) - 1]
            return v.rearrange("p (%s) -> p %s" % (" ".join(names), " ".join(names)),
                               **dict(zip(names, shape[1:])))

        rows0 = lay([P, 2, T, F], at=0)
        rows_end = used[0]
        adj_o = lay([P, 2, NT, P // 2])[:, :, :, :].bitcast(BF16)
        winv = lay([P, NT, W // 2]).bitcast(I16)
        eat = lay([P, T, F])
        zeros_z = lay([P, T * F // 5])
        hot_lo = lay([P, 2, WB, P // 2]).bitcast(BF16)
        hot_hi = lay([P, 2, WB, P // 2]).bitcast(BF16)
        pair_i = lay([P, P // 2]).bitcast(I16)
        pair_f = lay([P, 2, P])
        keys = lay([P, 2, P // 2]).bitcast(BF16)
        dst_i = lay([P, EP], I32, at=rows_end)
        dst_f = lay([P, EP])
        junk = lay([P, EP])
        samp_i = lay([P, NR], I32)
        samp_f = lay([P, NR])
        samp_bc = lay([P, NR])
        ends_bc = lay([P, 2, P])
        found = lay([P, 2, SC, DB], I32, at=rows_end)
        found_f = lay([P, 2, SC, DB])
        junk_s = lay([P, DB])
        shift1 = lay([P, P])
        shift2 = lay([P, P])
        win = lay([P, NT, W], I32, at=rows_end)
        win_m = lay([P, NT, W])
        win_lim = lay([P, 2, NT])
        xcur = lay([P, NT, F], at=0)
        tcur = lay([P, NT, F])
        node_end = used[0]
        got = lay([P, NT, W3])
        got_ea = tcur
        kv_o = lay([P, NT, 2 * F], at=node_end + NT * W3)
        q_o = lay([P, NT, F])
        zc = lay([P, CT, F])
        zT = lay([P, HT * P])
        got64 = arena[:, node_end:node_end + NT * F].rearrange("p (a b) -> p a b", a=NT)
        rows12 = lay([P, 2, T, F], at=node_end)
        parts = lay([P, NT, 3 * F // 2], at=node_end + NT * F).bitcast(BF16)
        adj_i = lay([P, GC // 2, GB, GH * P // 2]).bitcast(BF16)
        sum_a = lay([P, GB * P])
        sum_b = lay([P, GB * P])
        kv = lay([P, NS, TS, 2 * F], at=0)
        qf = lay([P, T, F])
        acc = lay([P, T + 1, W3])
        prod = lay([P, TS, F])
        score = lay([P, TS, H])
        arg = lay([P, 2, TS, H])
        keepf = lay([P, T, H])
        bias_i = lay([P, 2, T, H])
        ea_in = lay([P, T * D32])
        ea_T = lay([P, JB * P])
        mlp_h = lay([P, JB * P])
        seam_m = lay([P, 8, P], at=0)

        psum = ctx.enter_context(nc.psum_tensor("psum", [P, 8, 512], F32))
        bank = [psum[:, i, :] for i in range(8)]

        s_ident = sem("s_ident")
        s_iota = sem("s_iota")
        s_zeroed = sem("s_zeroed")
        s_dst = sem("s_dst")
        s_samp = sem("s_samp")
        s_wt = sem("s_wt")
        s_wt_cp = sem("s_wt_cp")
        s_wt_T = sem("s_wt_T")
        s_ends = sem("s_ends")
        s_ends_bc = sem("s_ends_bc")
        s_samp_f = sem("s_samp_f")
        s_samp_bc = sem("s_samp_bc")
        s_chain = sem("s_chain")
        s_setup_done = sem("s_setup_done")
        s_level1 = sem("s_level1")
        s_found = [sem(f"s_found{i}") for i in range(2)]
        s_found_f = [sem(f"s_found_f{i}") for i in range(2)]
        s_found_used = [sem(f"s_found_used{i}") for i in range(2)]
        s_search = sem("s_search")
        s_first = sem("s_first")
        s_shift = sem("s_shift")
        s_shifted = sem("s_shifted")
        s_sqrt = sem("s_sqrt")

        e_idx = [sem(f"edge_idx{i}") for i in range(2)]
        e_scanned = [sem(f"edge_scanned{i}") for i in range(2)]
        e_stored = [sem(f"edge_stored{i}") for i in range(2)]
        e_free = [sem(f"edge_free{i}") for i in range(2)]
        e_mask = sem("edge_mask")
        e_carry = sem("edge_carry_saved")
        e_all_stored = sem("edge_all_stored")
        e_table = sem("edge_table_stored")
        node_var = sem("node_var")
        node_std = sem("node_std")

        class Seam:
            def __init__(self, name):
                self.t = sem(f"{name}_seam_transposed")
                self.scan = sem(f"{name}_seam_scanned")
                self.back = sem(f"{name}_seam_back")
                self.row = sem(f"{name}_seam_row")
                self.sum = sem(f"{name}_seam_sum")
                self.put = sem(f"{name}_seam_put")

        edge_seam = Seam("edge")

        gathered = [[sem(f"edge_gathered{j}{i}") for i in range(2)] for j in range(2)]

        class EdgePass:
            def __init__(self, i, name, table, scan, maximum, rows):
                self.i, self.table, self.scan, self.maximum, self.rows = i, table, scan, maximum, rows
                self.v = [i * ((NB + 1) // 2), i * (NB // 2)]
                self.gathered = gathered[i // 2]
                self.g0 = [v * T * 16 for v in ((NB + 1) // 2, NB // 2)] if i % 2 else [0, 0]
                self.mask0 = NB * (i + 1) if i else 0
                self.carry0 = i * (NB + 1) + 1

        node_rows = sem("node_rows")
        node_z = sem("node_z")
        node_zt = sem("node_z_transposed")
        node_ztc = sem("node_zt_copied")
        node_chain = sem("node_chain")
        node_mm = sem("node_product")
        got_sems = {k: [sem(f"{k}_got{i}") for i in range(2)] for k in ("n0", "layer", "n4")}

        class NodeStage:
            def __init__(self, chain0, norm0, rows0, z0, mm0, got, got0):
                self.norm0, self.rows0, self.z0, self.mm0 = norm0 * NC, rows0 * NC, z0 * NC, mm0 * NC
                self.chain0 = chain0 * NC
                self.got = got_sems[got]
                self.got0 = [got0 * ((NC + 1) // 2), got0 * (NC // 2)]

        p0 = EdgePass(0, "max", x, scan_max, True, rows0)
        p1 = EdgePass(1, "sum1", tab_x1, scan_x1, False, rows12)
        p2 = EdgePass(2, "sum2", tab_t2, scan_t2, False, rows12)
        p3 = EdgePass(3, "sum3", tab_t3, scan_t3, False, rows12)
        n0 = NodeStage(0, 0, 0, 0, 0, "n0", 0)
        n1 = NodeStage(10, 1, 1, 0, 0, "layer", 0)
        n2 = NodeStage(23, 2, 2, 0, 0, "layer", 1)
        n3 = NodeStage(27, 2, 3, 1, 1, "layer", 2)
        n4 = NodeStage(40, 3, 4, 3, 2, "n4", 0)
        ea_seam, a_seam = Seam("ea"), Seam("att")
        ea_loaded = sem("ea_loaded")
        ea_scanned = sem("ea_scanned")
        ea_stored = sem("ea_stored")
        ea_carry = sem("ea_carry")
        mlp_in = sem("mlp_in")
        mlp_T = sem("mlp_T")
        mlp_Tc = sem("mlp_Tc")
        mlp_z = sem("mlp_z")
        mlp_a = sem("mlp_a")
        mlp_b = sem("mlp_b")
        mlp_bc = sem("mlp_bc")
        s_zero_edge = sem("s_zero_edge")
        ea_got = [sem(f"ea_got{i}") for i in range(2)]
        s_win = sem("s_win")
        s_win_idx = sem("s_win_idx")
        s_flag_in = sem("s_flag_in")
        s_flag_T = sem("s_flag_T")
        s_flag = sem("s_flag")
        b_pair = sem("b_pair")
        b_turned = sem("b_turned")
        b_keys = sem("b_keys")
        b_hot = sem("b_hot")
        b_count = sem("b_count")
        b_out = sem("b_out")
        b_stored = [sem(f"b_stored{i}") for i in range(2)]
        m_split = sem("m_split")
        m_used = sem("m_used")
        m_loaded = [sem(f"m_loaded{i}") for i in range(GC // 2)]
        m_done = sem("m_done")
        m_copied = sem("m_copied")
        m_folded = sem("m_folded")
        m_got = sem("m_got")
        x_loaded = sem("x_loaded")
        x_pad = sem("x_pad")
        x3_loaded = sem("x3_loaded")
        x3_stored = sem("x3_stored")
        qkv_mm = sem("qkv_mm")
        qkv_copied = sem("qkv_copied")
        q_tab = sem("q_tab")
        q_scat = sem("q_scat")
        q_first = sem("q_first")
        q_first_put = sem("q_first_put")
        a_idx = [sem(f"a_idx{i}") for i in range(2)]
        a_kv = [sem(f"a_kv{i}") for i in range(NS)]
        a_free = [sem(f"a_free{i}") for i in range(NS)]
        a_init = sem("a_init")
        a_slot = sem("a_slot")
        ea_back_read = sem("ea_back_read")
        a_q = sem("a_q")
        a_chain = sem("a_chain")
        a_q_used = sem("a_q_used")
        a_arg = sem("a_arg")
        a_exp = sem("a_exp")
        a_scan = sem("a_scan")
        a_stored = sem("a_stored")
        a_all_stored = sem("a_all_stored")
        a_tail = sem("a_tail")
        a_dexp = sem("a_dexp")
        a_dexped = sem("a_dexped")
        out_rows = sem("out_rows")
        m_chain = sem("m_chain")
        slow_chain = sem("slow_chain")
        b_chain = sem("b_chain")
        s_slow = sem("s_slow")
        begun = sem("begun")

        src_v = src.rearrange("(p t) -> p t", p=P)
        dst_v = dst.rearrange("(p t) -> p t", p=P)
        dst_rows = dst.rearrange("(r c) -> r c", c=DB)
        ea64_v = ea64.rearrange("(p t) f -> p (t f)", p=P)
        ea32_v = ea32.rearrange("(p t) f -> p (t f)", p=P)
        q_edge_v = q_edge[0:E, :].rearrange("(p t) f -> p (t f)", p=P)

        def scan_v(s):
            return s.rearrange("(p t) f -> p (t f)", p=P)

        def tiles(t):
            return t.rearrange("(t p) f -> p t f", p=P)

        def flat(v):
            return v.rearrange("p a b -> p (a b)")

        def over(v, n):
            a = v.shape[1]
            return v.rearrange("p (a o) -> p a o", o=1).to_broadcast([v.shape[0], a, n])

        def chunk(v, c):
            return v[:, bass.ds(c * CT, CT), :]

        n_weights = 2 * 6 + G4 * 3 + 4 + 3

        block = ctx.enter_context(nc.Block())

        @block.sync
        def _(sp):
            sp.dma_start(dst_i, dst_v).then_inc(s_dst, 16)
            sp.dma_start(samp_i[0:1, :], dst.rearrange("(o r c) -> o r c", o=1, c=DB)[:, :, 0],
                         allow_slow_non_contiguous=True).then_inc(s_samp, 16)
            sp.wait_ge(s_zeroed, 1)
            nw = 0
            for h in range(2):
                d = slice(h * F, (h + 1) * F)
                for w, o in ((W1, w1_bd), (W2, w2_bd), (WO, wo_bd)):
                    sp.dma_start(o[d, d], w).then_inc(s_wt, 16)
                for i, w in enumerate((WQ, WK, WV)):
                    a = h * 3 * F + i * F
                    sp.dma_start(wqkv_bd[d, a:a + F], w).then_inc(s_wt, 16)
                nw += 6
            for i in range(G4):
                d = slice(i * D32, (i + 1) * D32)
                sp.dma_start(we1_bd[d, d], We1).then_inc(s_wt, 16)
                sp.dma_start(we2_bd[d, i * H:(i + 1) * H], We2).then_inc(s_wt, 16)
                sp.dma_start(be1_col[d, :], be1.rearrange("(p o) -> p o", o=1)).then_inc(s_wt, 16)
                nw += 3
            for b, o in ((be2, be2_row[:, :]), (b1, b1_row[:, :]), (b2, b2_row[:, :]), (bO, bo_row[:, :]),
                         (bQ, bqkv_row[:, 0:F]), (bK, bqkv_row[:, F:2 * F]), (bV, bqkv_row[:, 2 * F:3 * F])):
                sp.dma_start(o, b.rearrange("(o n) -> o n", o=1)).then_inc(s_wt, 16)
                nw += 1
            assert nw == n_weights

            def edge_pass(p, layer0=False):
                for k in range(2):
                    sp.dma_start(idx_st[:, k, :], src_v[:, k * T:(k + 1) * T]).then_inc(e_idx[k], 16)
                    sp.sem_inc(e_free[k], 1)
                if layer0:
                    sp.wait_ge(s_setup_done, 1)
                    sp.dma_start(flat(eat), ea64_v[:, 0:T * F]).then_inc(ea_loaded, 16)

                def step(k, b, n, more=2):
                    sp.wait_ge(p.gathered[b], (n + 1) * (16 * T) + p.g0[b])
                    if more > 1:
                        sp.dma_start(idx_st[:, b, :], src_v[:, bass.ds((k + 2) * T, T)]).then_inc(e_idx[b], 16)
                    if layer0:
                        sp.wait_ge(ea_scanned, k + 1)
                        sp.dma_start(scan_v(scan_ea)[:, bass.ds(k * (T * F), T * F)], flat(eat)).then_inc(ea_stored, 16)
                        sp.dma_start(q_edge_v[:, bass.ds(k * (T * F), T * F)].rearrange("p (a b) -> p a b", a=5),
                                     zeros_z.rearrange("p (o b) -> p o b", o=1).to_broadcast([P, 5, T * F // 5])).then_inc(s_zero_edge, 16)
                        if more > 0:
                            sp.wait_ge(ea_stored, (k + 1) * 16)
                            sp.wait_ge(ea_carry, k + 2)
                            sp.dma_start(flat(eat), ea64_v[:, bass.ds((k + 1) * (T * F), T * F)]).then_inc(ea_loaded, 16)
                    sp.wait_ge(e_scanned[b], n + (p.v[b] + 1))
                    sp.dma_start(scan_v(p.scan)[:, bass.ds(k * (T * F), T * F)], flat(p.rows[:, b])).then_inc(e_stored[b], 16)
                    sp.wait_ge(e_stored[b], (n + (p.v[b] + 1)) * 16)
                    sp.sem_inc(e_free[b], 1)
                with sp.Fori(0, NB // 2 - 1) as g:
                    step(2 * g, 0, g)
                    step(2 * g + 1, 1, g)
                step(NB - 3, 0, NB // 2 - 1)
                step(NB - 2, 1, NB // 2 - 1, more=1)
                step(NB - 1, 0, NB // 2, more=0)
                if layer0:
                    sp.wait_ge(s_zero_edge, 16 * NB)
                    sp.wait_ge(ea_stored, 16 * NB)
                sp.wait_ge(e_carry, p.carry0 + 1 + NB)
                sp.sem_inc(e_all_stored, 1)

            def product_loads(layer):
                def group(g, nb):
                    for c in range(GC):
                        i = c % (GC // 2)
                        sp.wait_ge(m_used, g * GC + (layer * (NGR + 1) * GC + c + 1))
                        sp.dma_start(adj_i[:, i, 0:nb, :],
                                     adj[c // (GC // 2)][bass.ds(g * GB, nb), :, i * GH:(i + 1) * GH, :]
                                     .rearrange("b p h d -> p b (h d)"))\
                          .then_inc(m_loaded[i], 16)
                with sp.Fori(0, NGR) as g:
                    group(g, GB)
                group(NGR, NT % GB)

            def layer(i, p):
                with sp.If(fast == 1):
                    product_loads(i)
                with sp.Else():
                    edge_pass(p)

            def store_rows(s, done, table, rows):
                def step(c):
                    sp.wait_ge(node_rows, c + (s.rows0 + 1))
                    sp.dma_start(chunk(tiles(table), c), chunk(rows, c)).then_inc(done, 16)
                chunks(sp, NC, step)

            edge_pass(p0, layer0=True)
            sp.wait_ge(s_flag, 1)
            fast = sp.value_load(flag[0:1, 0:1], min_val=0, max_val=1)
            sp.wait_ge(x_pad, 1)
            sp.dma_start(xcur[:, 0:NT - 1, :], x[0:(NT - 1) * P, :].rearrange("(t p) f -> p t f", p=P)).then_inc(x_loaded, 16)
            sp.dma_start(xcur[0:LAST, NT - 1, :], x[(NT - 1) * P:N, :]).then_inc(x_loaded, 16)
            store_rows(n0, e_table, tab_x1, xcur)
            layer(0, p1)
            store_rows(n1, e_table, tab_t2, tcur)
            layer(1, p2)
            store_rows(n2, e_table, tab_t3, tcur)
            layer(2, p3)

            def tables(c):
                sp.wait_ge(node_rows, c + (n3.rows0 + 1))
                sp.dma_start(chunk(tiles(tab_x3), c), chunk(xcur, c)).then_inc(x3_stored, 16)
                sp.wait_ge(qkv_copied, (c + 1) * HT)
                sp.dma_start(chunk(tiles(tab_kv), c), chunk(kv_o, c)).then_inc(q_tab, 16)
                sp.dma_start(chunk(tiles(tab_q), c), chunk(q_o, c)).then_inc(q_tab, 16)
            chunks(sp, NC, tables)
            sp.wait_ge(x3_stored, 16 * NC)
            sp.wait_ge(q_scat, 16 * NT)
            sp.wait_ge(q_first, 16)
            sp.dma_start(q_edge[0:E, :].rearrange("(p t) f -> p t f", p=P)[:, 0, :], seam_row[:, 0:F]).then_inc(q_first_put, 16)
            sp.wait_ge(q_first_put, 16)

            sp.wait_ge(q_tab, 2 * 16 * NC)
            sp.sem_inc(a_slot, 1)
            for k in range(2):
                sp.dma_start(idx_st[:, k, :], src_v[:, k * T:(k + 1) * T]).then_inc(a_idx[k], 16)
            sp.dma_start(flat(qf), q_edge_v[:, 0:T * F]).then_inc(a_q, 16)
            sp.dma_start(ea_in, ea32_v[:, 0:T * D32]).then_inc(mlp_in, 16)

            def att(k, b, n, more=2):
                if more > 0:
                    sp.wait_ge(mlp_bc, (k + 1) * NG)
                    sp.dma_start(ea_in, ea32_v[:, bass.ds((k + 1) * (T * D32), T * D32)]).then_inc(mlp_in, 16)
                if more > 1:
                    for u in range(NS):
                        sp.wait_ge(a_kv[u], (k + 1) * (16 * TS))
                    sp.dma_start(idx_st[:, b, :], src_v[:, bass.ds((k + 2) * T, T)]).then_inc(a_idx[b], 16)
                sp.wait_ge(a_q_used, k + 1)
                if more > 0:
                    sp.dma_start(flat(qf), q_edge_v[:, bass.ds((k + 1) * (T * F), T * F)]).then_inc(a_q, 16)
                sp.wait_ge(a_scan, k + 1)
                sp.dma_start(scan_v(scan_att)[:, bass.ds(k * (T * W3), T * W3)], flat(acc[:, 1:T + 1, :])).then_inc(a_stored, 16)
                sp.wait_ge(a_stored, (k + 1) * 16)
                sp.sem_inc(a_slot, 1)
            with sp.Fori(0, NB // 2 - 1) as g:
                att(2 * g, 0, g)
                att(2 * g + 1, 1, g)
            att(NB - 3, 0, NB // 2 - 1)
            att(NB - 2, 1, NB // 2 - 1, more=1)
            att(NB - 1, 0, NB // 2, more=0)
            sp.wait_ge(a_stored, 16 * NB)
            sp.sem_inc(a_all_stored, 1)
            sp.wait_ge(a_seam.put, 16)
            sp.dma_start(xcur, tiles(tab_x3)).then_inc(x3_loaded, 16)

            with sp.Fori(0, NC - 1) as c:
                sp.wait_ge(node_rows, c + (n4.rows0 + 1))
                sp.dma_start(out[bass.ds(c * (CT * P), CT * P), :].rearrange("(t p) f -> p t f", p=P), chunk(xcur, c)).then_inc(out_rows, 16)
            sp.wait_ge(node_rows, n4.rows0 + NC)
            a = (NC - 1) * CT
            sp.dma_start(out[a * P:(NT - 1) * P, :].rearrange("(t p) f -> p t f", p=P), xcur[:, a:NT - 1, :]).then_inc(out_rows, 16)
            sp.dma_start(out[(NT - 1) * P:N, :], xcur[0:LAST, NT - 1, :]).then_inc(out_rows, 16)
            sp.wait_ge(out_rows, 16 * (NC + 1))

        @block.gpsimd
        def _(pool):
            def gather(dst_ap, table, idx):
                return pool.indirect_dma_start(dst_ap, None, table, bass.IndirectOffsetOnAxis(ap=idx, axis=0))

            def scatter(table, idx, src_ap):
                return pool.indirect_dma_start(table, bass.IndirectOffsetOnAxis(ap=idx, axis=0), src_ap, None)

            pool.memset(ident[:, :], 0.0).then_inc(s_ident, 1)
            pool.iota(node_id[:, :], [[P, NT]], base=0, channel_multiplier=1, allow_small_or_imprecise_dtypes=True).then_inc(s_iota, 1)
            pool.iota(small[:, 0:1], [[0, 1]], base=0, channel_multiplier=1, allow_small_or_imprecise_dtypes=True).then_inc(s_iota, 1)
            pool.iota(lane[:, :], [[1, P]], base=0, channel_multiplier=0, allow_small_or_imprecise_dtypes=True).then_inc(s_iota, 1)
            pool.wait_ge(s_ident, 1)
            pool.affine_select(out=ident[:, :], in_=ident[:, :], compare_op=ALU.not_equal, fill=1.0, base=0,
                               pattern=[[-1, P]], channel_multiplier=1).then_inc(s_ident, 1)
            def edge_block(p, k, b, n):
                pool.wait_ge(e_idx[b], (n + (p.v[b] + 1)) * 16)
                pool.wait_ge(e_free[b], n + (p.v[b] + p.i + 1))
                pool.wait_ge(e_carry, k + p.carry0)
                pool.sem_inc(begun, 1)
                for t in range(T):
                    gather(p.rows[:, b, t, :], p.table, idx_st[:, b, t:t + 1]).then_inc(p.gathered[b], 16)

            def edge_pass(p):
                ring(pool, NB, lambda k, b, n: edge_block(p, k, b, n))

            def seam_fix(scan, sm, i=1, width=F):
                gather(seam_row[:, 0:W3 if width == A3 else F], scan, seam_idx[:, :]).then_inc(sm.row, 16)
                pool.wait_ge(sm.sum, i)
                scatter(scan, seam_idx[:, :], seam_row[:, 0:W3 if width == A3 else F]).then_inc(sm.put, 16)
                pool.wait_ge(sm.put, 16 * i)

            def fetch_nodes(sems, visits, pieces):
                per = 16 * CT * len(pieces)
                for c in range(NC):
                    if c >= 2:
                        pool.wait_ge(sems[c % 2], per * (c // 2 + visits[c % 2]))
                    for t in range(c * CT, (c + 1) * CT):
                        for rows, scan in pieces:
                            gather(rows[:, t, :], scan, end_idx[:, t:t + 1]).then_inc(sems[c % 2], 16)

            edge_block(p0, 0, 0, 0)
            pool.wait_ge(s_level1, 1)
            for c in range(NT // SC):
                if c >= 2:
                    pool.wait_ge(s_found_f[c % 2], c // 2)
                for i in range(SC):
                    t = c * SC + i
                    gather(found[:, c % 2, i, :], dst_rows, blk_idx[:, t:t + 1]).then_inc(s_found[c % 2], 16)
            pool.wait_ge(s_win_idx, 1)
            src_1 = src.rearrange("(e o) -> e o", o=1)
            for t in range(NT):
                gather(win[:, t, :], src_1, win_idx[:, t:t + 1]).then_inc(s_win, 16)
            with pool.Fori(0, NB // 2) as g:
                edge_block(p0, 2 * g + 1, 1, g)
                edge_block(p0, 2 * g + 2, 0, g + 1)
            pool.wait_ge(e_all_stored, 1)
            seam_fix(scan_max, edge_seam, 1)
            seam_fix(scan_ea, ea_seam)
            for b in range(2):
                pool.wait_ge(b_stored[b], 32 * (NT // 2 + 1))
            fetch_nodes(n0.got, n0.got0, [(got64, scan_max)])
            pool.wait_ge(s_flag, 1)
            fast = pool.value_load(flag[0:1, 0:1], min_val=0, max_val=1)

            def layer(s, p, scan):
                with pool.If(fast == 0):
                    edge_pass(p)
                    pool.wait_ge(e_all_stored, p.i + 1)
                    seam_fix(scan, edge_seam, p.i + 1)
                    fetch_nodes(s.got, s.got0, [(got64, scan)])

            pool.wait_ge(e_table, 16 * NC)
            fetch_nodes(ea_got, [0, 0], [(got_ea, scan_ea)])
            layer(n1, p1, scan_x1)
            pool.wait_ge(e_table, 2 * 16 * NC)
            layer(n2, p2, scan_t2)
            pool.wait_ge(e_table, 3 * 16 * NC)
            layer(n3, p3, scan_t3)
            pool.wait_ge(s_zero_edge, 16 * NB)
            pool.wait_ge(qkv_copied, HT * NC)
            for t in range(NT):
                scatter(q_edge, q_idx[:, t:t + 1], q_o[:, t, :]).then_inc(q_scat, 16)
            pool.wait_ge(q_tab, 2 * 16 * NC)
            gather(seam_row[:, 0:F], tab_q, first_idx[:, :]).then_inc(q_first, 16)
            pool.wait_ge(q_scat, 16 * NT)
            pool.wait_ge(x3_stored, 16 * NC)

            def att(k, b, n):
                pool.wait_ge(a_idx[b], (n + 1) * 16)
                for u in range(NS):
                    pool.wait_ge(a_free[u], k + 1)
                    pool.sem_inc(begun, 1)
                    for t in range(TS):
                        i = u * TS + t
                        gather(kv[:, u, t, :], tab_kv, idx_st[:, b, i:i + 1]).then_inc(a_kv[u], 16)
            ring(pool, NB, att)
            pool.wait_ge(a_all_stored, 1)
            seam_fix(scan_att, a_seam, 1, A3)
            fetch_nodes(n4.got, n4.got0, [(got, scan_att)])

        @block.scalar
        def _(act):
            for i, w in enumerate((w1_bd, w2_bd)):
                act.wait_ge(s_wt_T, i + 1)
                act.activation(w[:, :], bank[i][:, 0:P], ACT.Copy).then_inc(s_wt_cp, 1)
            act.wait_ge(s_samp, 16)
            act.activation(samp_f[0:1, :], samp_i[0:1, :], ACT.Copy).then_inc(s_samp_f, 1)
            act.wait_ge(s_samp_bc, 1)
            act.activation(samp_bc[:, 0:512], bank[2][:, :], ACT.Copy).then_inc(s_samp_f, 1)
            act.activation(samp_bc[:, 512:NR], bank[3][:, 0:NR - 512], ACT.Copy).then_inc(s_samp_f, 1)

            def mlp(k, b, n):
                for q in range(NG):
                    act.wait_ge(mlp_T, k * NG + (q + 1))
                    act.activation(ea_T, bank[0], ACT.Copy).then_inc(mlp_Tc, 1)
                    act.wait_ge(mlp_z, k * NG + (q + 1))
                    act.activation(mlp_h, bank[1], ACT.Silu, bias=be1_col[:, :]).then_inc(mlp_a, 1)
                    t0 = min(q * MG, T - MG)
                    act.wait_ge(mlp_b, k * NG + (q + 1))
                    act.activation(flat(bias_i[:, b, t0:t0 + MG, :]), bank[2][:, 0:MG * H], ACT.Copy).then_inc(mlp_bc, 1)

            def conv(c, b, n):
                act.wait_ge(s_found[b], (n + 1) * (16 * SC))
                act.wait_ge(s_found_used[b], n + 1)
                act.activation(flat(found_f[:, b]), flat(found[:, b]), ACT.Copy).then_inc(s_found_f[b], 1)
            ring(act, NT // SC, conv)
            act.wait_ge(s_sqrt, 1)
            act.activation(dis[:, :], deg1[:, :], ACT.Sqrt).then_inc(s_sqrt, 1)

            def pair(j):
                act.wait_ge(b_turned, j + 1)
                act.activation(keys, psum[:, 6, 0:2 * P].rearrange("p (a b) -> p a b", a=2), ACT.Copy).then_inc(b_keys, 1)
                for h in range(2):
                    act.wait_ge(b_stored[h], j * 32 + 32)
                    act.sem_inc(begun, 1)
                    with act.Fori(0, NBH // 2) as q:
                        for i in range(2):
                            m = j * (2 * NBH) + (2 * q + (h * NBH + i))
                            act.wait_ge(b_count, m + 3)
                            o = adj_o[:, h, :, :].rearrange("p h (a w) -> p a h w", a=2)
                            act.activation(o[:, :, :, bass.ds((2 * q + i) * WB, WB)],
                                           psum[:, 2 * i:2 * i + 2, 0:WB * NT].rearrange("p a (w h) -> p a h w", w=WB),
                                           ACT.Copy).then_inc(b_out, 1)
                    act.wait_ge(b_out, j * (2 * NBH) + ((h + 1) * NBH + 2))
                    for i, a in enumerate(adj):
                        act.dma_start(a[bass.ds(2 * j + h, 1), :, :, :].rearrange("b p h d -> p (b h d)"),
                                      flat(adj_o[:, h, i * (NT // 2):(i + 1) * (NT // 2), :])).then_inc(b_stored[h], 16)
            act.sem_inc(b_out, 2)
            for h in range(2):
                act.sem_inc(b_stored[h], 32)
            chunks(act, NT // 2, pair)
            act.wait_ge(s_flag, 1)
            fast = act.value_load(flag[0:1, 0:1], min_val=0, max_val=1)

            def product_copies(layer):
                def group(g, b, nb):
                    act.wait_ge(m_done, g + (layer * (NGR + 1) + 1))
                    for v, k in ((sum_a, 2 * b), (sum_b, 2 * b + 1)):
                        for j in range(nb // 2):
                            c = slice(j * 2 * P, (j + 1) * 2 * P)
                            i = act.activation(v[:, c].rearrange("p (a h w) -> p h a w", a=2, h=2),
                                               bank[k][:, c].rearrange("p (h a w) -> p h a w", a=2, h=2), ACT.Copy)
                    i.then_inc(m_copied, 1)
                with act.Fori(0, NGR // 2) as g:
                    group(2 * g, 0, GB)
                    group(2 * g + 1, 1, GB)
                group(NGR, 0, NT % GB)

            def layer(i):
                with act.If(fast == 1):
                    product_copies(i)

            def std(s, c):
                act.wait_ge(node_var, c + (s.norm0 + 1))
                act.activation(st[:, 2, :], st[:, 1, :], ACT.Sqrt).then_inc(node_std, 1)

            def copies(s, z):
                act.wait_ge(node_zt, z + s.z0)
                act.activation(zT[:, 0:4 * P], bank[0][:, :], ACT.Copy).then_inc(node_ztc, 1)
                act.activation(zT[:, 4 * P:HT * P], bank[1][:, 0:(HT - 4) * P], ACT.Copy).then_inc(node_ztc, 1)

            chunks(act, NC, lambda c: std(n0, c))
            layer(0)
            chunks(act, NC, lambda c: std(n1, c))
            layer(1)
            chunks(act, NC, lambda c: copies(n2, c + 1))
            layer(2)

            def stage3(c):
                copies(n3, 2 * c + 1)
                std(n3, c)
                copies(n3, 2 * c + 2)
                for j in range(HT):
                    act.wait_ge(qkv_mm, c * HT + (j + 1))
                    v = bank[4 + j % 4][:, 0:6 * F].rearrange("p (a b) -> p a b", a=2)
                    act.activation(kv_o[:, bass.ds(c * CT + 2 * j, 2), :], v[:, :, F:3 * F], ACT.Copy)
                    act.activation(q_o[:, bass.ds(c * CT + 2 * j, 2), :], v[:, :, 0:F], ACT.Copy,
                                   scale=float(DK) ** -0.5).then_inc(qkv_copied, 1)
            chunks(act, NC, stage3)

            def att(k):
                for u in range(NS):
                    act.wait_ge(a_arg, k * NS + (u + 1))
                    act.activation(acc[:, 1 + u * TS:1 + (u + 1) * TS, F:A3], arg[:, 0], ACT.Exp)
                    act.activation(keepf[:, u * TS:(u + 1) * TS, :], arg[:, 1], ACT.Exp).then_inc(a_exp, 1)
            mlp(0, 0, 0)
            with act.Fori(0, NB // 2) as g:
                mlp(2 * g + 1, 1, g)
                att(2 * g)
                mlp(2 * g + 2, 0, g + 1)
                att(2 * g + 1)
            att(NB - 1)
            act.wait_ge(a_dexp, 1)
            act.activation(seam_m[0:A3, 3:5, :], seam_m[0:A3, 3:5, :], ACT.Exp).then_inc(a_dexped, 1)
            act.wait_ge(a_dexp, 2)
            act.activation(seam_m[:, 6:8, 0:A3], seam_m[:, 6:8, 0:A3], ACT.Exp).then_inc(a_dexped, 1)

            def stage4(c):
                copies(n4, c + 1)
                std(n4, c)
            chunks(act, NC, stage4)

        @block.tensor
        def _(pe):
            pe.wait_ge(s_ident, 2)
            pe.wait_ge(s_wt, 16 * n_weights)
            for i, w in enumerate((w1_bd, w2_bd)):
                pe.transpose(bank[i][:, 0:P], w[:, :], ident[:, :]).then_inc(s_wt_T, 1)
            pe.wait_ge(s_samp_f, 1)
            pe.wait_ge(s_zeroed, 1)
            pe.matmul(bank[2][:, :], ones_row[:, :], samp_f[0:1, 0:512], start=True, stop=True)
            pe.matmul(bank[3][:, 0:NR - 512], ones_row[:, :], samp_f[0:1, 512:NR], start=True, stop=True).then_inc(s_samp_bc, 1)
            pe.wait_ge(s_ends, 1)
            for i in range(2):
                pe.matmul(bank[6 + i][:, 0:P], ends_bc[:, i, :], ident[:, :], start=True, stop=True).then_inc(s_ends_bc, 1)

            def mlp(k, b, n):
                for q in range(NG):
                    g = k * NG + q
                    t0 = min(q * MG, T - MG)
                    if q == 0:
                        pe.wait_ge(mlp_in, (k + 1) * 16)
                    for j in range(JB):
                        i = pe.transpose(bank[0][:, j * P:(j + 1) * P],
                                         ea_in[:, t0 * D32 + j * P:t0 * D32 + (j + 1) * P], ident[:, :])
                    i.then_inc(mlp_T, 1)
                    pe.wait_ge(mlp_Tc, g + 1)
                    pe.matmul(bank[1], we1_bd[:, :], ea_T, start=True, stop=True).then_inc(mlp_z, 1)
                    pe.wait_ge(mlp_a, g + 1)
                    pe.matmul(bank[2][:, 0:MG * H].rearrange("p (a b) -> p a b", a=MG), ones_row[:, :],
                              be2_row[:, :].rearrange("p (o b) -> p o b", o=1).to_broadcast([1, MG, H]), start=True, stop=False)
                    for j in range(JB):
                        i = pe.matmul(bank[2][:, j * G4 * H:(j + 1) * G4 * H], mlp_h[:, j * P:(j + 1) * P], we2_bd[:, :],
                                      start=False, stop=j == JB - 1)
                    i.then_inc(mlp_b, 1)
                    pe.wait_ge(mlp_bc, g + 1)
            pe.wait_ge(s_wt_cp, 2)
            pe.wait_ge(s_samp_f, 3)
            pe.wait_ge(s_first, 1)
            pe.wait_ge(s_shift, 2)
            pe.matmul(bank[3][:, 0:NT], shift1, row_first[:, 0:NT], start=True, stop=False)
            pe.matmul(bank[3][:, 0:NT], shift2, row_first[:, 1:NT + 1], start=False, stop=True).then_inc(s_shifted, 1)
            pe.wait_ge(s_flag_in, 1)
            pe.transpose(bank[5][0:1, 0:P], small[:, 4:5], ident[:, :]).then_inc(s_flag_T, 1)

            def pair(j):
                pe.wait_ge(b_pair, j + 1)
                for i in range(2):
                    t = pe.transpose(bank[6][:, i * P:(i + 1) * P], pair_f[:, i, :], ident[:, :])
                t.then_inc(b_turned, 1)
                with pe.Fori(0, NBH) as q:
                    for i in range(2):
                        m = j * (2 * NBH) + (2 * q + i)
                        pe.wait_ge(b_hot, m + 1)
                        pe.wait_ge(b_out, m + 1)
                        for w in range(WB):
                            for a in range(2):
                                r = slice(W * a, W * (a + 1))
                                t = pe.matmul(psum[:, 2 * i + a, w * NT:(w + 1) * NT], hot_lo[r, i, w, :], hot_hi[r, i, w, 0:NT],
                                              start=True, stop=True)
                        t.then_inc(b_count, 1)
            pe.sem_inc(b_count, 2)
            chunks(pe, NT // 2, pair)

            def seam_turn(sm, i, tails, ready, extra=1, width=F):
                pe.wait_ge(ready, i * (NB + 1) + extra)
                pe.transpose(bank[6][0:width, 0:P], tails, ident[:, :]).then_inc(sm.t, 1)
                pe.wait_ge(sm.scan, i)
                pe.transpose(bank[7][:, 0:width], seam[0:width, 1, :], ident[0:width, 0:width]).then_inc(sm.back, 1)

            seam_turn(ea_seam, 1, carry_ea[:, :], ea_carry, 0)
            pe.wait_ge(ea_back_read, 1)
            seam_turn(edge_seam, 1, carry[:, :], e_carry)
            pe.wait_ge(s_flag, 1)
            fast = pe.value_load(flag[0:1, 0:1], min_val=0, max_val=1)

            def products(layer):
                def group(g, b, nb):
                    top, low = bank[2 * b][:, 0:nb * P], bank[2 * b + 1][:, 0:nb * P]

                    def cols(t):
                        c, i = divmod(t, GH)
                        return adj_i[:, c % (GC // 2), 0:nb, i * P:(i + 1) * P]

                    for t in range(NT):
                        c = t // GH
                        if t % GH == 0:
                            v = c // (GC // 2) + 1
                            pe.wait_ge(m_loaded[c % (GC // 2)], g * 32 + 16 * (2 * (NGR + 1) * layer + v))
                        pe.matmul(top.rearrange("p (a b) -> p a b", a=nb), parts[:, t, 0:2 * F], cols(t),
                                  start=t == 0, stop=t == NT - 1)
                        if t % 2:
                            for a in range(2):
                                i = pe.matmul(low[F * a:F * (a + 1), :].rearrange("p (a b) -> p a b", a=nb),
                                              parts[:, t - 1 + a, 2 * F:3 * F], cols(t - 1 + a),
                                              start=t == 1, stop=t == NT - 1, tile_position=(0, F * a))
                            n = (t + 1) // GH - (t - 1) // GH
                            if t == NT - 1:
                                i.then_inc(m_done, 1)
                            elif n:
                                i.then_inc(m_used, 1)
                    pe.wait_ge(m_copied, g + (layer * (NGR + 1) + 1))
                    pe.sem_inc(m_used, 1)
                    pe.wait_ge(m_got, g + (layer * (NGR + 1) + 1))
                    for k in range(nb):
                        out_k = bank[4 + b][:, k * F:(k + 1) * F]
                        for n, v in enumerate((sum_a, sum_b)):
                            i = pe.matmul(out_k, v[:, k * P:(k + 1) * P], fold[:, :], start=n == 0, stop=n == 1)
                    i.then_inc(m_folded, 1)
                with pe.Fori(0, NGR // 2) as g:
                    group(2 * g, 0, GB)
                    group(2 * g + 1, 1, GB)
                group(NGR, 0, NT % GB)

            def layer(i):
                with pe.If(fast == 1):
                    if i == 0:
                        pe.sem_inc(m_used, GC // 2)
                    pe.wait_ge(m_split, i + 1)
                    products(i)
                with pe.Else():
                    seam_turn(edge_seam, i + 2, carry[:, :], e_carry)

            def product(s, z, w, brow):
                pe.wait_ge(node_ztc, (z + s.z0) * 2)
                for h, (a, b) in enumerate(((0, 4), (4, HT))):
                    n = 2 * (b - a)
                    pe.matmul(bank[2 + h][:, 0:n * F].rearrange("p (a b) -> p a b", a=n), ones_row[:, :],
                              brow[:, :].rearrange("p (o b) -> p o b", o=1).to_broadcast([1, n, F]), start=True, stop=False)
                    for j in range(a, b):
                        i = pe.matmul(bank[2 + h][:, (j - a) * P:(j - a + 1) * P], zT[:, j * P:(j + 1) * P], w[:, :],
                                      start=False, stop=j == b - 1)
                i.then_inc(node_mm, 1)

            def turn(s, z, v):
                pe.wait_ge(node_z, z + s.z0)
                for j in range(HT):
                    i = pe.transpose(bank[j // 4][:, (j % 4) * P:(j % 4 + 1) * P], v(j), ident[:, :])
                i.then_inc(node_zt, 1)

            def from_z(j):
                return flat(zc[:, 2 * j:2 * j + 2, :])

            def stage2(c):
                turn(n2, c + 1, from_z)
                product(n2, c + 1, w1_bd, b1_row)

            def stage3(c):
                turn(n3, 2 * c + 1, from_z)
                product(n3, 2 * c + 1, w2_bd, b2_row)
                turn(n3, 2 * c + 2, from_z)
                pe.wait_ge(node_ztc, (2 * c + (n3.z0 + 2)) * 2)
                for j in range(HT):
                    if j >= 4:
                        pe.wait_ge(qkv_copied, c * HT + (j - 3))
                    pe.matmul(bank[4 + j % 4][:, 0:6 * F].rearrange("p (a b) -> p a b", a=2), ones_row[:, :],
                              bqkv_row[:, :].rearrange("p (o b) -> p o b", o=1).to_broadcast([1, 2, 3 * F]), start=True, stop=False)
                    pe.matmul(bank[4 + j % 4][:, 0:6 * F], zT[:, j * P:(j + 1) * P], wqkv_bd[:, :], start=False, stop=True)\
                      .then_inc(qkv_mm, 1)

            def stage4(c):
                turn(n4, c + 1, from_z)
                product(n4, c + 1, wo_bd, bo_row)

            layer(0)
            layer(1)
            chunks(pe, NC, stage2)
            layer(2)
            chunks(pe, NC, stage3)
            ring(pe, NB, mlp)
            pe.wait_ge(a_tail, 1)
            pe.transpose(bank[6][0:A3, 0:P], seam_m[:, 0, 0:A3], ident[:, :])
            pe.transpose(bank[5][0:A3, 0:P], seam_m[:, 1, 0:A3], ident[:, :]).then_inc(a_seam.t, 1)
            pe.wait_ge(a_seam.scan, 1)
            pe.transpose(bank[7][:, 0:A3], seam_m[0:A3, 5, :], ident[0:A3, 0:A3])
            pe.transpose(bank[4][:, 0:A3], seam_m[0:A3, 2, :], ident[0:A3, 0:A3]).then_inc(a_seam.back, 1)
            chunks(pe, NC, stage4)

        @block.vector
        def _(dve):
            ch = Chain(dve, s_chain)
            for w in (w1_bd, w2_bd, wo_bd, wqkv_bd, we1_bd, we2_bd, carry, carry_ea, carry_q):
                dve.memset(w[:, :], 0.0)
            dve.memset(blk_idx[:, :], 0)
            ch(dve.memset(ones_row[:, :], 1.0))
            dve.sem_inc(s_zeroed, 1)
            dve.sem_inc(e_carry, 2)
            dve.wait_ge(s_dst, 16)
            ch(dve.tensor_copy(dst_f, dst_i))
            ch(dve.tensor_copy(first_idx[:, :], dst_i[:, 0:1]))
            for i, c in enumerate((0, EP - 1)):
                ch(dve.tensor_copy(ends_bc[:, i, :], dst_f[:, c:c + 1].to_broadcast([P, P])))
            dve.sem_inc(s_ends, 1)
            dve.memset(inside[:, 0:1], 0.0)
            ch(dve.tensor_tensor(inside[:, 1:EP], dst_f[:, 1:EP], dst_f[:, 0:EP - 1], ALU.is_equal))
            ch(dve.tensor_scalar(junk, dst_f, dst_f[:, 0:1], 0.0, ALU.is_equal, ALU.add, accum_out=small[:, 1:2]))
            dve.wait_ge(s_iota, 3)
            ch(dve.tensor_scalar(small[:, 2:3], small[:, 0:1], float(EP), -1.0, ALU.mult, ALU.add))
            ch(dve.tensor_tensor(seam_idx[:, :], small[:, 2:3], small[:, 1:2], ALU.add))
            dve.wait_ge(s_ends_bc, 2)
            first, last = bank[6][:, 0:P], bank[7][:, 0:P]
            ch(dve.tensor_copy(ends_bc[:, 0, :], first))
            ch(dve.memset(same[:, 0:1], 0.0))
            ch(dve.tensor_tensor(same[:, 1:P], ends_bc[:, 0, 1:P], last[:, 0:P - 1], ALU.is_equal))
            ch(dve.memset(through[:, 0:1], 0.0))
            ch(dve.tensor_tensor(through[:, 1:P], ends_bc[:, 0, 0:P - 1], last[:, 0:P - 1], ALU.is_equal))
            ch(dve.tensor_tensor(through[:, :], through[:, :], same[:, :], ALU.mult))
            for a, b in ((same, same_neg), (through, through_neg)):
                ch(dve.tensor_scalar(b[:, :], a[:, :], 1.0, None, ALU.subtract))
            dve.wait_ge(s_samp_f, 3)
            with dve.Fori(0, NT) as t:
                dve.tensor_scalar(junk[:, 0:NR], samp_bc, node_id[:, bass.ds(t, 1)], 0.0, ALU.is_lt, ALU.add,
                                  accum_out=cnt[:, bass.ds(t, 1)]).then_inc(s_search, 1)
                dve.wait_ge(s_search, t + 1)
            ch(dve.tensor_scalar(blk_base[:, :], cnt[:, :], 1.0, 0.0, ALU.subtract, ALU.max))
            ch(dve.tensor_copy(blk_idx[:, :], blk_base[:, :]))
            dve.tensor_copy(lane_bf[:, :], lane[:, :])
            dve.wait_ge(s_ident, 2)
            ch(dve.tensor_tensor(fold[:, :], ident[:, 0:F], ident[:, F:P], ALU.add))
            ch(dve.tensor_scalar(blk_base[:, :], blk_base[:, :], float(DB), None, ALU.mult))
            dve.sem_inc(s_level1, 1)

            def run_scan(p, buf, c, mask, chain, maximum):
                for f in range(F):
                    i = dve.tensor_tensor_scan(buf[:, :, f], mask, buf[:, :, f], c[:, f:f + 1],
                                               ALU.add if maximum else ALU.mult, ALU.max if maximum else ALU.add)
                return i

            def mask_of(k, out, low=None):
                m = inside[:, bass.ds(k * T, T)]
                if low is None:
                    return dve.tensor_scalar(out, m, 1.0, None, ALU.mult)
                return dve.tensor_scalar(out, m, 1.0, low, ALU.subtract, ALU.mult)

            def gather_scan(p, k, b, n):
                dve.wait_ge(p.gathered[b], (n + 1) * (16 * T) + p.g0[b])
                dve.wait_ge(e_carry, k + (p.carry0 + 1))
                run_scan(p, p.rows[:, b], carry, blk_mask[:, 0, :], None, p.maximum).then_inc(e_scanned[b], 1)
                dve.wait_ge(e_scanned[b], n + (p.v[b] + 1))
                dve.tensor_copy(carry[:, :], p.rows[:, b, T - 1, :]).then_inc(e_carry, 1)

            def edge_pass(p):
                dve.sem_inc(e_carry, 1)

                def step(k, b, n):
                    mask_of(k, blk_mask[:, 0, :]).then_inc(e_mask, 1)
                    dve.wait_ge(e_mask, k + (p.mask0 + 1))
                    gather_scan(p, k, b, n)
                ring(dve, NB, step)

            def count_pair(j):
                ch = Chain(dve, b_chain, j * 4)
                two = winv[:, bass.ds(2 * j, 2), :]
                three = "p (a b) -> p a b"
                ch(dve.tensor_scalar(pair_i.rearrange(three, a=2), two, P - 1, None, ALU.bitwise_and))
                ch(dve.tensor_scalar(pair_f[:, 0, :], pair_i, 1.0, None, ALU.mult))
                ch(dve.tensor_scalar(pair_f[:, 1, :], pair_i, 1.0 / P, None, ALU.mult))
                ch(dve.scalar_tensor_tensor(pair_f[:, 1, :].rearrange(three, a=2), two, 1.0 / P,
                                            pair_f[:, 1, :].rearrange(three, a=2), ALU.mult, ALU.subtract))
                dve.sem_inc(b_pair, 1)
                dve.wait_ge(b_keys, j + 1)
                dve.sem_inc(begun, 1)
                with dve.Fori(0, NBH) as q:
                    for i in range(2):
                        m = j * (2 * NBH) + (2 * q + i)
                        dve.wait_ge(b_count, m + 1)
                        for v, out, n in ((0, hot_lo, P), (1, hot_hi, NT)):
                            k = keys[:, v, bass.ds((2 * q + i) * WB, WB)].rearrange("p (w o) -> p w o", o=1)
                            t = dve.tensor_tensor(out[:, i, :, 0:n],
                                                  lane_bf[:, 0:n].rearrange("p (o l) -> p o l", o=1).to_broadcast([P, WB, n]),
                                                  k.to_broadcast([P, WB, n]), ALU.is_equal)
                        t.then_inc(b_hot, 1)

            def pass0():
                dve.sem_inc(ea_carry, 1)

                def step(k, b, n, pairs=2):
                    mask_of(k, blk_mask[:, 1, :]).then_inc(e_mask, 1)
                    mask_of(k, blk_mask[:, 0, :], BIG).then_inc(e_mask, 1)
                    dve.wait_ge(e_mask, k * 2 + 2)
                    dve.wait_ge(ea_loaded, (k + 1) * 16)
                    dve.wait_ge(ea_carry, k + 1)
                    run_scan(p0, eat, carry_ea, blk_mask[:, 1, :], None, False).then_inc(ea_scanned, 1)
                    dve.wait_ge(ea_scanned, k + 1)
                    dve.tensor_copy(carry_ea[:, :], eat[:, T - 1, :]).then_inc(ea_carry, 1)
                    count_pair(2 * k)
                    gather_scan(p0, k, b, n)
                    if pairs > 1:
                        count_pair(2 * k + 1)
                with dve.Fori(0, NB // 2) as g:
                    step(2 * g, 0, g)
                    step(2 * g + 1, 1, g)
                step(NB - 1, 0, NB // 2, pairs=1)

            def seam_scan(sm, i, maximum, ch=ch):
                a, b = (same_neg, through_neg) if maximum else (same, through)
                ch(dve.memset(seam[:, 1, 0:1], -BIG if maximum else 0.0))
                dve.wait_ge(sm.t, i)
                if maximum:
                    ch(dve.tensor_scalar(seam[:, 0, :], a[:, :], BIG, None, ALU.mult))
                    ch(dve.tensor_scalar(seam[:, 2, :], b[:, :], BIG, None, ALU.mult))
                    ch(dve.tensor_tensor(seam[0:F, 0, 1:P], bank[6][0:F, 0:P - 1], seam[0:F, 0, 1:P], ALU.add))
                    ch(dve.tensor_tensor_scan(seam[0:F, 1, 1:P], seam[0:F, 2, 1:P], seam[0:F, 0, 1:P], -BIG, ALU.add, ALU.max))
                else:
                    ch(dve.tensor_tensor(seam[0:F, 0, 1:P], bank[6][0:F, 0:P - 1], a[0:F, 1:P], ALU.mult))
                    ch(dve.tensor_tensor_scan(seam[0:F, 1, 1:P], b[0:F, 1:P], seam[0:F, 0, 1:P], 0.0, ALU.mult, ALU.add))
                dve.sem_inc(sm.scan, 1)

            def seam_add(sm, i, maximum):
                dve.wait_ge(sm.back, i)
                dve.wait_ge(sm.row, 16 * i)
                dve.tensor_tensor(seam_row[:, 0:F], seam_row[:, 0:F], bank[7][:, 0:F],
                                  ALU.max if maximum else ALU.add).then_inc(sm.sum, 1)

            for b in range(2):
                dve.sem_inc(s_found_used[b], 1)

            def count(c, b, n):
                dve.wait_ge(s_found_f[b], n + 1)
                for i in range(SC):
                    t = c * SC + i
                    dve.tensor_scalar(junk_s, found_f[:, b, i, :], node_id[:, bass.ds(t, 1)], 0.0, ALU.is_lt, ALU.add,
                                      accum_out=cnt[:, bass.ds(t, 1)]).then_inc(s_search, 1)
                    dve.wait_ge(s_search, t + (NT + 1))
                dve.sem_inc(s_found_used[b], 1)
            ring(dve, NT // SC, count)
            ch(dve.memset(row_first[:, NT:NT + 1], float(E)))
            ch(dve.tensor_tensor(row_first[:, 0:NT], cnt[:, :], blk_base[:, :], ALU.add))
            dve.sem_inc(s_first, 1)
            ch(dve.tensor_scalar(cnt[:, :], row_first[:, 0:NT], float(E - W), None, ALU.min))
            ch(dve.tensor_copy(win_idx[:, :], cnt[:, :]))
            dve.sem_inc(s_win_idx, 1)
            ch(dve.memset(shift1, 0.0))
            ch(dve.memset(shift2, 0.0))
            ch(dve.tensor_copy(shift1[:, 0:P - 1], ident[:, 1:P]))
            ch(dve.tensor_copy(shift2[:, P - 1:P], ident[:, 0:1]))
            dve.sem_inc(s_shift, 2)
            dve.wait_ge(s_shifted, 1)
            ch(dve.tensor_tensor(deg[:, :], bank[3][:, 0:NT], row_first[:, 0:NT], ALU.subtract))
            ch(dve.tensor_scalar(has[:, :], deg[:, :], 1.0, None, ALU.min))
            ch(dve.tensor_scalar(deg1[:, :], deg[:, :], 1.0, None, ALU.add))
            dve.sem_inc(s_sqrt, 1)
            ch(dve.tensor_scalar(end_idx[:, :], bank[3][:, 0:NT], -1.0, 0.0, ALU.add, ALU.max))
            ch(dve.tensor_tensor(win_lim[:, 0, :], row_first[:, 0:NT], cnt[:, :], ALU.subtract))
            ch(dve.tensor_tensor(win_lim[:, 1, :], win_lim[:, 0, :], deg[:, :], ALU.add))
            ch(dve.tensor_scalar(small[:, 3:4], small[:, 0:1], float(E), None, ALU.add))
            ch(dve.tensor_scalar(cnt[:, :], row_first[:, 0:NT], small[:, 3:4], None, ALU.subtract))
            ch(dve.tensor_tensor(cnt[:, :], cnt[:, :], has[:, :], ALU.mult))
            ch(dve.tensor_scalar(q_idx[:, :], cnt[:, :], small[:, 3:4], None, ALU.add))
            dve.wait_ge(s_sqrt, 2)
            ch(dve.reciprocal(dis[:, :], dis[:, :]))
            ch(dve.reduce_max(small[:, 4:5], deg[:, :], AX.X))
            dve.sem_inc(s_flag_in, 1)
            dve.wait_ge(s_flag_T, 1)
            ch(dve.reduce_max(small[0:1, 5:6], bank[5][0:1, 0:P], AX.X))
            ch(dve.tensor_scalar(flag[:, :], small[0:1, 5:6], float(W), None, ALU.is_le))
            dve.sem_inc(s_flag, 1)
            dve.wait_ge(s_win, 16 * NT)
            lane_w = lane[:, 0:W].rearrange("p (o l) -> p o l", o=1).to_broadcast([P, NT, W])
            ch(dve.tensor_tensor(win_m, lane_w, over(win_lim[:, 1, :], W), ALU.is_lt))
            ch(dve.tensor_scalar(win.bitcast(F32), win, 1.0, None, ALU.add))
            ch(dve.tensor_tensor(win.bitcast(F32), win.bitcast(F32), win_m, ALU.mult))
            ch(dve.tensor_tensor(win_m, lane_w, over(win_lim[:, 0, :], W), ALU.is_ge))
            ch(dve.tensor_tensor(win_m, win.bitcast(F32), win_m, ALU.mult))
            ch(dve.tensor_scalar(winv, win_m, 1.0, None, ALU.subtract))
            ch(dve.memset(zeros_z, 0.0))
            dve.sem_inc(s_setup_done, 1)

            pass0()
            seam_scan(ea_seam, 1, False)
            dve.wait_ge(ea_seam.back, 1)
            ch(dve.tensor_copy(seam_c[:, :], bank[7][:, 0:F]))
            dve.sem_inc(ea_back_read, 1)
            seam_scan(edge_seam, 1, True)
            seam_add(edge_seam, 1, True)
            dve.wait_ge(edge_seam.put, 16)
            dve.wait_ge(ea_seam.row, 16)
            dve.tensor_tensor(seam_row[:, 0:F], seam_row[:, 0:F], seam_c[:, :], ALU.add).then_inc(ea_seam.sum, 1)
            dve.wait_ge(ea_seam.put, 16)
            dve.wait_ge(e_all_stored, 1)
            ch(dve.memset(xcur[:, NT - 1, :], 0.0))
            dve.sem_inc(x_pad, 1)
            fast = dve.value_load(flag[0:1, 0:1], min_val=0, max_val=1)

            def product_rows(layer, cur):
                ch = Chain(dve, m_chain, layer * NC * 5)
                for c in range(NC):
                    t = slice(c * CT, (c + 1) * CT)
                    rest = got64[:, t, :]
                    ch(dve.tensor_copy(parts[:, t, 0:F], cur[:, t, :]))
                    ch(dve.tensor_tensor(rest, cur[:, t, :], parts[:, t, 0:F], ALU.subtract))
                    ch(dve.tensor_copy(parts[:, t, F:2 * F], rest))
                    ch(dve.tensor_tensor(rest, rest, parts[:, t, F:2 * F], ALU.subtract))
                    ch(dve.tensor_copy(parts[:, t, 2 * F:3 * F], rest))
                dve.sem_inc(m_split, 1)
                if layer == 0:
                    dve.sem_inc(m_got, 1)

                def group(g, b, nb):
                    dve.wait_ge(m_folded, g + (layer * (NGR + 1) + 1))
                    dve.tensor_scalar(got64[:, bass.ds(g * GB, nb), :], bank[4 + b][:, 0:nb * F].rearrange("p (a b) -> p a b", a=nb),
                                      1.0, None, ALU.mult).then_inc(m_got, 1)
                with dve.Fori(0, NGR // 2) as g:
                    group(2 * g, 0, GB)
                    group(2 * g + 1, 1, GB)
                group(NGR, 0, NT % GB)
                dve.wait_ge(m_got, (layer + 1) * (NGR + 1) + 1)

            def gathered_rows(p, s):
                edge_pass(p)
                seam_scan(edge_seam, p.i + 1, False, Chain(dve, slow_chain, (p.i - 1) * 3))
                seam_add(edge_seam, p.i + 1, False)

                def step(c, b, n):
                    dve.wait_ge(s.got[b], (n + (s.got0[b] + 1)) * (16 * CT))
                    dve.tensor_tensor(chunk(got64, c), chunk(got64, c), over(cols(has, c), F), ALU.mult).then_inc(s_slow, 1)
                ring(dve, NC, step)
                dve.wait_ge(s_slow, p.i * NC)

            def layer(i, p, s, cur):
                with dve.If(fast == 1):
                    product_rows(i, cur)
                with dve.Else():
                    gathered_rows(p, s)

            def cols(v, c):
                return v[:, bass.ds(c * CT, CT)]

            def norm(s, ch, c):
                ch(dve.reduce_sum(st[:, 0, :], ln_a[:, :, :], AX.X))
                ch(dve.tensor_scalar(st[:, 0, :], st[:, 0, :], 1.0 / F, None, ALU.mult))
                ch(dve.tensor_tensor(ln_a[:, :, :], ln_a[:, :, :], over(st[:, 0, :], F), ALU.subtract))
                ch(dve.tensor_tensor(ln_b[:, :, :], ln_a[:, :, :], ln_a[:, :, :], ALU.mult))
                ch(dve.reduce_sum(st[:, 1, :], ln_b[:, :, :], AX.X))
                ch(dve.tensor_scalar(st[:, 1, :], st[:, 1, :], 1.0 / F, EPS, ALU.mult, ALU.add))
                dve.sem_inc(node_var, 1)
                dve.wait_ge(node_std, c + (s.norm0 + 1))
                ch(dve.reciprocal(st[:, 3, :], st[:, 2, :]))
                ch(dve.tensor_tensor(chunk(xcur, c), ln_a[:, :, :], over(st[:, 3, :], F), ALU.mult))

            def stage0(c, b, n):
                ch = Chain(dve, node_chain, c * 10 + n0.chain0)
                dve.wait_ge(n0.got[b], (n + 1) * (16 * CT))
                ch(dve.tensor_tensor(ln_a[:, :, :], chunk(got64, c), over(cols(has, c), F), ALU.mult))
                ch(dve.tensor_tensor(ln_a[:, :, :], ln_a[:, :, :], chunk(xcur, c), ALU.add))
                norm(n0, ch, c)
                assert ch.n == 10
                dve.sem_inc(node_rows, 1)
            dve.wait_ge(x_loaded, 32)
            ring(dve, NC, stage0)

            dve.wait_ge(e_table, 16 * NC)
            layer(0, p1, n1, xcur)

            def stage1(c, b, n):
                ch = Chain(dve, node_chain, c * 13 + n1.chain0)
                dve.wait_ge(ea_got[b], (n + 1) * (16 * CT))
                ch(dve.tensor_tensor(ln_a[:, :, :], chunk(got_ea, c), over(cols(has, c), F), ALU.mult))
                ch(dve.tensor_tensor(ln_a[:, :, :], ln_a[:, :, :], chunk(got64, c), ALU.add))
                ch(dve.tensor_tensor(ln_b[:, :, :], chunk(xcur, c), over(cols(deg1, c), F), ALU.mult))
                ch(dve.tensor_tensor(ln_a[:, :, :], ln_a[:, :, :], ln_b[:, :, :], ALU.add))
                norm(n1, ch, c)
                ch(dve.tensor_tensor(chunk(tcur, c), chunk(xcur, c), over(cols(dis, c), F), ALU.mult))
                assert ch.n == 13
                dve.sem_inc(node_rows, 1)
            ring(dve, NC, stage1)

            def conv_in(s, ch, c, b, n):
                ch(dve.tensor_tensor(zc, chunk(got64, c), chunk(tcur, c), ALU.add))
                ch(dve.tensor_tensor(zc, zc, over(cols(dis, c), F), ALU.mult))

            def halves():
                for h, (a, e) in enumerate(((0, 8), (8, CT))):
                    yield a, e, bank[2 + h][:, 0:(e - a) * F].rearrange("p (a b) -> p a b", b=F)

            layer(1, p2, n2, tcur)

            def stage2(c, b, n):
                ch = Chain(dve, node_chain, c * 4 + n2.chain0)
                conv_in(n2, ch, c, b, n)
                dve.sem_inc(node_z, 1)
                dve.wait_ge(node_mm, c + (n2.mm0 + 1))
                for a, e, v in halves():
                    ch(dve.scalar_tensor_tensor(tcur[:, bass.ds(c * CT + a, e - a), :], v, 0.0,
                                                over(dis[:, bass.ds(c * CT + a, e - a)], F), ALU.max, ALU.mult))
                assert ch.n == 4
                dve.sem_inc(node_rows, 1)
            ring(dve, NC, stage2)

            layer(2, p3, n3, tcur)

            def stage3(c, b, n):
                ch = Chain(dve, node_chain, c * 13 + n3.chain0)
                conv_in(n3, ch, c, b, n)
                dve.sem_inc(node_z, 1)
                dve.wait_ge(node_mm, c + (n3.mm0 + 1))
                for a, e, v in halves():
                    ch(dve.tensor_tensor(ln_a[:, a:e, :], v, xcur[:, bass.ds(c * CT + a, e - a), :], ALU.add))
                norm(n3, ch, c)
                ch(dve.tensor_scalar(zc, chunk(xcur, c), 1.0, None, ALU.mult))
                assert ch.n == 13
                dve.sem_inc(node_z, 1)
                dve.sem_inc(node_rows, 1)
                dve.wait_ge(node_zt, 2 * c + (n3.z0 + 2))
            ring(dve, NC, stage3)

            dve.wait_ge(q_scat, 16 * NT)
            dve.wait_ge(x3_stored, 16 * NC)
            dve.wait_ge(q_tab, 2 * 16 * NC)
            dve.memset(acc[:, 0, :], 0.0).then_inc(a_init, 1)
            for u in range(NS):
                dve.sem_inc(a_free[u], 1)
            KA = 1 + 1 + NS * 7 + 2

            def heads(v):
                return v.rearrange("p a (h d) -> p a h d", h=H)

            def per_feature(v):
                return v.rearrange("p a (h o) -> p a h o", o=1).to_broadcast([P, TS, H, DK])

            def att(k, b, n):
                ch = Chain(dve, a_chain, k * KA)
                ch(mask_of(k, blk_mask[:, 0, :]))
                dve.wait_ge(a_q, (k + 1) * 16)
                dve.wait_ge(mlp_bc, (k + 1) * NG)
                for f in range(F):
                    i = dve.tensor_tensor_scan(qf[:, :, f], blk_mask[:, 0, :], qf[:, :, f], carry_q[:, f:f + 1], ALU.mult, ALU.add)
                ch(i)
                for u in range(NS):
                    t = slice(u * TS, (u + 1) * TS)
                    t1 = slice(1 + u * TS, 1 + (u + 1) * TS)
                    if u == 0:
                        dve.tensor_copy(carry_q[:, :], qf[:, T - 1, :])
                        dve.tensor_scalar(blk_mask[:, 1, :], blk_mask[:, 0, :], 1.0, LOW, ALU.subtract, ALU.mult)
                    dve.wait_ge(a_kv[u], (k + 1) * (16 * TS))
                    ch(dve.tensor_tensor(prod, kv[:, u, :, 0:F], qf[:, t, :], ALU.mult))
                    ch(dve.reduce_sum(score, heads(prod), AX.X))
                    ch(dve.tensor_tensor(score, score, bias_i[:, b, t, :], ALU.add))
                    if u == 0:
                        dve.wait_ge(a_slot, k + 1)
                    for h in range(H):
                        i = dve.tensor_tensor_scan(acc[:, t1, A3 + h], blk_mask[:, 1, t], score[:, :, h],
                                                   acc[:, u * TS, A3 + h:A3 + h + 1], ALU.add, ALU.max)
                    ch(i)
                    dve.tensor_tensor(arg[:, 0], score, acc[:, t1, A3:W3], ALU.subtract)
                    ch(dve.tensor_tensor(arg[:, 1], acc[:, t, A3:W3], over(blk_mask[:, 1, t], H), ALU.add))
                    ch(dve.tensor_tensor(arg[:, 1], arg[:, 1], acc[:, t1, A3:W3], ALU.subtract))
                    dve.sem_inc(a_arg, 1)
                    if u == NS - 1:
                        dve.sem_inc(a_q_used, 1)
                    dve.wait_ge(a_exp, k * NS + (u + 1))
                    ch(dve.tensor_tensor(heads(acc[:, t1, 0:F]), heads(kv[:, u, :, F:2 * F]),
                                         per_feature(acc[:, t1, F:A3]), ALU.mult))
                    dve.sem_inc(a_free[u], 1)
                for f in range(A3):
                    h = f // DK if f < F else f - F
                    i = dve.tensor_tensor_scan(acc[:, 1:T + 1, f], keepf[:, :, h], acc[:, 1:T + 1, f], acc[:, 0, f:f + 1],
                                               ALU.mult, ALU.add)
                ch(i)
                ch(dve.tensor_copy(acc[:, 0, :], acc[:, T, :]))
                assert ch.n == KA, ch.n
                dve.sem_inc(a_scan, 1)
            dve.wait_ge(a_init, 1)
            ring(dve, NB, att)

            dve.wait_ge(a_all_stored, 1)

            def spread(out, m):
                dve.tensor_copy(out[:, 0:F].rearrange("p (h d) -> p h d", h=H), m.rearrange("p (h o) -> p h o", o=1).to_broadcast([P, H, DK]))
                return dve.tensor_copy(out[:, F:A3], m)
            dve.tensor_copy(seam_m[:, 0, 0:A3], acc[:, 0, 0:A3])
            ch(spread(seam_m[:, 1, :], acc[:, 0, A3:W3]))
            dve.sem_inc(a_tail, 1)
            dve.wait_ge(a_seam.t, 1)
            q = slice(0, A3)
            aT, mT = bank[6][q, 0:P - 1], bank[5][q, 0:P - 1]
            row = seam_m[q]
            ch(dve.tensor_scalar(seam_m[:, 6, :], same_neg[:, :], LOW, None, ALU.mult))
            ch(dve.tensor_scalar(seam_m[:, 7, :], through_neg[:, :], LOW, None, ALU.mult))
            ch(dve.memset(row[:, 2, 0:1], -LOW))
            ch(dve.tensor_tensor(row[:, 6, 1:P], mT, row[:, 6, 1:P], ALU.add))
            ch(dve.tensor_tensor_scan(row[:, 2, 1:P], row[:, 7, 1:P], row[:, 6, 1:P], -LOW, ALU.add, ALU.max))
            ch(dve.memset(row[:, 3:5, 0:1], 0.0))
            ch(dve.tensor_tensor(row[:, 3, 1:P], row[:, 2, 0:P - 1], row[:, 7, 1:P], ALU.add))
            ch(dve.tensor_tensor(row[:, 3, 1:P], row[:, 3, 1:P], row[:, 2, 1:P], ALU.subtract))
            ch(dve.tensor_tensor(row[:, 4, 1:P], row[:, 6, 1:P], row[:, 2, 1:P], ALU.subtract))
            dve.sem_inc(a_dexp, 1)
            dve.wait_ge(a_dexped, 1)
            ch(dve.tensor_tensor(row[:, 4, 1:P], aT, row[:, 4, 1:P], ALU.mult))
            ch(dve.memset(row[:, 5, 0:1], 0.0))
            ch(dve.tensor_tensor_scan(row[:, 5, 1:P], row[:, 3, 1:P], row[:, 4, 1:P], 0.0, ALU.mult, ALU.add))
            dve.sem_inc(a_seam.scan, 1)
            dve.wait_ge(a_seam.back, 1)
            dve.wait_ge(a_seam.row, 16)
            ch(spread(seam_m[:, 0, :], seam_row[:, A3:W3]))
            ch(dve.tensor_tensor(seam_m[:, 1, 0:A3], seam_m[:, 0, 0:A3], bank[4][:, 0:A3], ALU.max))
            dve.tensor_tensor(seam_m[:, 6, 0:A3], seam_m[:, 0, 0:A3], seam_m[:, 1, 0:A3], ALU.subtract)
            ch(dve.tensor_tensor(seam_m[:, 7, 0:A3], bank[4][:, 0:A3], seam_m[:, 1, 0:A3], ALU.subtract))
            dve.sem_inc(a_dexp, 1)
            dve.wait_ge(a_dexped, 2)
            ch(dve.tensor_tensor(seam_row[:, 0:A3], seam_row[:, 0:A3], seam_m[:, 6, 0:A3], ALU.mult))
            ch(dve.tensor_tensor(seam_m[:, 7, 0:A3], bank[7][:, 0:A3], seam_m[:, 7, 0:A3], ALU.mult))
            ch(dve.tensor_tensor(seam_row[:, 0:A3], seam_row[:, 0:A3], seam_m[:, 7, 0:A3], ALU.add))
            dve.sem_inc(a_seam.sum, 1)

            def stage4(c, b, n):
                ch = Chain(dve, node_chain, c * 14 + n4.chain0)
                dve.wait_ge(n4.got[b], (n + 1) * (16 * CT))
                g = chunk(got, c)
                ch(dve.tensor_scalar(rden[:, :, :], g[:, :, F:A3], 1e-12, None, ALU.add))
                ch(dve.reciprocal(rden[:, :, :], rden[:, :, :]))
                ch(dve.tensor_tensor(heads(zc), heads(g[:, :, 0:F]),
                                     rden[:, :, :].rearrange("p a (h o) -> p a h o", o=1).to_broadcast([P, CT, H, DK]), ALU.mult))
                ch(dve.tensor_tensor(zc, zc, over(cols(has, c), F), ALU.mult))
                dve.sem_inc(node_z, 1)
                dve.wait_ge(node_mm, c + (n4.mm0 + 1))
                for a, e, v in halves():
                    ch(dve.tensor_tensor(ln_a[:, a:e, :], v, xcur[:, bass.ds(c * CT + a, e - a), :], ALU.add))
                norm(n4, ch, c)
                assert ch.n == 14
                dve.sem_inc(node_rows, 1)
            dve.wait_ge(x3_loaded, 16)
            ring(dve, NC, stage4)


_INS = ['x', 'src', 'dst', 'edge_attr_32', 'edge_attr_64', 'L2_gnn_W1', 'L2_gnn_b1', 'L2_gnn_W2', 'L2_gnn_b2',
        'L3_gnn_WQ', 'L3_gnn_bQ', 'L3_gnn_WK', 'L3_gnn_bK', 'L3_gnn_WV', 'L3_gnn_bV', 'L3_gnn_WO', 'L3_gnn_bO',
        'L3_gnn_We1', 'L3_gnn_be1', 'L3_gnn_We2', 'L3_gnn_be2']


def kernel(**inputs):
    import numpy as _np
    import concourse.bacc as _bacc
    from concourse import mybir as _mybir
    from concourse.bass_utils import run_bass_kernel_spmd as _run

    nc = _bacc.Bacc("TRN2", target_bir_lowering=False, num_devices=1)
    arrays, args = {}, []
    for name in _INS:
        a = _np.ascontiguousarray(inputs[name])
        arrays[f"in_{name}_dram"] = a
        args.append(nc.dram_tensor(f"in_{name}_dram", a.shape, _mybir.dt.from_np(a.dtype), kind="ExternalInput").ap())
    out = nc.dram_tensor("out_0_dram", inputs["x"].shape, _mybir.dt.float32, kind="ExternalOutput").ap()
    build_gnn(nc, *args, out)
    r = _run(nc, [arrays], core_ids=[0])
    return r.results[0]["out_0_dram"]
```

```python
import concourse.bass as bass
from concourse import mybir
from contextlib import ExitStack

P = 128


def ring(eng, count, step):
    with eng.Fori(0, count // 2) as g:
        step(2 * g, 0, g)
        step(2 * g + 1, 1, g)
    if count % 2:
        step(count - 1, 0, count // 2)


def chunks(eng, count, step):
    with eng.Fori(0, count) as c:
        step(c)


def nothing(*_):
    pass


def in_turn(eng, count, groups, group, start, mid, late, late_at=1, finish=nothing):
    def chunk(c, before):
        for q in range(groups):
            group(c, q)
            if before is not None and q == 0:
                mid(before)
            if before is not None and q == late_at:
                late(before)
        start(c)
    chunk(0, None)
    with eng.Fori(0, count - 1) as c:
        chunk(c + 1, c)
    finish()
    mid(count - 1)
    late(count - 1)


class Chain:

    def __init__(self, eng, sem, base=0):
        self.eng, self.sem, self.base, self.n = eng, sem, base, 0

    def __call__(self, ins):
        self.n += 1
        ins.then_inc(self.sem, 1)
        self.eng.wait_ge(self.sem, self.base + self.n)


def build_gnn(nc, x, src, dst, ea32, ea64, W1, b1, W2, b2, WQ, bQ, WK, bK, WV, bV, WO, bO,
              We1, be1, We2, be2, out):
    F32, I32, BF16, I16 = mybir.dt.float32, mybir.dt.int32, mybir.dt.bfloat16, mybir.dt.int16
    ALU, ACT, AX = mybir.AluOpType, mybir.ActivationFunctionType, mybir.AxisListType

    N, F = x.shape
    E = src.shape[0]
    D32 = ea32.shape[1]
    H = be2.shape[0]
    DK = F // H
    EP = E // P
    T = 125
    NB = EP // T
    TS = 25
    NS = T // TS
    NT = -(-N // P)
    NPAD = NT * P
    LAST = N - (NT - 1) * P
    CT = 14
    NC = NT // CT
    DB = 625
    NR = E // DB
    SC = 7
    W = F
    WB = 4
    NBH = P // 2 // WB
    GH = 7
    GC = NT // GH
    GB = 4
    QB = [GB] * (CT // GB) + [CT % GB]
    NQ = len(QB)
    MS = 4
    G4 = P // D32
    MG = 16
    NG = -(-T // MG)
    JB = MG // G4
    HT = CT // 2
    W3 = F + 2 * H
    A3 = F + H
    BIG = 1.5e38
    LOW = 1.0e30
    EPS = 1e-5

    nc_ctx = ExitStack()
    with nc_ctx as ctx:
        def dram(name, shape, dt=F32):
            return nc.dram_tensor(name, shape, dt).ap()

        def sem(name):
            return ctx.enter_context(nc.semaphore(name))

        tab_x1 = dram("tab_x1", (NPAD, F))
        tab_t2 = dram("tab_t2", (NPAD, F))
        tab_t3 = dram("tab_t3", (NPAD, F))
        tab_x3 = dram("tab_x3", (NPAD, F))
        tab_q = dram("tab_q", (NPAD, F))
        tab_kv = dram("tab_kv", (NPAD, 2 * F))
        scan_max = dram("scan_max", (E, F))
        scan_ea = dram("scan_ea", (E, F))
        scan_x1 = dram("scan_x1", (E, F))
        scan_t2 = dram("scan_t2", (E, F))
        scan_t3 = dram("scan_t3", (E, F))
        scan_att = dram("scan_att", (E, W3))
        q_edge = dram("q_edge", (E + P, F))
        adj = [dram(f"adj{i}", (NT, P, NT // 2, P), BF16) for i in range(2)]

        def keep(name, shape, dt=F32):
            return ctx.enter_context(nc.sbuf_tensor(name, shape, dt))

        inside = keep("inside", [P, EP], BF16)
        ident = keep("ident", [P, P])
        ones_row = keep("ones_row", [1, P])
        node_id = keep("node_id", [P, NT])
        row_first = keep("row_first", [P, NT + 1])
        end_idx = keep("end_idx", [P, NT], I32)
        q_idx = keep("q_idx", [P, NT], I32)
        blk_idx = keep("blk_idx", [P, NT], I32)
        has = keep("has", [P, NT])
        deg = keep("deg", [P, NT])
        dis = keep("dis", [P, NT])
        seam_idx = keep("seam_idx", [P, 1], I32)
        first_idx = keep("first_idx", [P, 1], I32)
        same = keep("same", [P, P])
        through = keep("through", [P, P])
        same_neg = keep("same_neg", [P, P])
        through_neg = keep("through_neg", [P, P])
        carry = keep("carry", [P, F])
        carry_ea = keep("carry_ea", [P, F])
        carry_q = keep("carry_q", [P, F])
        blk_mask = keep("blk_mask", [P, 2, T])
        idx_st = keep("idx_st", [P, 2, T], I32)
        w1_bd = keep("w1_bd", [P, P])
        w2_bd = keep("w2_bd", [P, P])
        wo_bd = keep("wo_bd", [P, P])
        wqkv_bd = keep("wqkv_bd", [P, 2 * 3 * F])
        we1_bd = keep("we1_bd", [P, P])
        we2_bd = keep("we2_bd", [P, G4 * H])
        be1_col = keep("be1_col", [P, 1])
        be2_row = keep("be2_row", [1, H])
        b1_row = keep("b1_row", [1, F])
        b2_row = keep("b2_row", [1, F])
        bo_row = keep("bo_row", [1, F])
        bqkv_row = keep("bqkv_row", [1, 3 * F])
        deg1 = keep("deg1", [P, NT])
        cnt = keep("cnt", [P, NT])
        blk_base = keep("blk_base", [P, NT])
        small = keep("small", [P, 8])
        fold = keep("fold", [P, F])
        lane = keep("lane", [P, P])
        lane_bf = keep("lane_bf", [P, P], BF16)
        flag = keep("flag", [1, 1], I32)
        seam_c = keep("seam_c", [P, F])
        seam_row = keep("seam_row", [P, W3])
        seam = keep("seam", [P, 3, P])
        st = keep("st", [P, 4, CT])
        rden = keep("rden", [P, CT, H])
        ln_a = keep("ln_a", [P, CT, F])
        ln_b = keep("ln_b", [P, CT, F])

        win_idx = keep("win_idx", [P, NT], I32)

        AR = nc.sbuf_bytes_remaining // 4 // 16 * 16 - 64
        arena = keep("arena", [P, AR])
        used = [0]

        def lay(shape, dt=F32, at=None):
            n = 1
            for s in shape[1:]:
                n *= s
            if at is not None:
                used[0] = at
            o = used[0]
            used[0] += -(-n // 16) * 16
            assert used[0] <= AR, (used[0], AR)
            v = arena[:, o:o + n]
            if dt is not F32:
                v = v.bitcast(dt)
            if len(shape) == 2:
                return v
            names = "abcd"[:len(shape) - 1]
            return v.rearrange("p (%s) -> p %s" % (" ".join(names), " ".join(names)),
                               **dict(zip(names, shape[1:])))

        rows0 = lay([P, 2, T, F], at=0)
        rows_end = used[0]
        adj_o = lay([P, 2, NT, P // 2])[:, :, :, :].bitcast(BF16)
        winv = lay([P, NT, W // 2]).bitcast(I16)
        eat = lay([P, T, F])
        zeros_z = lay([P, T * F // 5])
        hot_lo = lay([P, 2, WB, P // 2]).bitcast(BF16)
        hot_hi = lay([P, 2, WB, P // 2]).bitcast(BF16)
        pair_i = lay([P, P // 2]).bitcast(I16)
        pair_f = lay([P, 2, P])
        keys = lay([P, 2, P // 2]).bitcast(BF16)
        dst_i = lay([P, EP], I32, at=rows_end)
        dst_f = lay([P, EP])
        junk = lay([P, EP])
        samp_i = lay([P, NR], I32)
        samp_f = lay([P, NR])
        samp_bc = lay([P, NR])
        ends_bc = lay([P, 2, P])
        found = lay([P, 2, SC, DB], I32, at=rows_end)
        found_f = lay([P, 2, SC, DB])
        junk_s = lay([P, DB])
        shift1 = lay([P, P])
        shift2 = lay([P, P])
        win = lay([P, NT, W], I32, at=rows_end)
        win_m = lay([P, NT, W])
        win_lim = lay([P, 2, NT])
        xcur = lay([P, NT, F], at=0)
        tcur = lay([P, NT, F])
        node_end = used[0]
        got = lay([P, NT, W3])
        got_ea = tcur
        zc = lay([P, CT, F], at=AR - CT * F * 5 - 16)
        zT = lay([P, HT * P])
        kv_o = lay([P, CT, 2 * F])
        q_o = lay([P, CT, F])
        got64 = arena[:, node_end:node_end + NT * F].rearrange("p (a b) -> p a b", a=NT)
        rows12 = lay([P, 2, T, F], at=node_end)
        parts = lay([P, NT, 3 * F // 2], at=node_end + NT * F).bitcast(BF16)
        adj_i = lay([P, MS, GB, GH * P // 2]).bitcast(BF16)
        sum_a = lay([P, GB * P])
        sum_b = lay([P, GB * P])
        assert used[0] <= AR - CT * F * 5 - 16
        kv = lay([P, NS, TS, 2 * F], at=0)
        qf = lay([P, T, F])
        acc = lay([P, T + 1, W3])
        prod = lay([P, TS, F])
        score = lay([P, TS, H])
        arg = lay([P, 2, TS, H])
        keepf = lay([P, T, H])
        bias_i = lay([P, 2, T, H])
        ea_in = lay([P, T * D32])
        ea_T = lay([P, JB * P])
        mlp_h = lay([P, JB * P])
        seam_m = lay([P, 8, P], at=0)

        psum = ctx.enter_context(nc.psum_tensor("psum", [P, 8, 512], F32))
        bank = [psum[:, i, :] for i in range(8)]
        sums = ((bank[0], bank[1]), (bank[3], bank[4]))
        turned = [(7, 0, 4), (2, GB * F, 2), (6, 3 * P, 1)]

        s_ident = sem("s_ident")
        s_iota = sem("s_iota")
        s_zeroed = sem("s_zeroed")
        s_dst = sem("s_dst")
        s_samp = sem("s_samp")
        s_wt = sem("s_wt")
        s_wt_cp = sem("s_wt_cp")
        s_wt_T = sem("s_wt_T")
        s_ends = sem("s_ends")
        s_ends_bc = sem("s_ends_bc")
        s_samp_f = sem("s_samp_f")
        s_samp_bc = sem("s_samp_bc")
        s_chain = sem("s_chain")
        s_setup_done = sem("s_setup_done")
        s_level1 = sem("s_level1")
        s_found = [sem(f"s_found{i}") for i in range(2)]
        s_found_f = [sem(f"s_found_f{i}") for i in range(2)]
        s_found_used = [sem(f"s_found_used{i}") for i in range(2)]
        s_search = sem("s_search")
        s_first = sem("s_first")
        s_shift = sem("s_shift")
        s_shifted = sem("s_shifted")
        s_sqrt = sem("s_sqrt")

        e_idx = [sem(f"edge_idx{i}") for i in range(2)]
        e_scanned = [sem(f"edge_scanned{i}") for i in range(2)]
        e_stored = [sem(f"edge_stored{i}") for i in range(2)]
        e_free = [sem(f"edge_free{i}") for i in range(2)]
        e_mask = sem("edge_mask")
        e_carry = sem("edge_carry_saved")
        e_all_stored = sem("edge_all_stored")
        e_table = sem("edge_table_stored")
        node_var = sem("node_var")
        node_std = sem("node_std")

        class Seam:
            def __init__(self, name):
                self.t = sem(f"{name}_seam_transposed")
                self.scan = sem(f"{name}_seam_scanned")
                self.back = sem(f"{name}_seam_back")
                self.row = sem(f"{name}_seam_row")
                self.sum = sem(f"{name}_seam_sum")
                self.put = sem(f"{name}_seam_put")

        edge_seam = Seam("edge")

        gathered = [[sem(f"edge_gathered{j}{i}") for i in range(2)] for j in range(2)]

        class EdgePass:
            def __init__(self, i, name, table, scan, maximum, rows):
                self.i, self.table, self.scan, self.maximum, self.rows = i, table, scan, maximum, rows
                self.v = [i * ((NB + 1) // 2), i * (NB // 2)]
                self.gathered = gathered[i // 2]
                self.g0 = [v * T * 16 for v in ((NB + 1) // 2, NB // 2)] if i % 2 else [0, 0]
                self.mask0 = NB * (i + 1) if i else 0
                self.carry0 = i * (NB + 1) + 1

        node_rows = sem("node_rows")
        node_z = sem("node_z")
        node_zt = sem("node_z_transposed")
        node_ztc = sem("node_zt_copied")
        node_chain = sem("node_chain")
        node_mm = sem("node_product")
        got_sems = {k: [sem(f"{k}_got{i}") for i in range(2)] for k in ("n0", "layer", "n4")}

        class NodeStage:
            def __init__(self, chain0, norm0, rows0, z0, mm0, got, got0):
                self.norm0, self.rows0, self.z0, self.mm0 = norm0 * NC, rows0 * NC, z0 * NC, mm0 * NC
                self.chain0 = chain0 * NC
                self.got = got_sems[got]
                self.got0 = [got0 * ((NC + 1) // 2), got0 * (NC // 2)]

        p0 = EdgePass(0, "max", x, scan_max, True, rows0)
        p1 = EdgePass(1, "sum1", tab_x1, scan_x1, False, rows12)
        p2 = EdgePass(2, "sum2", tab_t2, scan_t2, False, rows12)
        p3 = EdgePass(3, "sum3", tab_t3, scan_t3, False, rows12)
        n0 = NodeStage(0, 0, 0, 0, 0, "n0", 0)
        n1 = NodeStage(10, 1, 1, 0, 0, "layer", 0)
        n2 = NodeStage(23, 2, 2, 0, 0, "layer", 1)
        n3 = NodeStage(27, 2, 3, 1, 1, "layer", 2)
        n4 = NodeStage(40, 3, 4, 3, 2, "n4", 0)
        ea_seam, a_seam = Seam("ea"), Seam("att")
        ea_loaded = sem("ea_loaded")
        ea_scanned = sem("ea_scanned")
        ea_stored = sem("ea_stored")
        ea_carry = sem("ea_carry")
        mlp_in = sem("mlp_in")
        mlp_T = sem("mlp_T")
        mlp_Tc = sem("mlp_Tc")
        mlp_z = sem("mlp_z")
        mlp_a = sem("mlp_a")
        mlp_b = sem("mlp_b")
        mlp_bc = sem("mlp_bc")
        s_zero_edge = sem("s_zero_edge")
        ea_got = [sem(f"ea_got{i}") for i in range(2)]
        s_win = sem("s_win")
        s_win_idx = sem("s_win_idx")
        s_flag_in = sem("s_flag_in")
        s_flag_T = sem("s_flag_T")
        s_flag = sem("s_flag")
        b_pair = sem("b_pair")
        b_turned = sem("b_turned")
        b_keys = sem("b_keys")
        b_hot = sem("b_hot")
        b_count = sem("b_count")
        b_out = sem("b_out")
        b_stored = [sem(f"b_stored{i}") for i in range(2)]
        m_split = sem("m_split")
        m_used = sem("m_used")
        m_loaded = [sem(f"m_loaded{i}") for i in range(MS)]
        m_copied = sem("m_copied")
        m_folded = sem("m_folded")
        m_got = sem("m_got")
        x_loaded = sem("x_loaded")
        x_pad = sem("x_pad")
        x3_loaded = sem("x3_loaded")
        x3_stored = sem("x3_stored")
        qkv_mm = sem("qkv_mm")
        qkv_copied = sem("qkv_copied")
        q_tab = sem("q_tab")
        q_scat = sem("q_scat")
        q_free = sem("q_free")
        q_first = sem("q_first")
        q_first_put = sem("q_first_put")
        a_idx = [sem(f"a_idx{i}") for i in range(2)]
        a_kv = [sem(f"a_kv{i}") for i in range(NS)]
        a_free = [sem(f"a_free{i}") for i in range(NS)]
        a_init = sem("a_init")
        a_slot = sem("a_slot")
        ea_back_read = sem("ea_back_read")
        a_q = sem("a_q")
        a_chain = sem("a_chain")
        a_q_used = sem("a_q_used")
        a_arg = sem("a_arg")
        a_exp = sem("a_exp")
        a_scan = sem("a_scan")
        a_stored = sem("a_stored")
        a_all_stored = sem("a_all_stored")
        a_tail = sem("a_tail")
        a_dexp = sem("a_dexp")
        a_dexped = sem("a_dexped")
        out_rows = sem("out_rows")
        m_chain = sem("m_chain")
        slow_chain = sem("slow_chain")
        b_chain = sem("b_chain")
        s_slow = sem("s_slow")
        begun = sem("begun")

        src_v = src.rearrange("(p t) -> p t", p=P)
        dst_v = dst.rearrange("(p t) -> p t", p=P)
        dst_rows = dst.rearrange("(r c) -> r c", c=DB)
        ea64_v = ea64.rearrange("(p t) f -> p (t f)", p=P)
        ea32_v = ea32.rearrange("(p t) f -> p (t f)", p=P)
        q_edge_v = q_edge[0:E, :].rearrange("(p t) f -> p (t f)", p=P)

        def scan_v(s):
            return s.rearrange("(p t) f -> p (t f)", p=P)

        def tiles(t):
            return t.rearrange("(t p) f -> p t f", p=P)

        def flat(v):
            return v.rearrange("p a b -> p (a b)")

        def over(v, n):
            a = v.shape[1]
            return v.rearrange("p (a o) -> p a o", o=1).to_broadcast([v.shape[0], a, n])

        def chunk(v, c):
            return v[:, bass.ds(c * CT, CT), :]

        n_weights = 2 * 6 + G4 * 3 + 4 + 3

        block = ctx.enter_context(nc.Block())

        @block.sync
        def _(sp):
            sp.dma_start(dst_i, dst_v).then_inc(s_dst, 16)
            sp.dma_start(samp_i[0:1, :], dst.rearrange("(o r c) -> o r c", o=1, c=DB)[:, :, 0],
                         allow_slow_non_contiguous=True).then_inc(s_samp, 16)
            sp.wait_ge(s_zeroed, 1)
            nw = 0
            for h in range(2):
                d = slice(h * F, (h + 1) * F)
                for w, o in ((W1, w1_bd), (W2, w2_bd), (WO, wo_bd)):
                    sp.dma_start(o[d, d], w).then_inc(s_wt, 16)
                for i, w in enumerate((WQ, WK, WV)):
                    a = h * 3 * F + i * F
                    sp.dma_start(wqkv_bd[d, a:a + F], w).then_inc(s_wt, 16)
                nw += 6
            for i in range(G4):
                d = slice(i * D32, (i + 1) * D32)
                sp.dma_start(we1_bd[d, d], We1).then_inc(s_wt, 16)
                sp.dma_start(we2_bd[d, i * H:(i + 1) * H], We2).then_inc(s_wt, 16)
                sp.dma_start(be1_col[d, :], be1.rearrange("(p o) -> p o", o=1)).then_inc(s_wt, 16)
                nw += 3
            for b, o in ((be2, be2_row[:, :]), (b1, b1_row[:, :]), (b2, b2_row[:, :]), (bO, bo_row[:, :]),
                         (bQ, bqkv_row[:, 0:F]), (bK, bqkv_row[:, F:2 * F]), (bV, bqkv_row[:, 2 * F:3 * F])):
                sp.dma_start(o, b.rearrange("(o n) -> o n", o=1)).then_inc(s_wt, 16)
                nw += 1
            assert nw == n_weights

            def edge_pass(p, layer0=False):
                for k in range(2):
                    sp.dma_start(idx_st[:, k, :], src_v[:, k * T:(k + 1) * T]).then_inc(e_idx[k], 16)
                    sp.sem_inc(e_free[k], 1)
                if layer0:
                    sp.wait_ge(s_setup_done, 1)
                    sp.dma_start(flat(eat), ea64_v[:, 0:T * F]).then_inc(ea_loaded, 16)

                def step(k, b, n, more=2):
                    sp.wait_ge(p.gathered[b], (n + 1) * (16 * T) + p.g0[b])
                    if more > 1:
                        sp.dma_start(idx_st[:, b, :], src_v[:, bass.ds((k + 2) * T, T)]).then_inc(e_idx[b], 16)
                    if layer0:
                        sp.wait_ge(ea_scanned, k + 1)
                        sp.dma_start(scan_v(scan_ea)[:, bass.ds(k * (T * F), T * F)], flat(eat)).then_inc(ea_stored, 16)
                        sp.dma_start(q_edge_v[:, bass.ds(k * (T * F), T * F)].rearrange("p (a b) -> p a b", a=5),
                                     zeros_z.rearrange("p (o b) -> p o b", o=1).to_broadcast([P, 5, T * F // 5])).then_inc(s_zero_edge, 16)
                        if more > 0:
                            sp.wait_ge(ea_stored, (k + 1) * 16)
                            sp.wait_ge(ea_carry, k + 2)
                            sp.dma_start(flat(eat), ea64_v[:, bass.ds((k + 1) * (T * F), T * F)]).then_inc(ea_loaded, 16)
                    sp.wait_ge(e_scanned[b], n + (p.v[b] + 1))
                    sp.dma_start(scan_v(p.scan)[:, bass.ds(k * (T * F), T * F)], flat(p.rows[:, b])).then_inc(e_stored[b], 16)
                    sp.wait_ge(e_stored[b], (n + (p.v[b] + 1)) * 16)
                    sp.sem_inc(e_free[b], 1)
                with sp.Fori(0, NB // 2 - 1) as g:
                    step(2 * g, 0, g)
                    step(2 * g + 1, 1, g)
                step(NB - 3, 0, NB // 2 - 1)
                step(NB - 2, 1, NB // 2 - 1, more=1)
                step(NB - 1, 0, NB // 2, more=0)
                if layer0:
                    sp.wait_ge(s_zero_edge, 16 * NB)
                    sp.wait_ge(ea_stored, 16 * NB)
                sp.wait_ge(e_carry, p.carry0 + 1 + NB)
                sp.sem_inc(e_all_stored, 1)

            def product_loads(layer, late):
                def group(c, q):
                    nb = QB[q]
                    for k in range(GC):
                        i = (q * GC + k) % MS
                        h, g = divmod(k, GC // 2)
                        sp.wait_ge(m_used, c * (NQ * GC) + (layer * NC * NQ * GC + q * GC + k + 1))
                        sp.dma_start(adj_i[:, i, 0:nb, :],
                                     adj[h][bass.ds(c * CT + q * GB, nb), :, g * GH:(g + 1) * GH, :]
                                     .rearrange("b p h d -> p b (h d)")).then_inc(m_loaded[i], 16)
                in_turn(sp, NC, NQ, group, nothing, nothing, late, NQ - 2)

            def layer(i, p, store, late):
                with sp.If(fast == 1):
                    product_loads(i, late)
                with sp.Else():
                    edge_pass(p)
                    chunks(sp, NC, store)

            def store_rows(s, table, rows):
                def step(c):
                    sp.wait_ge(node_rows, c + (s.rows0 + 1))
                    sp.dma_start(chunk(tiles(table), c), chunk(rows, c)).then_inc(e_table, 16)
                return step

            edge_pass(p0, layer0=True)
            sp.wait_ge(s_flag, 1)
            fast = sp.value_load(flag[0:1, 0:1], min_val=0, max_val=1)
            sp.wait_ge(x_pad, 1)
            sp.dma_start(xcur[:, 0:NT - 1, :], x[0:(NT - 1) * P, :].rearrange("(t p) f -> p t f", p=P)).then_inc(x_loaded, 16)
            sp.dma_start(xcur[0:LAST, NT - 1, :], x[(NT - 1) * P:N, :]).then_inc(x_loaded, 16)
            chunks(sp, NC, store_rows(n0, tab_x1, xcur))
            layer(0, p1, store_rows(n1, tab_t2, tcur), nothing)
            layer(1, p2, store_rows(n2, tab_t3, tcur), nothing)

            def store_x3(c):
                sp.wait_ge(node_rows, c + (n3.rows0 + 1))
                sp.dma_start(chunk(tiles(tab_x3), c), chunk(xcur, c)).then_inc(x3_stored, 16)
            layer(2, p3, store_x3, store_x3)
            sp.wait_ge(x3_stored, 16 * NC)
            sp.wait_ge(q_scat, 16 * NT)
            sp.wait_ge(q_first, 16)
            sp.dma_start(q_edge[0:E, :].rearrange("(p t) f -> p t f", p=P)[:, 0, :], seam_row[:, 0:F]).then_inc(q_first_put, 16)
            sp.wait_ge(q_first_put, 16)

            sp.wait_ge(q_tab, 2 * 16 * (NC + 1))
            sp.sem_inc(a_slot, 1)
            for k in range(2):
                sp.dma_start(idx_st[:, k, :], src_v[:, k * T:(k + 1) * T]).then_inc(a_idx[k], 16)
            sp.dma_start(flat(qf), q_edge_v[:, 0:T * F]).then_inc(a_q, 16)
            sp.dma_start(ea_in, ea32_v[:, 0:T * D32]).then_inc(mlp_in, 16)

            def att(k, b, n, more=2):
                if more > 0:
                    sp.wait_ge(mlp_bc, (k + 1) * NG)
                    sp.dma_start(ea_in, ea32_v[:, bass.ds((k + 1) * (T * D32), T * D32)]).then_inc(mlp_in, 16)
                if more > 1:
                    for u in range(NS):
                        sp.wait_ge(a_kv[u], (k + 1) * (16 * TS))
                    sp.dma_start(idx_st[:, b, :], src_v[:, bass.ds((k + 2) * T, T)]).then_inc(a_idx[b], 16)
                sp.wait_ge(a_q_used, k + 1)
                if more > 0:
                    sp.dma_start(flat(qf), q_edge_v[:, bass.ds((k + 1) * (T * F), T * F)]).then_inc(a_q, 16)
                sp.wait_ge(a_scan, k + 1)
                sp.dma_start(scan_v(scan_att)[:, bass.ds(k * (T * W3), T * W3)], flat(acc[:, 1:T + 1, :])).then_inc(a_stored, 16)
                sp.wait_ge(a_stored, (k + 1) * 16)
                sp.sem_inc(a_slot, 1)
            with sp.Fori(0, NB // 2 - 1) as g:
                att(2 * g, 0, g)
                att(2 * g + 1, 1, g)
            att(NB - 3, 0, NB // 2 - 1)
            att(NB - 2, 1, NB // 2 - 1, more=1)
            att(NB - 1, 0, NB // 2, more=0)
            sp.wait_ge(a_stored, 16 * NB)
            sp.sem_inc(a_all_stored, 1)
            sp.wait_ge(a_seam.put, 16)
            sp.dma_start(xcur, tiles(tab_x3)).then_inc(x3_loaded, 16)

            with sp.Fori(0, NC - 1) as c:
                sp.wait_ge(node_rows, c + (n4.rows0 + 1))
                sp.dma_start(out[bass.ds(c * (CT * P), CT * P), :].rearrange("(t p) f -> p t f", p=P), chunk(xcur, c)).then_inc(out_rows, 16)
            sp.wait_ge(node_rows, n4.rows0 + NC)
            a = (NC - 1) * CT
            sp.dma_start(out[a * P:(NT - 1) * P, :].rearrange("(t p) f -> p t f", p=P), xcur[:, a:NT - 1, :]).then_inc(out_rows, 16)
            sp.dma_start(out[(NT - 1) * P:N, :], xcur[0:LAST, NT - 1, :]).then_inc(out_rows, 16)
            sp.wait_ge(out_rows, 16 * (NC + 1))

        @block.gpsimd
        def _(pool):
            def gather(dst_ap, table, idx):
                return pool.indirect_dma_start(dst_ap, None, table, bass.IndirectOffsetOnAxis(ap=idx, axis=0))

            def scatter(table, idx, src_ap):
                return pool.indirect_dma_start(table, bass.IndirectOffsetOnAxis(ap=idx, axis=0), src_ap, None)

            pool.memset(ident[:, :], 0.0).then_inc(s_ident, 1)
            pool.iota(node_id[:, :], [[P, NT]], base=0, channel_multiplier=1, allow_small_or_imprecise_dtypes=True).then_inc(s_iota, 1)
            pool.iota(small[:, 0:1], [[0, 1]], base=0, channel_multiplier=1, allow_small_or_imprecise_dtypes=True).then_inc(s_iota, 1)
            pool.iota(lane[:, :], [[1, P]], base=0, channel_multiplier=0, allow_small_or_imprecise_dtypes=True).then_inc(s_iota, 1)
            pool.wait_ge(s_ident, 1)
            pool.affine_select(out=ident[:, :], in_=ident[:, :], compare_op=ALU.not_equal, fill=1.0, base=0,
                               pattern=[[-1, P]], channel_multiplier=1).then_inc(s_ident, 1)
            def edge_block(p, k, b, n):
                pool.wait_ge(e_idx[b], (n + (p.v[b] + 1)) * 16)
                pool.wait_ge(e_free[b], n + (p.v[b] + p.i + 1))
                pool.wait_ge(e_carry, k + p.carry0)
                pool.sem_inc(begun, 1)
                for t in range(T):
                    gather(p.rows[:, b, t, :], p.table, idx_st[:, b, t:t + 1]).then_inc(p.gathered[b], 16)

            def edge_pass(p):
                ring(pool, NB, lambda k, b, n: edge_block(p, k, b, n))

            def seam_fix(scan, sm, i=1, width=F):
                gather(seam_row[:, 0:W3 if width == A3 else F], scan, seam_idx[:, :]).then_inc(sm.row, 16)
                pool.wait_ge(sm.sum, i)
                scatter(scan, seam_idx[:, :], seam_row[:, 0:W3 if width == A3 else F]).then_inc(sm.put, 16)
                pool.wait_ge(sm.put, 16 * i)

            def fetch_nodes(sems, visits, pieces):
                per = 16 * CT * len(pieces)
                for c in range(NC):
                    if c >= 2:
                        pool.wait_ge(sems[c % 2], per * (c // 2 + visits[c % 2]))
                    for t in range(c * CT, (c + 1) * CT):
                        for rows, scan in pieces:
                            gather(rows[:, t, :], scan, end_idx[:, t:t + 1]).then_inc(sems[c % 2], 16)

            edge_block(p0, 0, 0, 0)
            pool.wait_ge(s_level1, 1)
            for c in range(NT // SC):
                if c >= 2:
                    pool.wait_ge(s_found_f[c % 2], c // 2)
                for i in range(SC):
                    t = c * SC + i
                    gather(found[:, c % 2, i, :], dst_rows, blk_idx[:, t:t + 1]).then_inc(s_found[c % 2], 16)
            pool.wait_ge(s_win_idx, 1)
            src_1 = src.rearrange("(e o) -> e o", o=1)
            for t in range(NT):
                gather(win[:, t, :], src_1, win_idx[:, t:t + 1]).then_inc(s_win, 16)
            with pool.Fori(0, NB // 2) as g:
                edge_block(p0, 2 * g + 1, 1, g)
                edge_block(p0, 2 * g + 2, 0, g + 1)
            pool.wait_ge(e_all_stored, 1)
            seam_fix(scan_max, edge_seam, 1)
            seam_fix(scan_ea, ea_seam)
            for b in range(2):
                pool.wait_ge(b_stored[b], 32 * (NT // 2 + 1))
            fetch_nodes(n0.got, n0.got0, [(got64, scan_max)])
            pool.wait_ge(s_flag, 1)
            fast = pool.value_load(flag[0:1, 0:1], min_val=0, max_val=1)

            def layer(s, p, scan):
                with pool.If(fast == 0):
                    pool.wait_ge(e_table, p.i * 16 * NC)
                    edge_pass(p)
                    pool.wait_ge(e_all_stored, p.i + 1)
                    seam_fix(scan, edge_seam, p.i + 1)
                    fetch_nodes(s.got, s.got0, [(got64, scan)])

            fetch_nodes(ea_got, [0, 0], [(got_ea, scan_ea)])
            layer(n1, p1, scan_x1)
            layer(n2, p2, scan_t2)
            layer(n3, p3, scan_t3)
            pool.wait_ge(s_zero_edge, 16 * NB)
            pool.sem_inc(q_free, 1)
            for c in range(NC):
                pool.wait_ge(qkv_copied, HT * (c + 1))
                for t in range(CT):
                    scatter(q_edge, q_idx[:, c * CT + t:c * CT + t + 1], q_o[:, t, :]).then_inc(q_scat, 16)
                pool.wait_ge(q_scat, 16 * CT * (c + 1))
                pool.sem_inc(q_free, 1)
            pool.wait_ge(q_tab, 2 * 16 * (NC + 1))
            gather(seam_row[:, 0:F], tab_q, first_idx[:, :]).then_inc(q_first, 16)
            pool.wait_ge(q_scat, 16 * NT)
            pool.wait_ge(x3_stored, 16 * NC)

            def att(k, b, n):
                pool.wait_ge(a_idx[b], (n + 1) * 16)
                for u in range(NS):
                    pool.wait_ge(a_free[u], k + 1)
                    pool.sem_inc(begun, 1)
                    for t in range(TS):
                        i = u * TS + t
                        gather(kv[:, u, t, :], tab_kv, idx_st[:, b, i:i + 1]).then_inc(a_kv[u], 16)
            ring(pool, NB, att)
            pool.wait_ge(a_all_stored, 1)
            seam_fix(scan_att, a_seam, 1, A3)
            fetch_nodes(n4.got, n4.got0, [(got, scan_att)])

        @block.scalar
        def _(act):
            for i, w in enumerate((w1_bd, w2_bd)):
                act.wait_ge(s_wt_T, i + 1)
                act.activation(w[:, :], bank[i][:, 0:P], ACT.Copy).then_inc(s_wt_cp, 1)
            act.wait_ge(s_samp, 16)
            act.activation(samp_f[0:1, :], samp_i[0:1, :], ACT.Copy).then_inc(s_samp_f, 1)
            act.wait_ge(s_samp_bc, 1)
            act.activation(samp_bc[:, 0:512], bank[2][:, :], ACT.Copy).then_inc(s_samp_f, 1)
            act.activation(samp_bc[:, 512:NR], bank[3][:, 0:NR - 512], ACT.Copy).then_inc(s_samp_f, 1)

            def mlp(k, b, groups):
                for q in groups:
                    act.wait_ge(mlp_T, k * NG + (q + 1))
                    act.activation(ea_T, bank[0], ACT.Copy).then_inc(mlp_Tc, 1)
                    act.wait_ge(mlp_z, k * NG + (q + 1))
                    act.activation(mlp_h, bank[1], ACT.Silu, bias=be1_col[:, :]).then_inc(mlp_a, 1)
                    t0 = min(q * MG, T - MG)
                    act.wait_ge(mlp_b, k * NG + (q + 1))
                    act.activation(flat(bias_i[:, b, t0:t0 + MG, :]), bank[2][:, 0:MG * H], ACT.Copy).then_inc(mlp_bc, 1)

            def conv(c, b, n):
                act.wait_ge(s_found[b], (n + 1) * (16 * SC))
                act.wait_ge(s_found_used[b], n + 1)
                act.activation(flat(found_f[:, b]), flat(found[:, b]), ACT.Copy).then_inc(s_found_f[b], 1)
            ring(act, NT // SC, conv)
            act.wait_ge(s_sqrt, 1)
            act.activation(dis[:, :], deg1[:, :], ACT.Sqrt).then_inc(s_sqrt, 1)

            def pair(j):
                act.wait_ge(b_turned, j + 1)
                act.activation(keys, psum[:, 6, 0:2 * P].rearrange("p (a b) -> p a b", a=2), ACT.Copy).then_inc(b_keys, 1)
                for h in range(2):
                    act.wait_ge(b_stored[h], j * 32 + 32)
                    act.sem_inc(begun, 1)
                    with act.Fori(0, NBH // 2) as q:
                        for i in range(2):
                            m = j * (2 * NBH) + (2 * q + (h * NBH + i))
                            act.wait_ge(b_count, m + 3)
                            o = adj_o[:, h, :, :].rearrange("p h (a w) -> p a h w", a=2)
                            act.activation(o[:, :, :, bass.ds((2 * q + i) * WB, WB)],
                                           psum[:, 2 * i:2 * i + 2, 0:WB * NT].rearrange("p a (w h) -> p a h w", w=WB),
                                           ACT.Copy).then_inc(b_out, 1)
                    act.wait_ge(b_out, j * (2 * NBH) + ((h + 1) * NBH + 2))
                    for i, a in enumerate(adj):
                        act.dma_start(a[bass.ds(2 * j + h, 1), :, :, :].rearrange("b p h d -> p (b h d)"),
                                      flat(adj_o[:, h, i * (NT // 2):(i + 1) * (NT // 2), :])).then_inc(b_stored[h], 16)
            act.sem_inc(b_out, 2)
            for h in range(2):
                act.sem_inc(b_stored[h], 32)
            chunks(act, NT // 2, pair)
            act.wait_ge(s_flag, 1)
            fast = act.value_load(flag[0:1, 0:1], min_val=0, max_val=1)

            def copy_sums(layer):
                def group(c, q):
                    act.wait_ge(m_used, c * (NQ * GC) + (MS + (layer * NC * NQ + q + 1) * GC))
                    for k, v in zip(sums[q % 2], (sum_a, sum_b)):
                        for j in range(QB[q] // 2):
                            w = slice(j * 2 * P, (j + 1) * 2 * P)
                            i = act.activation(v[:, w].rearrange("p (a h w) -> p h a w", a=2, h=2),
                                               k[:, w].rearrange("p (h a w) -> p h a w", a=2, h=2), ACT.Copy)
                    i.then_inc(m_copied, 1)
                return group

            def std(s, c):
                act.wait_ge(node_var, c + (s.norm0 + 1))
                act.activation(st[:, 2, :], st[:, 1, :], ACT.Sqrt).then_inc(node_std, 1)

            def copies(s, z):
                act.wait_ge(node_zt, z + s.z0)
                j = 0
                for k, a, n in turned:
                    i = act.activation(zT[:, j * P:(j + n) * P], bank[k][:, a:a + n * P], ACT.Copy)
                    j += n
                i.then_inc(node_ztc, 1)

            def stage3_mid(c):
                copies(n3, 2 * c + 1)
                std(n3, c)

            def stage3_late(c):
                copies(n3, 2 * c + 2)
                act.wait_ge(q_tab, c * 32 + 32)
                act.wait_ge(q_free, c + 1)
                for j in range(HT):
                    act.wait_ge(qkv_mm, c * HT + (j + 1))
                    v = bank[5 + j % 3][:, 0:6 * F].rearrange("p (a b) -> p a b", a=2)
                    act.activation(kv_o[:, 2 * j:2 * j + 2, :], v[:, :, F:3 * F], ACT.Copy)
                    act.activation(q_o[:, 2 * j:2 * j + 2, :], v[:, :, 0:F], ACT.Copy,
                                   scale=float(DK) ** -0.5).then_inc(qkv_copied, 1)
                act.wait_ge(qkv_copied, c * HT + HT)
                act.dma_start(chunk(tiles(tab_kv), c), kv_o).then_inc(q_tab, 16)
                act.dma_start(chunk(tiles(tab_q), c), q_o).then_inc(q_tab, 16)

            def layer(i, start, mid=nothing, late=nothing):
                with act.If(fast == 1):
                    in_turn(act, NC, NQ, copy_sums(i), start, mid, late)
                with act.Else():
                    chunks(act, NC, lambda c: (start(c), mid(c), late(c)))

            chunks(act, NC, lambda c: std(n0, c))
            act.sem_inc(q_tab, 32)
            layer(0, lambda c: std(n1, c))
            layer(1, nothing, lambda c: copies(n2, c + 1))
            layer(2, nothing, stage3_mid, stage3_late)

            def att(k, after=None, b=0):
                for u in range(NS):
                    act.wait_ge(a_arg, k * NS + (u + 1))
                    act.activation(acc[:, 1 + u * TS:1 + (u + 1) * TS, F:A3], arg[:, 0], ACT.Exp)
                    act.activation(keepf[:, u * TS:(u + 1) * TS, :], arg[:, 1], ACT.Exp).then_inc(a_exp, 1)
                    if after is not None:
                        mlp(after, b, range(u * NG // (NS - 1), min((u + 1) * NG // (NS - 1), NG)))
            mlp(0, 0, range(NG))
            with act.Fori(0, NB // 2) as g:
                att(2 * g, 2 * g + 1, 1)
                att(2 * g + 1, 2 * g + 2, 0)
            att(NB - 1)
            act.wait_ge(a_dexp, 1)
            act.activation(seam_m[0:A3, 3:5, :], seam_m[0:A3, 3:5, :], ACT.Exp).then_inc(a_dexped, 1)
            act.wait_ge(a_dexp, 2)
            act.activation(seam_m[:, 6:8, 0:A3], seam_m[:, 6:8, 0:A3], ACT.Exp).then_inc(a_dexped, 1)

            def stage4(c):
                copies(n4, c + 1)
                std(n4, c)
            chunks(act, NC, stage4)

        @block.tensor
        def _(pe):
            pe.wait_ge(s_ident, 2)
            pe.wait_ge(s_wt, 16 * n_weights)
            for i, w in enumerate((w1_bd, w2_bd)):
                pe.transpose(bank[i][:, 0:P], w[:, :], ident[:, :]).then_inc(s_wt_T, 1)
            pe.wait_ge(s_samp_f, 1)
            pe.wait_ge(s_zeroed, 1)
            pe.matmul(bank[2][:, :], ones_row[:, :], samp_f[0:1, 0:512], start=True, stop=True)
            pe.matmul(bank[3][:, 0:NR - 512], ones_row[:, :], samp_f[0:1, 512:NR], start=True, stop=True).then_inc(s_samp_bc, 1)
            pe.wait_ge(s_ends, 1)
            for i in range(2):
                pe.matmul(bank[6 + i][:, 0:P], ends_bc[:, i, :], ident[:, :], start=True, stop=True).then_inc(s_ends_bc, 1)

            def mlp(k, b, n):
                for q in range(NG):
                    g = k * NG + q
                    t0 = min(q * MG, T - MG)
                    if q == 0:
                        pe.wait_ge(mlp_in, (k + 1) * 16)
                    for j in range(JB):
                        i = pe.transpose(bank[0][:, j * P:(j + 1) * P],
                                         ea_in[:, t0 * D32 + j * P:t0 * D32 + (j + 1) * P], ident[:, :])
                    i.then_inc(mlp_T, 1)
                    pe.wait_ge(mlp_Tc, g + 1)
                    pe.matmul(bank[1], we1_bd[:, :], ea_T, start=True, stop=True).then_inc(mlp_z, 1)
                    pe.wait_ge(mlp_a, g + 1)
                    pe.matmul(bank[2][:, 0:MG * H].rearrange("p (a b) -> p a b", a=MG), ones_row[:, :],
                              be2_row[:, :].rearrange("p (o b) -> p o b", o=1).to_broadcast([1, MG, H]), start=True, stop=False)
                    for j in range(JB):
                        i = pe.matmul(bank[2][:, j * G4 * H:(j + 1) * G4 * H], mlp_h[:, j * P:(j + 1) * P], we2_bd[:, :],
                                      start=False, stop=j == JB - 1)
                    i.then_inc(mlp_b, 1)
                    pe.wait_ge(mlp_bc, g + 1)
            pe.wait_ge(s_wt_cp, 2)
            pe.wait_ge(s_samp_f, 3)
            pe.wait_ge(s_first, 1)
            pe.wait_ge(s_shift, 2)
            pe.matmul(bank[3][:, 0:NT], shift1, row_first[:, 0:NT], start=True, stop=False)
            pe.matmul(bank[3][:, 0:NT], shift2, row_first[:, 1:NT + 1], start=False, stop=True).then_inc(s_shifted, 1)
            pe.wait_ge(s_flag_in, 1)
            pe.transpose(bank[5][0:1, 0:P], small[:, 4:5], ident[:, :]).then_inc(s_flag_T, 1)

            def pair(j):
                pe.wait_ge(b_pair, j + 1)
                for i in range(2):
                    t = pe.transpose(bank[6][:, i * P:(i + 1) * P], pair_f[:, i, :], ident[:, :])
                t.then_inc(b_turned, 1)
                with pe.Fori(0, NBH) as q:
                    for i in range(2):
                        m = j * (2 * NBH) + (2 * q + i)
                        pe.wait_ge(b_hot, m + 1)
                        pe.wait_ge(b_out, m + 1)
                        for w in range(WB):
                            for a in range(2):
                                r = slice(W * a, W * (a + 1))
                                t = pe.matmul(psum[:, 2 * i + a, w * NT:(w + 1) * NT], hot_lo[r, i, w, :], hot_hi[r, i, w, 0:NT],
                                              start=True, stop=True)
                        t.then_inc(b_count, 1)
            pe.sem_inc(b_count, 2)
            chunks(pe, NT // 2, pair)

            def seam_turn(sm, i, tails, ready, extra=1, width=F):
                pe.wait_ge(ready, i * (NB + 1) + extra)
                pe.transpose(bank[6][0:width, 0:P], tails, ident[:, :]).then_inc(sm.t, 1)
                pe.wait_ge(sm.scan, i)
                pe.transpose(bank[7][:, 0:width], seam[0:width, 1, :], ident[0:width, 0:width]).then_inc(sm.back, 1)

            seam_turn(ea_seam, 1, carry_ea[:, :], ea_carry, 0)
            pe.wait_ge(ea_back_read, 1)
            seam_turn(edge_seam, 1, carry[:, :], e_carry)
            pe.wait_ge(s_flag, 1)
            fast = pe.value_load(flag[0:1, 0:1], min_val=0, max_val=1)

            def products(layer):
                g0 = layer * NC * NQ

                def fold_sums(c, q):
                    pe.wait_ge(m_copied, c * NQ + (g0 + q + 1))
                    pe.wait_ge(m_got, c * NQ + (g0 + q + 1))
                    for k in range(QB[q]):
                        for n, v in enumerate((sum_a, sum_b)):
                            i = pe.matmul(bank[2][:, k * F:(k + 1) * F], v[:, k * P:(k + 1) * P], fold[:, :],
                                          start=n == 0, stop=n == 1)
                    i.then_inc(m_folded, 1)

                def group(c, q):
                    nb = QB[q]
                    top, low = sums[q % 2][0][:, 0:nb * P], sums[q % 2][1][:, 0:nb * P]

                    def cols(t):
                        k, i = divmod(t, GH)
                        return adj_i[:, (q * GC + k) % MS, 0:nb, i * P:(i + 1) * P]

                    for t in range(NT):
                        if t % CT == 0 and q == 0:
                            pe.wait_ge(m_split, layer * NC + t // CT + 1)
                        if t % GH == 0:
                            slot, v = (q * GC + t // GH) % MS, (q * GC + t // GH) // MS + 1
                            per = NQ * GC // MS
                            pe.wait_ge(m_loaded[slot], c * (16 * per) + 16 * (layer * NC * per + v))
                        pe.matmul(top.rearrange("p (a b) -> p a b", a=nb), parts[:, t, 0:2 * F], cols(t),
                                  start=t == 0, stop=t == NT - 1)
                        if t % 2:
                            for a in range(2):
                                i = pe.matmul(low[F * a:F * (a + 1), :].rearrange("p (a b) -> p a b", a=nb),
                                              parts[:, t - 1 + a, 2 * F:3 * F], cols(t - 1 + a),
                                              start=t == 1, stop=t == NT - 1, tile_position=(0, F * a))
                            n = (t + 1) // GH - (t - 1) // GH
                            if n:
                                i.then_inc(m_used, 1)
                        if t == CT - 1:
                            if q:
                                fold_sums(c, q - 1)
                            elif not isinstance(c, int):
                                fold_sums(c - 1, NQ - 1)
                return group, lambda: fold_sums(NC - 1, NQ - 1)

            def layer(i, mid=nothing, late=nothing):
                with pe.If(fast == 1):
                    if i == 0:
                        pe.sem_inc(m_used, MS)
                    group, last = products(i)
                    in_turn(pe, NC, NQ, group, nothing, mid, late, finish=last)
                with pe.Else():
                    seam_turn(edge_seam, i + 2, carry[:, :], e_carry)
                    chunks(pe, NC, lambda c: (mid(c), late(c)))

            def product(s, z, w, brow):
                pe.wait_ge(node_ztc, z + s.z0)
                for h, (a, b) in enumerate(((0, 4), (4, HT))):
                    n = 2 * (b - a)
                    pe.matmul(bank[5 + h][:, 0:n * F].rearrange("p (a b) -> p a b", a=n), ones_row[:, :],
                              brow[:, :].rearrange("p (o b) -> p o b", o=1).to_broadcast([1, n, F]), start=True, stop=False)
                    for j in range(a, b):
                        i = pe.matmul(bank[5 + h][:, (j - a) * P:(j - a + 1) * P], zT[:, j * P:(j + 1) * P], w[:, :],
                                      start=False, stop=j == b - 1)
                i.then_inc(node_mm, 1)

            def turn(s, z, v):
                pe.wait_ge(node_z, z + s.z0)
                for j, (k, a) in enumerate((k, a + i * P) for k, a, n in turned for i in range(n)):
                    i = pe.transpose(bank[k][:, a:a + P], v(j), ident[:, :])
                i.then_inc(node_zt, 1)

            def from_z(j):
                return flat(zc[:, 2 * j:2 * j + 2, :])

            def stage2(c):
                turn(n2, c + 1, from_z)
                product(n2, c + 1, w1_bd, b1_row)

            def stage3_mid(c):
                turn(n3, 2 * c + 1, from_z)
                product(n3, 2 * c + 1, w2_bd, b2_row)

            def stage3_late(c):
                turn(n3, 2 * c + 2, from_z)
                pe.wait_ge(node_ztc, 2 * c + (n3.z0 + 2))
                for j in range(HT):
                    if j >= 3:
                        pe.wait_ge(qkv_copied, c * HT + (j - 2))
                    pe.matmul(bank[5 + j % 3][:, 0:6 * F].rearrange("p (a b) -> p a b", a=2), ones_row[:, :],
                              bqkv_row[:, :].rearrange("p (o b) -> p o b", o=1).to_broadcast([1, 2, 3 * F]), start=True, stop=False)
                    pe.matmul(bank[5 + j % 3][:, 0:6 * F], zT[:, j * P:(j + 1) * P], wqkv_bd[:, :], start=False, stop=True)\
                      .then_inc(qkv_mm, 1)
                pe.wait_ge(qkv_copied, c * HT + HT)
                pe.sem_inc(begun, 1)

            def stage4(c):
                turn(n4, c + 1, from_z)
                product(n4, c + 1, wo_bd, bo_row)

            layer(0)
            layer(1, stage2)
            layer(2, stage3_mid, stage3_late)
            ring(pe, NB, mlp)
            pe.wait_ge(a_tail, 1)
            pe.transpose(bank[6][0:A3, 0:P], seam_m[:, 0, 0:A3], ident[:, :])
            pe.transpose(bank[5][0:A3, 0:P], seam_m[:, 1, 0:A3], ident[:, :]).then_inc(a_seam.t, 1)
            pe.wait_ge(a_seam.scan, 1)
            pe.transpose(bank[7][:, 0:A3], seam_m[0:A3, 5, :], ident[0:A3, 0:A3])
            pe.transpose(bank[4][:, 0:A3], seam_m[0:A3, 2, :], ident[0:A3, 0:A3]).then_inc(a_seam.back, 1)
            chunks(pe, NC, stage4)

        @block.vector
        def _(dve):
            ch = Chain(dve, s_chain)
            for w in (w1_bd, w2_bd, wo_bd, wqkv_bd, we1_bd, we2_bd, carry, carry_ea, carry_q):
                dve.memset(w[:, :], 0.0)
            dve.memset(blk_idx[:, :], 0)
            ch(dve.memset(ones_row[:, :], 1.0))
            dve.sem_inc(s_zeroed, 1)
            dve.sem_inc(e_carry, 2)
            dve.wait_ge(s_dst, 16)
            ch(dve.tensor_copy(dst_f, dst_i))
            ch(dve.tensor_copy(first_idx[:, :], dst_i[:, 0:1]))
            for i, c in enumerate((0, EP - 1)):
                ch(dve.tensor_copy(ends_bc[:, i, :], dst_f[:, c:c + 1].to_broadcast([P, P])))
            dve.sem_inc(s_ends, 1)
            dve.memset(inside[:, 0:1], 0.0)
            ch(dve.tensor_tensor(inside[:, 1:EP], dst_f[:, 1:EP], dst_f[:, 0:EP - 1], ALU.is_equal))
            ch(dve.tensor_scalar(junk, dst_f, dst_f[:, 0:1], 0.0, ALU.is_equal, ALU.add, accum_out=small[:, 1:2]))
            dve.wait_ge(s_iota, 3)
            ch(dve.tensor_scalar(small[:, 2:3], small[:, 0:1], float(EP), -1.0, ALU.mult, ALU.add))
            ch(dve.tensor_tensor(seam_idx[:, :], small[:, 2:3], small[:, 1:2], ALU.add))
            dve.wait_ge(s_ends_bc, 2)
            first, last = bank[6][:, 0:P], bank[7][:, 0:P]
            ch(dve.tensor_copy(ends_bc[:, 0, :], first))
            ch(dve.memset(same[:, 0:1], 0.0))
            ch(dve.tensor_tensor(same[:, 1:P], ends_bc[:, 0, 1:P], last[:, 0:P - 1], ALU.is_equal))
            ch(dve.memset(through[:, 0:1], 0.0))
            ch(dve.tensor_tensor(through[:, 1:P], ends_bc[:, 0, 0:P - 1], last[:, 0:P - 1], ALU.is_equal))
            ch(dve.tensor_tensor(through[:, :], through[:, :], same[:, :], ALU.mult))
            for a, b in ((same, same_neg), (through, through_neg)):
                ch(dve.tensor_scalar(b[:, :], a[:, :], 1.0, None, ALU.subtract))
            dve.wait_ge(s_samp_f, 3)
            with dve.Fori(0, NT) as t:
                dve.tensor_scalar(junk[:, 0:NR], samp_bc, node_id[:, bass.ds(t, 1)], 0.0, ALU.is_lt, ALU.add,
                                  accum_out=cnt[:, bass.ds(t, 1)]).then_inc(s_search, 1)
                dve.wait_ge(s_search, t + 1)
            ch(dve.tensor_scalar(blk_base[:, :], cnt[:, :], 1.0, 0.0, ALU.subtract, ALU.max))
            ch(dve.tensor_copy(blk_idx[:, :], blk_base[:, :]))
            dve.tensor_copy(lane_bf[:, :], lane[:, :])
            dve.wait_ge(s_ident, 2)
            ch(dve.tensor_tensor(fold[:, :], ident[:, 0:F], ident[:, F:P], ALU.add))
            ch(dve.tensor_scalar(blk_base[:, :], blk_base[:, :], float(DB), None, ALU.mult))
            dve.sem_inc(s_level1, 1)

            def run_scan(p, buf, c, mask, chain, maximum):
                for f in range(F):
                    i = dve.tensor_tensor_scan(buf[:, :, f], mask, buf[:, :, f], c[:, f:f + 1],
                                               ALU.add if maximum else ALU.mult, ALU.max if maximum else ALU.add)
                return i

            def mask_of(k, out, low=None):
                m = inside[:, bass.ds(k * T, T)]
                if low is None:
                    return dve.tensor_scalar(out, m, 1.0, None, ALU.mult)
                return dve.tensor_scalar(out, m, 1.0, low, ALU.subtract, ALU.mult)

            def gather_scan(p, k, b, n):
                dve.wait_ge(p.gathered[b], (n + 1) * (16 * T) + p.g0[b])
                dve.wait_ge(e_carry, k + (p.carry0 + 1))
                run_scan(p, p.rows[:, b], carry, blk_mask[:, 0, :], None, p.maximum).then_inc(e_scanned[b], 1)
                dve.wait_ge(e_scanned[b], n + (p.v[b] + 1))
                dve.tensor_copy(carry[:, :], p.rows[:, b, T - 1, :]).then_inc(e_carry, 1)

            def edge_pass(p):
                dve.sem_inc(e_carry, 1)

                def step(k, b, n):
                    mask_of(k, blk_mask[:, 0, :]).then_inc(e_mask, 1)
                    dve.wait_ge(e_mask, k + (p.mask0 + 1))
                    gather_scan(p, k, b, n)
                ring(dve, NB, step)

            def count_pair(j):
                ch = Chain(dve, b_chain, j * 4)
                two = winv[:, bass.ds(2 * j, 2), :]
                three = "p (a b) -> p a b"
                ch(dve.tensor_scalar(pair_i.rearrange(three, a=2), two, P - 1, None, ALU.bitwise_and))
                ch(dve.tensor_scalar(pair_f[:, 0, :], pair_i, 1.0, None, ALU.mult))
                ch(dve.tensor_scalar(pair_f[:, 1, :], pair_i, 1.0 / P, None, ALU.mult))
                ch(dve.scalar_tensor_tensor(pair_f[:, 1, :].rearrange(three, a=2), two, 1.0 / P,
                                            pair_f[:, 1, :].rearrange(three, a=2), ALU.mult, ALU.subtract))
                dve.sem_inc(b_pair, 1)
                dve.wait_ge(b_keys, j + 1)
                dve.sem_inc(begun, 1)
                with dve.Fori(0, NBH) as q:
                    for i in range(2):
                        m = j * (2 * NBH) + (2 * q + i)
                        dve.wait_ge(b_count, m + 1)
                        for v, out, n in ((0, hot_lo, P), (1, hot_hi, NT)):
                            k = keys[:, v, bass.ds((2 * q + i) * WB, WB)].rearrange("p (w o) -> p w o", o=1)
                            t = dve.tensor_tensor(out[:, i, :, 0:n],
                                                  lane_bf[:, 0:n].rearrange("p (o l) -> p o l", o=1).to_broadcast([P, WB, n]),
                                                  k.to_broadcast([P, WB, n]), ALU.is_equal)
                        t.then_inc(b_hot, 1)

            def pass0():
                dve.sem_inc(ea_carry, 1)

                def step(k, b, n, pairs=2):
                    mask_of(k, blk_mask[:, 1, :]).then_inc(e_mask, 1)
                    mask_of(k, blk_mask[:, 0, :], BIG).then_inc(e_mask, 1)
                    dve.wait_ge(e_mask, k * 2 + 2)
                    dve.wait_ge(ea_loaded, (k + 1) * 16)
                    dve.wait_ge(ea_carry, k + 1)
                    run_scan(p0, eat, carry_ea, blk_mask[:, 1, :], None, False).then_inc(ea_scanned, 1)
                    dve.wait_ge(ea_scanned, k + 1)
                    dve.tensor_copy(carry_ea[:, :], eat[:, T - 1, :]).then_inc(ea_carry, 1)
                    count_pair(2 * k)
                    gather_scan(p0, k, b, n)
                    if pairs > 1:
                        count_pair(2 * k + 1)
                with dve.Fori(0, NB // 2) as g:
                    step(2 * g, 0, g)
                    step(2 * g + 1, 1, g)
                step(NB - 1, 0, NB // 2, pairs=1)

            def seam_scan(sm, i, maximum, ch=ch):
                a, b = (same_neg, through_neg) if maximum else (same, through)
                ch(dve.memset(seam[:, 1, 0:1], -BIG if maximum else 0.0))
                dve.wait_ge(sm.t, i)
                if maximum:
                    ch(dve.tensor_scalar(seam[:, 0, :], a[:, :], BIG, None, ALU.mult))
                    ch(dve.tensor_scalar(seam[:, 2, :], b[:, :], BIG, None, ALU.mult))
                    ch(dve.tensor_tensor(seam[0:F, 0, 1:P], bank[6][0:F, 0:P - 1], seam[0:F, 0, 1:P], ALU.add))
                    ch(dve.tensor_tensor_scan(seam[0:F, 1, 1:P], seam[0:F, 2, 1:P], seam[0:F, 0, 1:P], -BIG, ALU.add, ALU.max))
                else:
                    ch(dve.tensor_tensor(seam[0:F, 0, 1:P], bank[6][0:F, 0:P - 1], a[0:F, 1:P], ALU.mult))
                    ch(dve.tensor_tensor_scan(seam[0:F, 1, 1:P], b[0:F, 1:P], seam[0:F, 0, 1:P], 0.0, ALU.mult, ALU.add))
                dve.sem_inc(sm.scan, 1)

            def seam_add(sm, i, maximum):
                dve.wait_ge(sm.back, i)
                dve.wait_ge(sm.row, 16 * i)
                dve.tensor_tensor(seam_row[:, 0:F], seam_row[:, 0:F], bank[7][:, 0:F],
                                  ALU.max if maximum else ALU.add).then_inc(sm.sum, 1)

            for b in range(2):
                dve.sem_inc(s_found_used[b], 1)

            def count(c, b, n):
                dve.wait_ge(s_found_f[b], n + 1)
                for i in range(SC):
                    t = c * SC + i
                    dve.tensor_scalar(junk_s, found_f[:, b, i, :], node_id[:, bass.ds(t, 1)], 0.0, ALU.is_lt, ALU.add,
                                      accum_out=cnt[:, bass.ds(t, 1)]).then_inc(s_search, 1)
                    dve.wait_ge(s_search, t + (NT + 1))
                dve.sem_inc(s_found_used[b], 1)
            ring(dve, NT // SC, count)
            ch(dve.memset(row_first[:, NT:NT + 1], float(E)))
            ch(dve.tensor_tensor(row_first[:, 0:NT], cnt[:, :], blk_base[:, :], ALU.add))
            dve.sem_inc(s_first, 1)
            ch(dve.tensor_scalar(cnt[:, :], row_first[:, 0:NT], float(E - W), None, ALU.min))
            ch(dve.tensor_copy(win_idx[:, :], cnt[:, :]))
            dve.sem_inc(s_win_idx, 1)
            ch(dve.memset(shift1, 0.0))
            ch(dve.memset(shift2, 0.0))
            ch(dve.tensor_copy(shift1[:, 0:P - 1], ident[:, 1:P]))
            ch(dve.tensor_copy(shift2[:, P - 1:P], ident[:, 0:1]))
            dve.sem_inc(s_shift, 2)
            dve.wait_ge(s_shifted, 1)
            ch(dve.tensor_tensor(deg[:, :], bank[3][:, 0:NT], row_first[:, 0:NT], ALU.subtract))
            ch(dve.tensor_scalar(has[:, :], deg[:, :], 1.0, None, ALU.min))
            ch(dve.tensor_scalar(deg1[:, :], deg[:, :], 1.0, None, ALU.add))
            dve.sem_inc(s_sqrt, 1)
            ch(dve.tensor_scalar(end_idx[:, :], bank[3][:, 0:NT], -1.0, 0.0, ALU.add, ALU.max))
            ch(dve.tensor_tensor(win_lim[:, 0, :], row_first[:, 0:NT], cnt[:, :], ALU.subtract))
            ch(dve.tensor_tensor(win_lim[:, 1, :], win_lim[:, 0, :], deg[:, :], ALU.add))
            ch(dve.tensor_scalar(small[:, 3:4], small[:, 0:1], float(E), None, ALU.add))
            ch(dve.tensor_scalar(cnt[:, :], row_first[:, 0:NT], small[:, 3:4], None, ALU.subtract))
            ch(dve.tensor_tensor(cnt[:, :], cnt[:, :], has[:, :], ALU.mult))
            ch(dve.tensor_scalar(q_idx[:, :], cnt[:, :], small[:, 3:4], None, ALU.add))
            dve.wait_ge(s_sqrt, 2)
            ch(dve.reciprocal(dis[:, :], dis[:, :]))
            ch(dve.reduce_max(small[:, 4:5], deg[:, :], AX.X))
            dve.sem_inc(s_flag_in, 1)
            dve.wait_ge(s_flag_T, 1)
            ch(dve.reduce_max(small[0:1, 5:6], bank[5][0:1, 0:P], AX.X))
            ch(dve.tensor_scalar(flag[:, :], small[0:1, 5:6], float(W), None, ALU.is_le))
            dve.sem_inc(s_flag, 1)
            dve.wait_ge(s_win, 16 * NT)
            lane_w = lane[:, 0:W].rearrange("p (o l) -> p o l", o=1).to_broadcast([P, NT, W])
            ch(dve.tensor_tensor(win_m, lane_w, over(win_lim[:, 1, :], W), ALU.is_lt))
            ch(dve.tensor_scalar(win.bitcast(F32), win, 1.0, None, ALU.add))
            ch(dve.tensor_tensor(win.bitcast(F32), win.bitcast(F32), win_m, ALU.mult))
            ch(dve.tensor_tensor(win_m, lane_w, over(win_lim[:, 0, :], W), ALU.is_ge))
            ch(dve.tensor_tensor(win_m, win.bitcast(F32), win_m, ALU.mult))
            ch(dve.tensor_scalar(winv, win_m, 1.0, None, ALU.subtract))
            ch(dve.memset(zeros_z, 0.0))
            dve.sem_inc(s_setup_done, 1)

            pass0()
            seam_scan(ea_seam, 1, False)
            dve.wait_ge(ea_seam.back, 1)
            ch(dve.tensor_copy(seam_c[:, :], bank[7][:, 0:F]))
            dve.sem_inc(ea_back_read, 1)
            seam_scan(edge_seam, 1, True)
            seam_add(edge_seam, 1, True)
            dve.wait_ge(edge_seam.put, 16)
            dve.wait_ge(ea_seam.row, 16)
            dve.tensor_tensor(seam_row[:, 0:F], seam_row[:, 0:F], seam_c[:, :], ALU.add).then_inc(ea_seam.sum, 1)
            dve.wait_ge(ea_seam.put, 16)
            dve.wait_ge(e_all_stored, 1)
            ch(dve.memset(xcur[:, NT - 1, :], 0.0))
            dve.sem_inc(x_pad, 1)
            fast = dve.value_load(flag[0:1, 0:1], min_val=0, max_val=1)

            def product_rows(layer, cur):
                ch = Chain(dve, m_chain, layer * NC * 5)
                for c in range(NC):
                    t = slice(c * CT, (c + 1) * CT)
                    rest = got64[:, t, :]
                    ch(dve.tensor_copy(parts[:, t, 0:F], cur[:, t, :]))
                    ch(dve.tensor_tensor(rest, cur[:, t, :], parts[:, t, 0:F], ALU.subtract))
                    ch(dve.tensor_copy(parts[:, t, F:2 * F], rest))
                    ch(dve.tensor_tensor(rest, rest, parts[:, t, F:2 * F], ALU.subtract))
                    ch(dve.tensor_copy(parts[:, t, 2 * F:3 * F], rest))
                    dve.sem_inc(m_split, 1)
                if layer == 0:
                    dve.sem_inc(m_got, 1)

            def copy_rows(layer):
                def group(c, q):
                    nb = QB[q]
                    dve.wait_ge(m_folded, c * NQ + (layer * NC * NQ + q + 1))
                    dve.tensor_scalar(got64[:, bass.ds(c * CT + q * GB, nb), :], bank[2][:, 0:nb * F].rearrange("p (a b) -> p a b", a=nb),
                                      1.0, None, ALU.mult).then_inc(m_got, 1)
                    if q == NQ - 1:
                        dve.wait_ge(m_got, c * NQ + (layer * NC * NQ + NQ + 1))
                return group

            def gathered_rows(p, s):
                edge_pass(p)
                seam_scan(edge_seam, p.i + 1, False, Chain(dve, slow_chain, (p.i - 1) * 3))
                seam_add(edge_seam, p.i + 1, False)

                def step(c, b, n):
                    dve.wait_ge(s.got[b], (n + (s.got0[b] + 1)) * (16 * CT))
                    dve.tensor_tensor(chunk(got64, c), chunk(got64, c), over(cols(has, c), F), ALU.mult).then_inc(s_slow, 1)
                ring(dve, NC, step)
                dve.wait_ge(s_slow, p.i * NC)

            def layer(i, p, s, cur, start, mid=nothing, late=nothing, first=nothing):
                with dve.If(fast == 1):
                    product_rows(i, cur)
                    first()
                    in_turn(dve, NC, NQ, copy_rows(i), start, mid, late)
                with dve.Else():
                    gathered_rows(p, s)
                    first()
                    chunks(dve, NC, lambda c: (start(c), mid(c), late(c)))

            def cols(v, c):
                return v[:, bass.ds(c * CT, CT)]

            def norm(s, ch, c):
                ch(dve.reduce_sum(st[:, 0, :], ln_a[:, :, :], AX.X))
                ch(dve.tensor_scalar(st[:, 0, :], st[:, 0, :], 1.0 / F, None, ALU.mult))
                ch(dve.tensor_tensor(ln_a[:, :, :], ln_a[:, :, :], over(st[:, 0, :], F), ALU.subtract))
                ch(dve.tensor_tensor(ln_b[:, :, :], ln_a[:, :, :], ln_a[:, :, :], ALU.mult))
                ch(dve.reduce_sum(st[:, 1, :], ln_b[:, :, :], AX.X))
                ch(dve.tensor_scalar(st[:, 1, :], st[:, 1, :], 1.0 / F, EPS, ALU.mult, ALU.add))
                dve.sem_inc(node_var, 1)
                dve.wait_ge(node_std, c + (s.norm0 + 1))
                ch(dve.reciprocal(st[:, 3, :], st[:, 2, :]))
                ch(dve.tensor_tensor(chunk(xcur, c), ln_a[:, :, :], over(st[:, 3, :], F), ALU.mult))

            def stage0(c, b, n):
                ch = Chain(dve, node_chain, c * 10 + n0.chain0)
                dve.wait_ge(n0.got[b], (n + 1) * (16 * CT))
                ch(dve.tensor_tensor(ln_a[:, :, :], chunk(got64, c), over(cols(has, c), F), ALU.mult))
                ch(dve.tensor_tensor(ln_a[:, :, :], ln_a[:, :, :], chunk(xcur, c), ALU.add))
                norm(n0, ch, c)
                assert ch.n == 10
                dve.sem_inc(node_rows, 1)
            dve.wait_ge(x_loaded, 32)
            ring(dve, NC, stage0)

            def before1():
                dve.wait_ge(e_table, 16 * NC)
                for b in range(2):
                    dve.wait_ge(ea_got[b], (NC + 1 - b) // 2 * (16 * CT))

            def stage1(c):
                ch = Chain(dve, node_chain, c * 13 + n1.chain0)
                ch(dve.tensor_tensor(ln_a[:, :, :], chunk(got_ea, c), over(cols(has, c), F), ALU.mult))
                ch(dve.tensor_tensor(ln_a[:, :, :], ln_a[:, :, :], chunk(got64, c), ALU.add))
                ch(dve.tensor_tensor(ln_b[:, :, :], chunk(xcur, c), over(cols(deg1, c), F), ALU.mult))
                ch(dve.tensor_tensor(ln_a[:, :, :], ln_a[:, :, :], ln_b[:, :, :], ALU.add))
                norm(n1, ch, c)
                ch(dve.tensor_tensor(chunk(tcur, c), chunk(xcur, c), over(cols(dis, c), F), ALU.mult))
                assert ch.n == 13
                dve.sem_inc(node_rows, 1)
            layer(0, p1, n1, xcur, stage1, first=before1)

            def conv_in(s, c, n):
                ch = Chain(dve, node_chain, c * n + s.chain0)
                ch(dve.tensor_tensor(zc, chunk(got64, c), chunk(tcur, c), ALU.add))
                ch(dve.tensor_tensor(zc, zc, over(cols(dis, c), F), ALU.mult))
                dve.sem_inc(node_z, 1)

            def halves():
                for h, (a, e) in enumerate(((0, 8), (8, CT))):
                    yield a, e, bank[5 + h][:, 0:(e - a) * F].rearrange("p (a b) -> p a b", b=F)

            def stage2(c):
                ch = Chain(dve, node_chain, c * 4 + (n2.chain0 + 2))
                dve.wait_ge(node_mm, c + (n2.mm0 + 1))
                for a, e, v in halves():
                    ch(dve.scalar_tensor_tensor(tcur[:, bass.ds(c * CT + a, e - a), :], v, 0.0,
                                                over(dis[:, bass.ds(c * CT + a, e - a)], F), ALU.max, ALU.mult))
                assert ch.n == 2
                dve.sem_inc(node_rows, 1)
            layer(1, p2, n2, tcur, lambda c: conv_in(n2, c, 4), stage2)

            def stage3(c):
                ch = Chain(dve, node_chain, c * 13 + (n3.chain0 + 2))
                dve.wait_ge(node_mm, c + (n3.mm0 + 1))
                for a, e, v in halves():
                    ch(dve.tensor_tensor(ln_a[:, a:e, :], v, xcur[:, bass.ds(c * CT + a, e - a), :], ALU.add))
                norm(n3, ch, c)
                ch(dve.tensor_scalar(zc, chunk(xcur, c), 1.0, None, ALU.mult))
                assert ch.n == 11
                dve.sem_inc(node_z, 1)
                dve.sem_inc(node_rows, 1)

            def late(c):
                dve.wait_ge(node_zt, 2 * c + (n3.z0 + 2))
                dve.sem_inc(begun, 1)
            layer(2, p3, n3, tcur, lambda c: conv_in(n3, c, 13), stage3, late)

            dve.wait_ge(q_scat, 16 * NT)
            dve.wait_ge(x3_stored, 16 * NC)
            dve.wait_ge(q_tab, 2 * 16 * (NC + 1))
            dve.memset(acc[:, 0, :], 0.0).then_inc(a_init, 1)
            for u in range(NS):
                dve.sem_inc(a_free[u], 1)
            KA = 1 + 1 + NS * 7 + 2

            def heads(v):
                return v.rearrange("p a (h d) -> p a h d", h=H)

            def per_feature(v):
                return v.rearrange("p a (h o) -> p a h o", o=1).to_broadcast([P, TS, H, DK])

            def att(k, b, n):
                ch = Chain(dve, a_chain, k * KA)
                ch(mask_of(k, blk_mask[:, 0, :]))
                dve.wait_ge(a_q, (k + 1) * 16)
                dve.wait_ge(mlp_bc, (k + 1) * NG)
                for f in range(F):
                    i = dve.tensor_tensor_scan(qf[:, :, f], blk_mask[:, 0, :], qf[:, :, f], carry_q[:, f:f + 1], ALU.mult, ALU.add)
                ch(i)
                for u in range(NS):
                    t = slice(u * TS, (u + 1) * TS)
                    t1 = slice(1 + u * TS, 1 + (u + 1) * TS)
                    if u == 0:
                        dve.tensor_copy(carry_q[:, :], qf[:, T - 1, :])
                        dve.tensor_scalar(blk_mask[:, 1, :], blk_mask[:, 0, :], 1.0, LOW, ALU.subtract, ALU.mult)
                    dve.wait_ge(a_kv[u], (k + 1) * (16 * TS))
                    ch(dve.tensor_tensor(prod, kv[:, u, :, 0:F], qf[:, t, :], ALU.mult))
                    ch(dve.reduce_sum(score, heads(prod), AX.X))
                    ch(dve.tensor_tensor(score, score, bias_i[:, b, t, :], ALU.add))
                    if u == 0:
                        dve.wait_ge(a_slot, k + 1)
                    for h in range(H):
                        i = dve.tensor_tensor_scan(acc[:, t1, A3 + h], blk_mask[:, 1, t], score[:, :, h],
                                                   acc[:, u * TS, A3 + h:A3 + h + 1], ALU.add, ALU.max)
                    ch(i)
                    dve.tensor_tensor(arg[:, 0], score, acc[:, t1, A3:W3], ALU.subtract)
                    ch(dve.tensor_tensor(arg[:, 1], acc[:, t, A3:W3], over(blk_mask[:, 1, t], H), ALU.add))
                    ch(dve.tensor_tensor(arg[:, 1], arg[:, 1], acc[:, t1, A3:W3], ALU.subtract))
                    dve.sem_inc(a_arg, 1)
                    if u == NS - 1:
                        dve.sem_inc(a_q_used, 1)
                    dve.wait_ge(a_exp, k * NS + (u + 1))
                    ch(dve.tensor_tensor(heads(acc[:, t1, 0:F]), heads(kv[:, u, :, F:2 * F]),
                                         per_feature(acc[:, t1, F:A3]), ALU.mult))
                    dve.sem_inc(a_free[u], 1)
                for f in range(A3):
                    h = f // DK if f < F else f - F
                    i = dve.tensor_tensor_scan(acc[:, 1:T + 1, f], keepf[:, :, h], acc[:, 1:T + 1, f], acc[:, 0, f:f + 1],
                                               ALU.mult, ALU.add)
                ch(i)
                ch(dve.tensor_copy(acc[:, 0, :], acc[:, T, :]))
                assert ch.n == KA, ch.n
                dve.sem_inc(a_scan, 1)
            dve.wait_ge(a_init, 1)
            ring(dve, NB, att)

            dve.wait_ge(a_all_stored, 1)

            def spread(out, m):
                dve.tensor_copy(out[:, 0:F].rearrange("p (h d) -> p h d", h=H), m.rearrange("p (h o) -> p h o", o=1).to_broadcast([P, H, DK]))
                return dve.tensor_copy(out[:, F:A3], m)
            dve.tensor_copy(seam_m[:, 0, 0:A3], acc[:, 0, 0:A3])
            ch(spread(seam_m[:, 1, :], acc[:, 0, A3:W3]))
            dve.sem_inc(a_tail, 1)
            dve.wait_ge(a_seam.t, 1)
            q = slice(0, A3)
            aT, mT = bank[6][q, 0:P - 1], bank[5][q, 0:P - 1]
            row = seam_m[q]
            ch(dve.tensor_scalar(seam_m[:, 6, :], same_neg[:, :], LOW, None, ALU.mult))
            ch(dve.tensor_scalar(seam_m[:, 7, :], through_neg[:, :], LOW, None, ALU.mult))
            ch(dve.memset(row[:, 2, 0:1], -LOW))
            ch(dve.tensor_tensor(row[:, 6, 1:P], mT, row[:, 6, 1:P], ALU.add))
            ch(dve.tensor_tensor_scan(row[:, 2, 1:P], row[:, 7, 1:P], row[:, 6, 1:P], -LOW, ALU.add, ALU.max))
            ch(dve.memset(row[:, 3:5, 0:1], 0.0))
            ch(dve.tensor_tensor(row[:, 3, 1:P], row[:, 2, 0:P - 1], row[:, 7, 1:P], ALU.add))
            ch(dve.tensor_tensor(row[:, 3, 1:P], row[:, 3, 1:P], row[:, 2, 1:P], ALU.subtract))
            ch(dve.tensor_tensor(row[:, 4, 1:P], row[:, 6, 1:P], row[:, 2, 1:P], ALU.subtract))
            dve.sem_inc(a_dexp, 1)
            dve.wait_ge(a_dexped, 1)
            ch(dve.tensor_tensor(row[:, 4, 1:P], aT, row[:, 4, 1:P], ALU.mult))
            ch(dve.memset(row[:, 5, 0:1], 0.0))
            ch(dve.tensor_tensor_scan(row[:, 5, 1:P], row[:, 3, 1:P], row[:, 4, 1:P], 0.0, ALU.mult, ALU.add))
            dve.sem_inc(a_seam.scan, 1)
            dve.wait_ge(a_seam.back, 1)
            dve.wait_ge(a_seam.row, 16)
            ch(spread(seam_m[:, 0, :], seam_row[:, A3:W3]))
            ch(dve.tensor_tensor(seam_m[:, 1, 0:A3], seam_m[:, 0, 0:A3], bank[4][:, 0:A3], ALU.max))
            dve.tensor_tensor(seam_m[:, 6, 0:A3], seam_m[:, 0, 0:A3], seam_m[:, 1, 0:A3], ALU.subtract)
            ch(dve.tensor_tensor(seam_m[:, 7, 0:A3], bank[4][:, 0:A3], seam_m[:, 1, 0:A3], ALU.subtract))
            dve.sem_inc(a_dexp, 1)
            dve.wait_ge(a_dexped, 2)
            ch(dve.tensor_tensor(seam_row[:, 0:A3], seam_row[:, 0:A3], seam_m[:, 6, 0:A3], ALU.mult))
            ch(dve.tensor_tensor(seam_m[:, 7, 0:A3], bank[7][:, 0:A3], seam_m[:, 7, 0:A3], ALU.mult))
            ch(dve.tensor_tensor(seam_row[:, 0:A3], seam_row[:, 0:A3], seam_m[:, 7, 0:A3], ALU.add))
            dve.sem_inc(a_seam.sum, 1)

            def stage4(c, b, n):
                ch = Chain(dve, node_chain, c * 14 + n4.chain0)
                dve.wait_ge(n4.got[b], (n + 1) * (16 * CT))
                g = chunk(got, c)
                ch(dve.tensor_scalar(rden[:, :, :], g[:, :, F:A3], 1e-12, None, ALU.add))
                ch(dve.reciprocal(rden[:, :, :], rden[:, :, :]))
                ch(dve.tensor_tensor(heads(zc), heads(g[:, :, 0:F]),
                                     rden[:, :, :].rearrange("p a (h o) -> p a h o", o=1).to_broadcast([P, CT, H, DK]), ALU.mult))
                ch(dve.tensor_tensor(zc, zc, over(cols(has, c), F), ALU.mult))
                dve.sem_inc(node_z, 1)
                dve.wait_ge(node_mm, c + (n4.mm0 + 1))
                for a, e, v in halves():
                    ch(dve.tensor_tensor(ln_a[:, a:e, :], v, xcur[:, bass.ds(c * CT + a, e - a), :], ALU.add))
                norm(n4, ch, c)
                assert ch.n == 14
                dve.sem_inc(node_rows, 1)
            dve.wait_ge(x3_loaded, 16)
            ring(dve, NC, stage4)


_INS = ['x', 'src', 'dst', 'edge_attr_32', 'edge_attr_64', 'L2_gnn_W1', 'L2_gnn_b1', 'L2_gnn_W2', 'L2_gnn_b2',
        'L3_gnn_WQ', 'L3_gnn_bQ', 'L3_gnn_WK', 'L3_gnn_bK', 'L3_gnn_WV', 'L3_gnn_bV', 'L3_gnn_WO', 'L3_gnn_bO',
        'L3_gnn_We1', 'L3_gnn_be1', 'L3_gnn_We2', 'L3_gnn_be2']


def kernel(**inputs):
    import numpy as _np
    import concourse.bacc as _bacc
    from concourse import mybir as _mybir
    from concourse.bass_utils import run_bass_kernel_spmd as _run

    nc = _bacc.Bacc("TRN2", target_bir_lowering=False, num_devices=1)
    arrays, args = {}, []
    for name in _INS:
        a = _np.ascontiguousarray(inputs[name])
        arrays[f"in_{name}_dram"] = a
        args.append(nc.dram_tensor(f"in_{name}_dram", a.shape, _mybir.dt.from_np(a.dtype), kind="ExternalInput").ap())
    out = nc.dram_tensor("out_0_dram", inputs["x"].shape, _mybir.dt.float32, kind="ExternalOutput").ap()
    build_gnn(nc, *args, out)
    r = _run(nc, [arrays], core_ids=[0])
    return r.results[0]["out_0_dram"]
```
